# Optimizing a Trainium2 kernel written in Bass

```python
import numpy as np
import jax
import jax.numpy as jnp

def _softmax(x, axis=-1):
    return jax.nn.softmax(x, axis=axis)
def _gelu(x):
    return jax.nn.gelu(x, approximate=True)
def _silu(x):
    return jax.nn.silu(x)
def _sigmoid(x):
    return jax.nn.sigmoid(x)
def _layernorm(x, axis=-1, eps=1e-5):
    m = jnp.mean(x, axis=axis, keepdims=True)
    v = jnp.var(x, axis=axis, keepdims=True)
    return (x - m) / jnp.sqrt(v + eps)
def _scatter_add(tgt, idx, src, axis=0):
    return tgt.at[idx].add(src)
def _segment_sum(src, seg, n):
    return jax.ops.segment_sum(src, seg, n)

kernel_name = 'mk_conv_preact_d2_conv_nchw512_8a238e'

def setup_inputs(seed: int = 0):
    np.random.seed(seed)
    _w = jnp.asarray
    def _rec_inputs():
        import jax
        import jax.numpy as jnp
        _gk = jax.random.key(seed)
        x = -0.0002928 + 1 * jax.random.normal(jax.random.fold_in(_gk, 1), (8, 512, 32, 32), jnp.float32)
        return x
    x = _rec_inputs()
    def _L0_conv_setup():
        import jax, jax.numpy as jnp
        import numpy as np
        B, C1, C2, N, F, HEADS, E = (8, 512, 512, 2, 32, 4, 0.5)
        C = int(C2 * E)
        HD = C // HEADS
        BN_EPS = 0.001

        def conv2d(x, w, pad):
            return jax.lax.conv_general_dilated(x, w, (1, 1), [(pad, pad), (pad, pad)], dimension_numbers=('NCHW', 'OIHW', 'NCHW'))

        def bn_eval(x, p):
            g, b, m, v = p
            s = (g / jnp.sqrt(v + BN_EPS))[:, None, None]
            return (x - m[:, None, None]) * s + b[:, None, None]

        def cbs(x, w, p, pad):
            return jax.nn.silu(bn_eval(conv2d(x, w, pad), p))

        def bot_attention(x, qkv_w, rw, rh):
            b, c, h, w = x.shape
            hw = h * w
            qkv = conv2d(x, qkv_w, 0).reshape(b, 3, HEADS, HD, hw)
            q, k, v = (qkv[:, 0], qkv[:, 1], qkv[:, 2])
            r = (rw + rh).reshape(1, HEADS, HD, hw)
            logits = jnp.einsum('bhdi,bhdj->bhij', q, k + r) * HD ** (-0.5)
            a = jax.nn.softmax(logits, axis=-1)
            out = jnp.einsum('bhij,bhdj->bhdi', a, v)
            return out.reshape(b, c, h, w)
        key = jax.random.key(seed)
        ks = iter(jax.random.split(key, 32))

        def nrm(shape, s=0.05):
            return jax.random.normal(next(ks), shape, jnp.float32) * s

        def bnp(cc):
            return jnp.stack([1.0 + 0.1 * jax.random.normal(next(ks), (cc,), jnp.float32), 0.1 * jax.random.normal(next(ks), (cc,), jnp.float32), 0.1 * jax.random.normal(next(ks), (cc,), jnp.float32), 0.5 + jax.random.uniform(next(ks), (cc,), jnp.float32)])
        return {'x': jax.random.normal(next(ks), (B, C1, F, F), jnp.float32), 'cv1_w': nrm((2 * C, C1, 1, 1)), 'cv1_bn': bnp(2 * C), 'cv2_w': nrm((C2, (2 + N) * C, 1, 1)), 'cv2_bn': bnp(C2), 'm_cv1_w': nrm((N, C, C, 3, 3)), 'm_cv1_bn': jnp.stack([bnp(C) for _ in range(N)]), 'm_qkv_w': nrm((N, 3 * C, C, 1, 1)), 'm_rw': jax.random.normal(next(ks), (N, 1, HEADS, HD, 1, F), jnp.float32), 'm_rh': jax.random.normal(next(ks), (N, 1, HEADS, HD, F, 1), jnp.float32), 'm_cv2_w': nrm((N, C, C, 1, 1)), 'm_cv2_bn': jnp.stack([bnp(C) for _ in range(N)])}
    _L0_conv_all = _L0_conv_setup()
    _L0_conv_in = {k: v for k, v in _L0_conv_all.items() if k in ('cv1_w', 'cv1_bn', 'cv2_w', 'cv2_bn', 'm_cv1_w', 'm_cv1_bn', 'm_qkv_w', 'm_rw', 'm_rh', 'm_cv2_w', 'm_cv2_bn', )}
    del _L0_conv_all

    def _L1_conv_setup():
        import jax, jax.numpy as jnp
        import numpy as np
        B, C_IN, H, W_ = (16, 512, 96, 96)
        C_OUT, K, G = (512, 1, 16)
        STRIDE, PAD, DIL = (1, 0, 1)
        key = jax.random.key(seed)
        k1, k2, k3, k4 = jax.random.split(key, 4)
        x = jax.random.normal(k1, (B, C_IN, H, W_), dtype=jnp.float32)
        conv = jax.random.normal(k2, (C_OUT, C_IN, K, K), dtype=jnp.float32)
        S = jax.random.normal(k3, (C_IN, G), dtype=jnp.float32)
        T = jax.random.normal(k4, (C_OUT, G), dtype=jnp.float32)
        return {'x': x, 'conv': conv, 'S': S, 'T': T}
    _L1_conv_all = _L1_conv_setup()
    _L1_conv_in = {k: v for k, v in _L1_conv_all.items() if k in ('conv', 'S', 'T', )}
    del _L1_conv_all

    return {
        "x": x,
        "L0_conv_cv1_w": _L0_conv_in["cv1_w"],
        "L0_conv_cv1_bn": _L0_conv_in["cv1_bn"],
        "L0_conv_cv2_w": _L0_conv_in["cv2_w"],
        "L0_conv_cv2_bn": _L0_conv_in["cv2_bn"],
        "L0_conv_m_cv1_w": _L0_conv_in["m_cv1_w"],
        "L0_conv_m_cv1_bn": _L0_conv_in["m_cv1_bn"],
        "L0_conv_m_qkv_w": _L0_conv_in["m_qkv_w"],
        "L0_conv_m_rw": _L0_conv_in["m_rw"],
        "L0_conv_m_rh": _L0_conv_in["m_rh"],
        "L0_conv_m_cv2_w": _L0_conv_in["m_cv2_w"],
        "L0_conv_m_cv2_bn": _L0_conv_in["m_cv2_bn"],
        "L1_conv_conv": _L1_conv_in["conv"],
        "L1_conv_S": _L1_conv_in["S"],
        "L1_conv_T": _L1_conv_in["T"],
    }

def reference(x, L0_conv_cv1_w, L0_conv_cv1_bn, L0_conv_cv2_w, L0_conv_cv2_bn, L0_conv_m_cv1_w, L0_conv_m_cv1_bn, L0_conv_m_qkv_w, L0_conv_m_rw, L0_conv_m_rh, L0_conv_m_cv2_w, L0_conv_m_cv2_bn, L1_conv_conv, L1_conv_S, L1_conv_T):
    import jax
    import jax.numpy as jnp
    def _L0_conv_ref(x, cv1_w, cv1_bn, cv2_w, cv2_bn, m_cv1_w, m_cv1_bn, m_qkv_w, m_rw, m_rh, m_cv2_w, m_cv2_bn):
        import jax, jax.numpy as jnp
        import numpy as np
        B, C1, C2, N, F, HEADS, E = (8, 512, 512, 2, 32, 4, 0.5)
        C = int(C2 * E)
        HD = C // HEADS
        BN_EPS = 0.001

        def conv2d(x, w, pad):
            return jax.lax.conv_general_dilated(x, w, (1, 1), [(pad, pad), (pad, pad)], dimension_numbers=('NCHW', 'OIHW', 'NCHW'))

        def bn_eval(x, p):
            g, b, m, v = p
            s = (g / jnp.sqrt(v + BN_EPS))[:, None, None]
            return (x - m[:, None, None]) * s + b[:, None, None]

        def cbs(x, w, p, pad):
            return jax.nn.silu(bn_eval(conv2d(x, w, pad), p))

        def bot_attention(x, qkv_w, rw, rh):
            b, c, h, w = x.shape
            hw = h * w
            qkv = conv2d(x, qkv_w, 0).reshape(b, 3, HEADS, HD, hw)
            q, k, v = (qkv[:, 0], qkv[:, 1], qkv[:, 2])
            r = (rw + rh).reshape(1, HEADS, HD, hw)
            logits = jnp.einsum('bhdi,bhdj->bhij', q, k + r) * HD ** (-0.5)
            a = jax.nn.softmax(logits, axis=-1)
            out = jnp.einsum('bhij,bhdj->bhdi', a, v)
            return out.reshape(b, c, h, w)
        t = cbs(x, cv1_w, cv1_bn, 0)
        ys = [t[:, :C], t[:, C:]]
        for i in range(N):
            yi = ys[-1]
            z = cbs(yi, m_cv1_w[i], m_cv1_bn[i], 1)
            z = bot_attention(z, m_qkv_w[i], m_rw[i], m_rh[i])
            z = jax.nn.silu(bn_eval(conv2d(z, m_cv2_w[i], 0), m_cv2_bn[i]))
            ys.append(yi + z)
        return cbs(jnp.concatenate(ys, axis=1), cv2_w, cv2_bn, 0)

    def _L1_conv_ref(x, conv, S, T):
        import jax, jax.numpy as jnp
        import numpy as np
        B, C_IN, H, W_ = (16, 512, 96, 96)
        C_OUT, K, G = (512, 1, 16)
        STRIDE, PAD, DIL = (1, 0, 1)
        s_hat = jax.nn.softmax(S, axis=1)
        t_hat = jax.nn.softmax(T, axis=1)
        s = jnp.argmax(s_hat, axis=1)
        t = jnp.argmax(t_hat, axis=1)
        c_in = S.shape[0]
        c_out = T.shape[0]
        s_gain = s_hat[jnp.arange(c_in), s]
        t_gain = t_hat[jnp.arange(c_out), t]
        x_scaled = x * s_gain[None, :, None, None]
        mask = (t[:, None] == s[None, :]).astype(conv.dtype)
        w_eff = conv * t_gain[:, None, None, None] * mask[:, :, None, None]
        dense = jax.lax.conv_general_dilated(x_scaled, w_eff, window_strides=(STRIDE, STRIDE), padding=((PAD, PAD), (PAD, PAD)), rhs_dilation=(DIL, DIL), dimension_numbers=('NCHW', 'OIHW', 'NCHW'))
        p = jnp.argsort(t, stable=True)
        return dense[:, p[p]]

    def _gn(v, G=32, eps=1e-5):
        B_, C_, H_, W_ = v.shape
        g = v.reshape(B_, G, C_ // G, H_, W_)
        m = jnp.mean(g, axis=(2, 3, 4), keepdims=True)
        s = jnp.var(g, axis=(2, 3, 4), keepdims=True)
        return ((g - m) / jnp.sqrt(s + eps)).reshape(v.shape)

    def _ln_c(v, eps=1e-6):
        m = jnp.mean(v, axis=1, keepdims=True)
        s = jnp.var(v, axis=1, keepdims=True)
        return (v - m) / jnp.sqrt(s + eps)

    def _ln_t(v, eps=1e-5):
        m = jnp.mean(v, axis=-1, keepdims=True)
        s = jnp.var(v, axis=-1, keepdims=True)
        return (v - m) / jnp.sqrt(s + eps)

    def _to_tokens(v):
        B_, C_, H_, W_ = v.shape
        return v.reshape(B_, C_, H_ * W_).transpose(0, 2, 1)
    def _from_tokens(t, like):
        B_, C_, H_, W_ = like.shape
        return t.transpose(0, 2, 1).reshape(B_, C_, H_, W_)

    x = x + _L0_conv_ref(_gn(x), L0_conv_cv1_w, L0_conv_cv1_bn, L0_conv_cv2_w, L0_conv_cv2_bn, L0_conv_m_cv1_w, L0_conv_m_cv1_bn, L0_conv_m_qkv_w, L0_conv_m_rw, L0_conv_m_rh, L0_conv_m_cv2_w, L0_conv_m_cv2_bn)
    x = x + _L1_conv_ref(_gn(x), L1_conv_conv, L1_conv_S, L1_conv_T)
    return x


_drawn_inputs = setup_inputs


def setup_inputs(seed=0):
    import zlib

    import numpy as np

    out = dict(_drawn_inputs(seed))
    spreads = {}
    factors = {}
    for name, (base, spread) in spreads.items():
        noise = np.random.default_rng([zlib.crc32(name.encode()), seed]).standard_normal(out[name].shape)
        drawn = base * np.exp(spread * noise) if base else spread * noise
        out[name] = jnp.asarray(drawn.astype(out[name].dtype))
    for name, factor in factors.items():
        out[name] = (out[name] * factor).astype(out[name].dtype)
    return out
```

```python
from contextlib import ExitStack

import concourse.bass as bass
from concourse import mybir
from concourse.alu_op_type import AluOpType as ALU

ACT = mybir.ActivationFunctionType
AX = mybir.AxisListType
F32 = mybir.dt.float32
F16 = mybir.dt.float16
I32 = mybir.dt.int32

P = 128
ACTIVATION_SCALE = 16.0
WEIGHT_TOP = 64.0
WS = WEIGHT_TOP * ACTIVATION_SCALE
V_SHIFT = 2.0 ** -8
SHIFT_UNIT = 1024.0
EXP_TOP = 5.545177444479562
BN_EPS, GN_EPS = 1e-3, 1e-5


class Done:

    def __init__(self, sem, count, lag=0):
        self.sem, self.count, self.lag = sem, count, lag


class Sem:
    def __init__(self, handle):
        self.handle, self.n = handle, 0


class Later:
    def __init__(self, name):
        self.name = name


def flat(after):
    return [d for a in after for d in (flat(a) if isinstance(a, (list, tuple)) else [a])]


class Section:

    ENGINES = ("tensor", "scalar", "vector", "gpsimd", "sync")

    def __init__(self, nc, ctx, name, loop):
        self.nc, self.ctx, self.name, self.loop = nc, ctx, name, loop
        self.queue = {e: [] for e in self.ENGINES}
        self.sems = {}
        self.kept = {}

    def sem(self, name):
        if name not in self.sems:
            self.sems[name] = Sem(self.ctx.enter_context(self.nc.semaphore(f"{self.name}_{name}")))
        return self.sems[name]

    def do(self, engine, fn, after=(), sem=None, inc=1, bare=False):
        s = self.sem(sem or engine)
        s.n += inc
        self.queue[engine].append((fn, flat(after), s, inc, bare))
        return Done(s, s.n)

    def pe(self, fn, after=()):
        return self.do("tensor", fn, after)

    def act(self, fn, after=()):
        return self.do("scalar", fn, after)

    def dve(self, fn, after=()):
        return self.do("vector", fn, after)

    def pool(self, fn, after=()):
        return self.do("gpsimd", fn, after, bare=True)

    def dma(self, sem, fn, after=()):
        return self.do("sync", fn, after, sem=sem, inc=16)

    def keep(self, name, *done):
        self.kept[name] = list(done)

    def last(self, name):
        if name in self.kept:
            return self.kept[name]
        return [Later(name)] if self.loop else []

    def resolve(self, after):
        for a in after:
            if isinstance(a, Later):
                for d in self.kept[a.name]:
                    yield Done(d.sem, d.count, d.lag + 1)
            else:
                yield a

    def emit(self, engine, e, i):
        seen = {}
        for fn, after, s, inc, bare in self.queue[engine]:
            need = {}
            for d in self.resolve(after):
                at = d.count - d.lag * d.sem.n
                if at > seen.get(d.sem, -10**9):
                    seen[d.sem] = need[d.sem] = at
            for d_sem, at in need.items():
                if self.loop:
                    e.wait_ge(d_sem.handle, i * d_sem.n + (d_sem.n + at))
                else:
                    e.wait_ge(d_sem.handle, at)
            if bare and need and self.loop:
                e.sem_inc(self.held.handle, 1)
            fn(e, i).then_inc(s.handle, inc)

    def finals(self, e):
        for s in self.sems.values():
            e.wait_ge(s.handle, s.n)


def build(nc, x, cv1_w, cv1_bn, cv2_w, cv2_bn, m_cv1_w, m_cv1_bn, m_qkv_w, m_rw, m_rh, m_cv2_w,
          m_cv2_bn, conv, S_logits, T_logits, out):
    B, C, H, W = x.shape
    HW = H * W
    NB, CH = m_cv1_w.shape[0], m_cv1_w.shape[1]
    G = S_logits.shape[1]
    HD = m_rw.shape[3]
    CT, HT, YT = C // P, CH // P, (2 + NB) * CH // P
    HALF = HW // 2
    ROWS = H // 2
    HP, WP = H + 2, W + 2
    TAPS = 9
    JT = HW // P
    VW = 2 * HD + 2
    HEADS = CH // HD
    QC = 2 * P
    GROUP = C // 32
    assert HEADS == 4 and HD == 64 and HW == 1024

    ctx = ExitStack()
    with ctx:
        def sb(name, shape, dt):
            return ctx.enter_context(nc.sbuf_tensor(name, shape, dt))

        w_cv1 = sb("w_cv1", [P, 2, CT, C], F16)
        w_cv2 = sb("w_cv2", [P, 2, YT, C], F16)
        w_l1 = sb("w_l1", [P, 2, CT, C], F16)
        w_qkv = sb("w_qkv", [P, NB, 2, HT, 3 * CH], F16)
        w_m2 = sb("w_m2", [P, NB, 2, HT, CH], F16)
        w_c3 = sb("w_c3", [P, 2, HT, TAPS, CH], F16)
        w_c3_dram = nc.dram_tensor("w_c3_dram", (NB, P, 2 * HT * TAPS * CH), F16, kind="Internal").ap()
        xn = sb("xn", [P, CT, HW], F32)
        xn_parts = xn[:, :, :].rearrange("p t n -> p (t n)").bitcast(F16).rearrange(
            "p (t s n) -> p t s n", t=CT, s=2)
        y_plain = sb("y_plain", [P, HT, 2, HW], F16)
        y_pad = sb("y_pad", [P, YT - HT, 2, HP * WP], F16)
        z = sb("z", [P, HT, 2, HW], F16)
        qk = sb("qk", [P, 2 * HEADS * HW // 2], F32)
        qk16 = qk[:, :].bitcast(F16).rearrange("p (s h n) -> p s h n", s=2, h=HEADS)
        q_stack, k_stack = qk16[:, 0], qk16[:, 1]
        q2_stack = sb("q2_stack", [P, HEADS, HW], F16)
        k2_stack = sb("k2_stack", [P, HEADS, HW], F16)
        x1 = qk[:, :].rearrange("p (t n) -> p t n", t=CT)
        v_ext = sb("v_ext", [P, JT, HEADS, VW], F16)
        probs = sb("probs", [P, 2, 2, JT, QC], F16)
        x1_parts = probs[:, :, :, :, :].rearrange("p a b c d -> p (a b c d)").rearrange(
            "p (t s n) -> p t s n", t=CT, s=2)
        wide = sb("wide", [P, 2, HW], F32)
        o_nat = sb("o_nat", [P, 2, JT, P], F32)
        x_again = sb("x_again", [P, 2, HALF], F32)
        o_raw = sb("o_raw", [P, 2, 2, 2 * HD + 1], F32)
        ident16 = sb("ident16", [P, P], F16)
        ident = sb("ident", [P, P], F32)
        group_mean = sb("group_mean", [P, P], F32)
        par = {n: sb(f"par_{n}", [P, t, 2], F32) for n, t in
               (("cv1_t", CT), ("cv1_y", CT), ("cv2_t", CT), ("cv2_y", CT), ("m1_t", NB * HT), ("m1_y", NB * HT),
                ("m2_t", NB * HT), ("m2_y", NB * HT))}
        qkv_unit = sb("qkv_unit", [P, NB, 6], F32)
        l1_unit = sb("l1_unit", [P, CT], F32)
        rw = sb("rw", [P, NB, HT, W], F32)
        rh = sb("rh", [P, NB, HT, H], F32)
        row_max = sb("row_max", [P, 2, JT, 2], F32)
        shift = sb("shift", [P, 2, 2, JT], F32)
        shift16 = sb("shift16", [P, 2, JT], F16)
        recip = sb("recip", [P, 2, 2], F32)
        stats = sb("stats", [P, 2, CT, 2, 6], F32)
        mv = sb("mv", [P, 2, CT, 2], F32)
        gn = sb("gn", [P, 2, 8, CT], F32)
        minus_half = sb("minus_half", [P, 16], F32)
        exp_top = sb("exp_top", [P, 1], F32)

        ps_u = ctx.enter_context(nc.psum_tensor("ps_u", [P, 4, HALF], F32))
        ps_a = ctx.enter_context(nc.psum_tensor("ps_a", [P, 2, HALF], F32))
        ps_o = ctx.enter_context(nc.psum_tensor("ps_o", [P, 2, HALF], F32))

        def pad_view(t, part, r0, c0, rows):
            m = y_pad[:, t, part, :].rearrange("p (r c) -> p r c", c=WP)
            return m[:, r0:r0 + rows, c0:c0 + W]

        def y_half(t, part, n):
            if t < HT:
                return y_plain[:, t, part, n * HALF:(n + 1) * HALF].rearrange("p (r c) -> p r c", c=W)
            return pad_view(t - HT, part, 1 + n * ROWS, 1, ROWS)

        def img(ap):
            return ap.rearrange("p (r c) -> p r c", c=W)

        HH = slice(0, HALF), slice(HALF, HW)

        def group_norm_stats(s, slot, tag, source_ready):
            g = gn[:, slot]
            aggr = [s.do("vector", lambda e, i, t=t: e.bn_aggr(mv[:, slot, t, :], stats[:, slot, t, :, :].rearrange("p a b -> p (a b)")),
                         after=[source_ready[t], s.last(tag + " factors used")], bare=True) for t in range(CT)]
            bank = s.last("O0 free")
            mean = s.pe(lambda e, i: e.matmul(ps_o[:, 0, 0:CT], group_mean[:, :], mv[:, slot, :, 0], start=True, stop=True),
                        after=[aggr[-1], bank])
            c1 = s.dve(lambda e, i: e.tensor_copy(g[:, 0, :], ps_o[:, 0, 0:CT]), after=[mean])
            c2 = s.dve(lambda e, i: e.tensor_tensor(g[:, 1, :], mv[:, slot, :, 0], g[:, 0, :], ALU.subtract), after=[c1])
            c3 = s.dve(lambda e, i: e.tensor_tensor(g[:, 2, :], g[:, 1, :], g[:, 1, :], ALU.mult), after=[c2])
            c4 = s.dve(lambda e, i: e.tensor_tensor(g[:, 3, :], g[:, 2, :], mv[:, slot, :, 1], ALU.add), after=[c3])
            var = s.pe(lambda e, i: e.matmul(ps_o[:, 0, 0:CT], group_mean[:, :], g[:, 3, :], start=True, stop=True),
                       after=[c4])
            c5 = s.dve(lambda e, i: e.tensor_scalar(g[:, 4, :], ps_o[:, 0, 0:CT], GN_EPS, None, ALU.add), after=[var])
            s.keep("O0 free", c5)
            rstd = s.pool(lambda e, i: e.tensor_tensor(g[:, 5, :], g[:, 4, :], minus_half[:, 0:CT], ALU.pow), after=[c5])
            c6 = s.dve(lambda e, i: e.tensor_scalar(g[:, 6, :], g[:, 5, :], ACTIVATION_SCALE, None, ALU.mult), after=[rstd])
            c7 = s.dve(lambda e, i: e.scalar_tensor_tensor(g[:, 7, :], g[:, 6, :], -1.0, g[:, 0, :], ALU.mult, ALU.mult), after=[c6])
            return c7

        wide_turn = [0]

        def normalise(s, slot, t, src, dst, ready, factors):
            w = wide_turn[0] % 2
            wide_turn[0] += 1
            g = gn[:, slot]
            f = s.dve(lambda e, i: e.tensor_scalar(wide[:, w, :], src, g[:, 6, t:t + 1], g[:, 7, t:t + 1], ALU.mult, ALU.add),
                      after=[ready, factors, s.last(f"wide{w} free")])
            hi = s.act(lambda e, i: e.activation(dst[:, 0, :], wide[:, w, :], ACT.Copy), after=[f])
            lo = s.dve(lambda e, i: e.tensor_tensor(dst[:, 1, :], wide[:, w, :], dst[:, 0, :], ALU.subtract), after=[hi])
            s.keep(f"wide{w} free", lo)
            return lo

        def load_x(s, batch_of):
            loaded = []
            for t in range(CT):
                def fn(e, i, t=t):
                    src = x[batch_of(i), t * P:(t + 1) * P, :, :].rearrange("b p h w -> p (b h w)")
                    return e.dma_start(xn[:, t, :], src)
                loaded.append(s.dma(f"x{t}", fn, after=[s.last("xn read")]))
            return loaded

        def group_norm_1(s, loaded):
            ready = []
            for t in range(CT):
                for n in range(2):
                    r = s.dve(lambda e, i, t=t, n=n: e.bn_stats(stats[:, 0, t, n, :], xn[:, t, HH[n]]), after=[loaded[t]])
                ready.append(r)
            factors = group_norm_stats(s, 0, "gn1", ready)
            parts = [normalise(s, 0, t, xn[:, t, :], xn_parts[:, t], loaded[t], factors) for t in range(CT)]
            s.keep("gn1 factors used", parts[-1])
            s.keep("gn1 parts", *parts)

        s = Section(nc, ctx, "setup", loop=False)
        stage = [qk[:, :], xn[:, :, :].rearrange("p t n -> p (t n)")]
        split = [probs[:, :, :, :, :].rearrange("p a b c d -> p (a b c d)"), y_pad[:, 0:4, :, :].rearrange("p a b c -> p (a b c)")]

        spare = q2_stack[:, :, :].rearrange("p h n -> p (h n)").bitcast(F32)
        spare_used = [0]

        def tmp(*shape):
            size = 1
            for n in shape:
                size *= n
            ap = spare[:, spare_used[0]:spare_used[0] + size]
            spare_used[0] += size
            names = "abcd"[:len(shape)]
            return ap.rearrange(f"p ({' '.join(names)}) -> p {' '.join(names)}", **dict(zip(names[1:], shape[1:]))) if len(shape) > 1 else ap

        ones = o_nat[:, 0, 0, :]
        m1 = s.pool(lambda e, i: e.memset(ident[:, :], 0.0))
        m2 = s.pool(lambda e, i: e.memset(group_mean[:, :], 1.0 / GROUP))
        m3 = s.pool(lambda e, i: e.memset(minus_half[:, :], -0.5))
        m4 = s.pool(lambda e, i: e.memset(ones, 1.0))
        s.pool(lambda e, i: e.memset(exp_top[:, :], EXP_TOP))
        id32 = s.pool(lambda e, i: e.affine_select(out=ident[:, :], in_=ident[:, :], compare_op=ALU.not_equal, fill=1.0,
                                                   base=0, pattern=[[-1, P]], channel_multiplier=1), after=[m1])
        gm3 = group_mean[:, :].rearrange("p (g q) -> p g q", q=GROUP)
        g1 = s.pool(lambda e, i: e.affine_select(out=gm3, in_=gm3, compare_op=ALU.is_ge, fill=0.0, base=0,
                                                 pattern=[[-GROUP, P // GROUP], [0, GROUP]], channel_multiplier=1), after=[m2])
        g2 = s.pool(lambda e, i: e.affine_select(out=gm3, in_=gm3, compare_op=ALU.is_ge, fill=0.0, base=GROUP - 1,
                                                 pattern=[[GROUP, P // GROUP], [0, GROUP]], channel_multiplier=-1), after=[g1])
        id16 = s.dve(lambda e, i: e.tensor_copy(ident16[:, :], ident[:, :]), after=[id32])

        bn_raw = {}
        with nc.allow_non_contiguous_dma(reason="a few KiB of parameters"):
            def bn_load(name, ap, tiles):
                t = tmp(4, tiles)
                bn_raw[name] = t
                return s.dma(f"bn_{name}", lambda e, i: e.dma_start(t[:, :, :], ap.rearrange("f (t p) -> p f t", p=P),
                                                                    allow_slow_non_contiguous=True))
            got_bn = {"cv1": bn_load("cv1", cv1_bn, CT), "cv2": bn_load("cv2", cv2_bn, CT)}
            for b in range(NB):
                got_bn[f"m1_{b}"] = bn_load(f"m1_{b}", m_cv1_bn[b], HT)
                got_bn[f"m2_{b}"] = bn_load(f"m2_{b}", m_cv2_bn[b], HT)
            got_r = []
            for b in range(NB):
                got_r.append(s.dma("r", lambda e, i, b=b: e.dma_start(
                    rw[:, b, :, :], m_rw[b].rearrange("a (t g) d h w -> (g d) (a t) (h w)", g=2))))
                got_r.append(s.dma("r", lambda e, i, b=b: e.dma_start(
                    rh[:, b, :, :], m_rh[b].rearrange("a (t g) d h w -> (g d) (a t) (h w)", g=2))))

        stage_turn = [0]
        bank_turn = [0]
        row_small = tmp(2, 4)

        def split_rows(w_f32, w_parts, unit_out, ready, slot):
            r = row_small[:, slot]
            a = s.dve(lambda e, i: e.tensor_reduce(r[:, 0:1], w_f32, AX.X, ALU.max, apply_absolute_value=True),
                      after=[ready, s.last(f"row_small{slot}")])
            b = s.dve(lambda e, i: e.tensor_scalar(r[:, 1:2], r[:, 0:1], 2.0 ** -100, None, ALU.max), after=[a])
            c = s.dve(lambda e, i: e.tensor_scalar(unit_out.bitcast(I32), r[:, 1:2].bitcast(I32), 0x7F800000, None,
                                                   ALU.bitwise_and), after=[b])
            d = s.dve(lambda e, i: e.reciprocal(r[:, 2:3], unit_out), after=[c])
            f = s.dve(lambda e, i: e.tensor_scalar(r[:, 3:4], r[:, 2:3], WEIGHT_TOP, None, ALU.mult), after=[d])
            g = s.act(lambda e, i: e.activation(w_f32, w_f32, ACT.Copy, scale=r[:, 3:4]), after=[f])
            hi = s.act(lambda e, i: e.activation(w_parts[0], w_f32, ACT.Copy), after=[g, s.last(f"split{slot} free")])
            lo = s.dve(lambda e, i: e.tensor_tensor(w_parts[1], w_f32, w_parts[0], ALU.subtract), after=[hi])
            s.keep(f"row_small{slot}", lo)
            s.keep(f"stage{slot} free", lo)
            return lo

        def transpose_out(blocks, ready):
            done = []
            for k in range(0, len(blocks), 8):
                part = blocks[k:k + 8]
                bank = bank_turn[0] % 4
                bank_turn[0] += 1
                pt = ps_u[:, bank, :].bitcast(F16)

                def fn(e, i, part=part, pt=pt):
                    for j, (src, _) in enumerate(part):
                        ins = e.transpose(pt[:, j * P:(j + 1) * P], src, ident16[:, :])
                    return ins
                t = s.pe(fn, after=[ready, id16, s.last(f"bank{bank} free")])
                runs = []
                for j, (_, (dst, count)) in enumerate(part):
                    if count:
                        runs.append((j, dst, count))
                for j, dst, count in runs:
                    src = pt[:, j * P:(j + count) * P]
                    if len(dst.shape) == 3:
                        src = src.rearrange("p (a b) -> p a b", a=count)
                    if bank % 2:
                        d = s.act(lambda e, i, dst=dst, src=src: e.activation(dst, src, ACT.Copy), after=[t])
                    else:
                        d = s.dve(lambda e, i, dst=dst, src=src: e.tensor_copy(dst, src), after=[t])
                s.keep(f"bank{bank} free", d)
                done.append(d)
            return done

        def weight_rows(name, rows, cols, dst_of, unit_out, taps=1):
            slot = stage_turn[0] % 2
            stage_turn[0] += 1
            wf = stage[slot][:, 0:cols * taps]
            wp = [split[slot][:, j * cols * taps:(j + 1) * cols * taps] for j in range(2)]
            got = s.dma(f"stage{slot}", lambda e, i: e.dma_start(wf, rows), after=[s.last(f"stage{slot} free")])
            parts = split_rows(wf, wp, unit_out, got, slot)
            blocks = []
            for j in range(2):
                for k in range(cols // P):
                    src = wp[j].rearrange("p (c t) -> p t c", t=taps)
                    if taps == 1:
                        blocks.append((src[:, 0, k * P:(k + 1) * P], (dst_of(j, k), 1)))
                    else:
                        for q in range(taps):
                            blocks.append((src[:, q, k * P:(k + 1) * P], (dst_of(j, k)[:, q, :], 1)))
            done = transpose_out(merge(blocks, taps, cols, dst_of), parts)
            s.keep(f"split{slot} free", *done)
            return done

        def merge(blocks, taps, cols, dst_of):
            if taps > 1:
                return blocks
            kt = cols // P
            out_blocks = []
            for n, (src, _) in enumerate(blocks):
                j, k = divmod(n, kt)
                out_blocks.append((src, (dst_of(j, slice(0, kt)), kt) if k == 0 else (None, 0)))
            return out_blocks

        w_done = []
        unit = {n: tmp(t) for n, t in (("cv1", CT), ("cv2", CT), ("m1", NB * HT), ("m2", NB * HT))}
        for b in range(NB):
            done_b = []
            for m in range(HT):
                before = s.last("w_c3 free")
                rows = m_cv1_w[b, m * P:(m + 1) * P].rearrange("o c h w -> o (c h w)")
                if before and m == 0:
                    s.keep("bank0 free", *s.last("bank0 free"), *before)
                    for q in range(1, 4):
                        s.keep(f"bank{q} free", *s.last(f"bank{q} free"), *before)
                done_b += weight_rows("c3", rows, CH, lambda j, k, m=m: w_c3[:, j, k, :, m * P:(m + 1) * P],
                                      unit["m1"][:, b * HT + m:b * HT + m + 1], TAPS)
            sent = s.dma("c3_out", lambda e, i, b=b: e.dma_start(
                w_c3_dram[b], w_c3[:, :, :, :, :].rearrange("p a b c d -> p (a b c d)")), after=[done_b])
            s.keep("w_c3 free", sent)
            w_done += done_b
        for m in range(CT):
            w_done += weight_rows("cv1", cv1_w[m * P:(m + 1) * P].rearrange("o c h w -> o (c h w)"), C,
                                  lambda j, k, m=m: w_cv1[:, j, k, m * P:(m + 1) * P], unit["cv1"][:, m:m + 1])
            w_done += weight_rows("cv2", cv2_w[m * P:(m + 1) * P].rearrange("o c h w -> o (c h w)"), YT * P,
                                  lambda j, k, m=m: w_cv2[:, j, k, m * P:(m + 1) * P], unit["cv2"][:, m:m + 1])
        for b in range(NB):
            for m in range(6):
                w_done += weight_rows("qkv", m_qkv_w[b, m * P:(m + 1) * P].rearrange("o c h w -> o (c h w)"), CH,
                                      lambda j, k, m=m, b=b: w_qkv[:, b, j, k, m * P:(m + 1) * P], qkv_unit[:, b, m:m + 1])
            for m in range(HT):
                w_done += weight_rows("m2", m_cv2_w[b, m * P:(m + 1) * P].rearrange("o c h w -> o (c h w)"), CH,
                                      lambda j, k, m=m, b=b: w_m2[:, b, j, k, m * P:(m + 1) * P],
                                      unit["m2"][:, b * HT + m:b * HT + m + 1])

        r1 = s.dve(lambda e, i: e.tensor_scalar(qkv_unit[:, :, 0:4], qkv_unit[:, :, 0:4], 1.0 / WEIGHT_TOP, None, ALU.mult), after=[w_done])
        r2 = s.dve(lambda e, i: e.tensor_scalar(qkv_unit[:, :, 4:6], qkv_unit[:, :, 4:6],
                                                ACTIVATION_SCALE / (WS * V_SHIFT), None, ALU.mult), after=[w_done])
        s.dve(lambda e, i: e.tensor_scalar(rw[:, :, :, :], rw[:, :, :, :], ACTIVATION_SCALE, None, ALU.mult), after=[got_r])
        s.dve(lambda e, i: e.tensor_scalar(rh[:, :, :, :], rh[:, :, :, :], ACTIVATION_SCALE, None, ALU.mult), after=[got_r])

        def bn_factors(name, raw, units, t0, tiles, out_scale):
            t = tmp(4, tiles)
            pt, py = par[name + "_t"][:, t0:t0 + tiles, :], par[name + "_y"][:, t0:t0 + tiles, :]
            a = s.dve(lambda e, i: e.tensor_scalar(t[:, 0, :], raw[:, 3, :], BN_EPS, None, ALU.add), after=[list(got_bn.values())])
            b = s.pool(lambda e, i: e.tensor_tensor(t[:, 1, :], t[:, 0, :], minus_half[:, 0:tiles], ALU.pow), after=[a, m3])
            c = s.dve(lambda e, i: e.tensor_tensor(t[:, 2, :], t[:, 1, :], raw[:, 0, :], ALU.mult), after=[b])
            d = s.dve(lambda e, i: e.tensor_tensor(t[:, 3, :], t[:, 2, :], raw[:, 2, :], ALU.mult), after=[c])
            f = s.dve(lambda e, i: e.tensor_tensor(t[:, 0, :], raw[:, 1, :], t[:, 3, :], ALU.subtract), after=[d])
            g = s.dve(lambda e, i: e.tensor_tensor(t[:, 1, :], t[:, 2, :], units, ALU.mult), after=[d, w_done])
            h = s.dve(lambda e, i: e.tensor_scalar(pt[:, :, 0], t[:, 1, :], 0.5 / WS, None, ALU.mult), after=[g])
            h = s.dve(lambda e, i: e.tensor_scalar(pt[:, :, 1], t[:, 0, :], 0.5, None, ALU.mult), after=[f])
            h = s.dve(lambda e, i: e.tensor_scalar(py[:, :, 0], t[:, 1, :], 0.5 * out_scale / WS, None, ALU.mult), after=[g])
            return s.dve(lambda e, i: e.tensor_scalar(py[:, :, 1], t[:, 0, :], 0.5 * out_scale, None, ALU.mult), after=[f])

        bn_factors("cv1", bn_raw["cv1"], unit["cv1"][:, :], 0, CT, ACTIVATION_SCALE)
        bn_factors("cv2", bn_raw["cv2"], unit["cv2"][:, :], 0, CT, 1.0)
        for b in range(NB):
            bn_factors("m1", bn_raw[f"m1_{b}"], unit["m1"][:, b * HT:(b + 1) * HT], b * HT, HT, ACTIVATION_SCALE)
            bn_factors("m2", bn_raw[f"m2_{b}"], unit["m2"][:, b * HT:(b + 1) * HT], b * HT, HT, ACTIVATION_SCALE)

        st = tmp(2, CT, G)
        st2 = tmp(2, CT, G)
        sm = tmp(8, 2, CT)
        iota_g = tmp(G)
        key_base = tmp(CT)
        iota_k = wide[:, 0, 0:C]
        got_s = s.dma("st", lambda e, i: e.dma_start(st[:, 0, :, :], S_logits.rearrange("(t p) g -> p t g", p=P)))
        got_t = s.dma("st", lambda e, i: e.dma_start(st[:, 1, :, :], T_logits.rearrange("(t p) g -> p t g", p=P)))
        i1 = s.pool(lambda e, i: e.iota(iota_g[:, :], pattern=[[1, G]], base=-G, channel_multiplier=0,
                                        allow_small_or_imprecise_dtypes=True))
        i2 = s.pool(lambda e, i: e.iota(key_base[:, :], pattern=[[P, CT]], base=0, channel_multiplier=1,
                                        allow_small_or_imprecise_dtypes=True))
        i3 = s.pool(lambda e, i: e.iota(iota_k, pattern=[[1, C]], base=0, channel_multiplier=0,
                                        allow_small_or_imprecise_dtypes=True), after=[m4])

        def bc(ap, n):
            return ap.unsqueeze(3).to_broadcast([P, 2, CT, n])
        a = s.dve(lambda e, i: e.tensor_reduce(sm[:, 0], st[:, :, :, :], AX.X, ALU.max), after=[got_s, got_t])
        a = s.dve(lambda e, i: e.tensor_tensor(st[:, :, :, :], st[:, :, :, :], bc(sm[:, 0], G), ALU.subtract), after=[a])
        a = s.act(lambda e, i: e.activation(st2[:, :, :, :], st[:, :, :, :], ACT.Exp), after=[a])
        a = s.dve(lambda e, i: e.tensor_reduce(sm[:, 1], st2[:, :, :, :], AX.X, ALU.add), after=[a])
        a = s.dve(lambda e, i: e.reciprocal(sm[:, 2], sm[:, 1]), after=[a])
        a = s.dve(lambda e, i: e.tensor_tensor(st2[:, :, :, :], st2[:, :, :, :], bc(sm[:, 2], G), ALU.mult), after=[a])
        gain = s.dve(lambda e, i: e.tensor_reduce(sm[:, 3], st2[:, :, :, :], AX.X, ALU.max), after=[a])
        a = s.dve(lambda e, i: e.tensor_tensor(st[:, :, :, :], st2[:, :, :, :], bc(sm[:, 3], G), ALU.is_ge), after=[gain])
        a = s.dve(lambda e, i: e.tensor_tensor(st[:, :, :, :], st[:, :, :, :],
                                               iota_g[:, :].unsqueeze(1).unsqueeze(1).to_broadcast([P, 2, CT, G]), ALU.mult), after=[a, i1])
        arg = s.dve(lambda e, i: e.tensor_reduce(sm[:, 4], st[:, :, :, :], AX.X, ALU.min), after=[a])
        key = s.dve(lambda e, i: e.scalar_tensor_tensor(sm[:, 5, 1, :], sm[:, 4, 1, :], float(C), key_base[:, :],
                                                        ALU.mult, ALU.add), after=[arg, i2])
        diag = o_nat[:, 1, 0:CT, :]

        def rows_of(col, ready, dst):
            last = ready
            for t in range(CT):
                last = s.dve(lambda e, i, t=t: e.tensor_scalar(diag[:, t, :], ident[:, :], col[:, t:t + 1], None, ALU.mult),
                             after=[last, id32, s.last("diag free")])

            def fn(e, i):
                for t in range(CT):
                    ins = e.matmul(ps_a[:, 0, t * P:(t + 1) * P], ones, diag[:, t, :], start=True, stop=True)
                return ins
            mm = s.pe(fn, after=[last, m4, s.last("a0 free")])
            cp = s.dve(lambda e, i: e.tensor_copy(dst, ps_a[:, 0, :]), after=[mm])
            s.keep("diag free", mm)
            s.keep("a0 free", cp)
            return cp
        s_row, g_row, k_row = x_again[:, 0, :], x_again[:, 1, :], wide[:, 0, C:2 * C]
        rs = rows_of(sm[:, 4, 0, :], arg, s_row)
        rg = rows_of(sm[:, 3, 0, :], gain, g_row)
        rk = rows_of(sm[:, 5, 1, :], key, k_row)
        rank = tmp(CT)
        cmp_ = wide[:, 1, 0:C]
        one_hot = z[:, :, :, :].rearrange("p a b c -> p (a b c)").bitcast(F32).rearrange("p (t k) -> p t k", t=CT)
        one_hot16 = v_ext[:, :, :, :].rearrange("p a b c -> p (a b c)")[:, 0:CT * C].rearrange("p (t k) -> p t k", t=CT)
        hot = []
        last = rk
        for t in range(CT):
            last = s.dve(lambda e, i, t=t: e.tensor_scalar(cmp_, k_row, sm[:, 5, 1, t:t + 1], None, ALU.is_lt), after=[last])
            last = s.dve(lambda e, i, t=t: e.tensor_reduce(rank[:, t:t + 1], cmp_, AX.X, ALU.add), after=[last])
            last = s.dve(lambda e, i, t=t: e.tensor_scalar(one_hot[:, t, :], iota_k, rank[:, t:t + 1], None, ALU.is_equal), after=[last, i3])
            hot.append(last)
            hot.append(s.dve(lambda e, i, t=t: e.tensor_copy(one_hot16[:, t, :], one_hot[:, t, :]), after=[last]))
        wl = y_plain[:, :, :, :].rearrange("p a b c -> p (a b c)").bitcast(F32).rearrange("p (t c) -> p t c", t=CT)
        masked = []
        for t in range(CT):
            got = s.dma(f"conv{t}", lambda e, i, t=t: e.dma_start(wl[:, t, :], conv[t * P:(t + 1) * P].rearrange("o c h w -> o (c h w)")))
            a = s.dve(lambda e, i, t=t: e.tensor_scalar(cmp_, s_row, sm[:, 4, 1, t:t + 1], sm[:, 3, 1, t:t + 1], ALU.is_equal, ALU.mult),
                      after=[rs, hot, masked])
            a = s.dve(lambda e, i, t=t: e.tensor_tensor(cmp_, cmp_, g_row, ALU.mult), after=[a, rg])
            masked.append(s.dve(lambda e, i, t=t: e.tensor_tensor(wl[:, t, :], wl[:, t, :], cmp_, ALU.mult), after=[a, got]))
        v_unit = tmp(CT)
        vp = split[0][:, 0:2 * CT * C].rearrange("p (t s c) -> p t s c", t=CT, s=2)
        v_done = []
        for m in range(CT):
            bank = m % 2

            def fn(e, i, m=m, bank=bank):
                for t in range(CT):
                    ins = e.matmul(ps_o[:, bank, :], one_hot[:, t, m * P:(m + 1) * P], wl[:, t, :], start=(t == 0), stop=(t == CT - 1))
                return ins
            mm = s.pe(fn, after=[masked, hot, s.last(f"perm{bank} free")])
            wf = stage[0][:, m * C:(m + 1) * C]
            cp = s.dve(lambda e, i, wf=wf, bank=bank: e.tensor_copy(wf, ps_o[:, bank, :]), after=[mm, s.last("stage0 free"), s.last("stage1 free")])
            s.keep(f"perm{bank} free", cp)
            s.keep("split0 free", *s.last("split0 free"), *s.last("split1 free"))
            v_done.append(split_rows(wf, [vp[:, m, 0, :], vp[:, m, 1, :]], v_unit[:, m:m + 1], cp, 0))
        for c in range(CT):
            for j in range(2):
                bank = (2 * c + j) % 2

                def fn(e, i, c=c, j=j, bank=bank):
                    for t in range(CT):
                        ins = e.matmul(ps_o[:, bank, :], vp[:, t, j, c * P:(c + 1) * P], one_hot16[:, t, :], start=(t == 0), stop=(t == CT - 1))
                    return ins
                mm = s.pe(fn, after=[v_done, hot, s.last(f"perm{bank} free")])
                cp = s.dve(lambda e, i, c=c, j=j, bank=bank: e.tensor_copy(w_l1[:, j, c, :], ps_o[:, bank, :]), after=[mm])
                s.keep(f"perm{bank} free", cp)

        def fn(e, i):
            for n in range(CT):
                for t in range(CT):
                    ins = e.matmul(ps_a[:, 0, n:n + 1], one_hot[:, t, n * P:(n + 1) * P], v_unit[:, t:t + 1], start=(t == 0), stop=(t == CT - 1))
            return ins
        mm = s.pe(fn, after=[v_done, s.last("a0 free")])
        l1f = s.dve(lambda e, i: e.tensor_scalar(l1_unit[:, :], ps_a[:, 0, 0:CT], 1.0 / WS, None, ALU.mult), after=[mm])

        all_pe = [mm, l1f]
        s.pool(lambda e, i: e.memset(y_pad[:, :, :, :], 0.0), after=[all_pe, s.last("split1 free")])
        k2z = s.pool(lambda e, i: e.memset(k2_stack[:, :, :], 0.0))
        for h in range(HEADS):
            row = HD if h % 2 == 0 else 0
            s.dve(lambda e, i, h=h, row=row: e.memset(k2_stack[row:row + 1, h, :], SHIFT_UNIT), after=[k2z])
        s.pool(lambda e, i: e.memset(q2_stack[:, :, :], 0.0), after=[Done(s.sem("vector"), s.sem("vector").n)])
        s.dve(lambda e, i: e.memset(v_ext[:, :, :, :], 1.0), after=[all_pe])
        s.keep("xn read", *s.last("stage1 free"))
        s.keep("wide0 free", *masked, *hot)
        s.keep("wide1 free", *masked, *hot)
        s.keep("O0 free", *s.last("perm0 free"))
        group_norm_1(s, load_x(s, lambda i: slice(0, 1)))
        setup = s

        s = Section(nc, ctx, "batch", loop=True)
        s.held = Sem(ctx.enter_context(nc.semaphore("held")))
        s.kept["gn1 parts"] = []
        turn = [0]

        def unit_group(matmuls, after, width=HALF):
            bank = turn[0] % 4
            turn[0] += 1

            def fn(e, i):
                for k, (lhsT, rhs) in enumerate(matmuls):
                    ins = e.matmul(ps_u[:, bank, :], lhsT, rhs, start=(k == 0), stop=(k == len(matmuls) - 1))
                return ins
            return bank, s.pe(fn, after=[after, s.last(f"U{bank} free")])

        def three(w_of, x_of):
            return [(w_of(0), x_of(0)), (w_of(0), x_of(1)), (w_of(1), x_of(0))]

        small_turn = [0]

        def silu(bank, mm, name, t, after=()):
            slot = small_turn[0] % 2
            small_turn[0] += 1
            th, yh = wide[:, slot, 0:HALF], wide[:, slot, HALF:HW]
            pt, py = par[name + "_t"], par[name + "_y"]
            a = s.act(lambda e, i: e.activation(th, ps_u[:, bank, :], ACT.Tanh, scale=pt[:, t, 0:1], bias=pt[:, t, 1:2]),
                      after=[mm, s.last(f"wide{slot} free")])
            b = s.act(lambda e, i: e.activation(yh, ps_u[:, bank, :], ACT.Identity, scale=py[:, t, 0:1], bias=py[:, t, 1:2]),
                      after=[mm])
            s.keep(f"U{bank} free", b)
            u = s.dve(lambda e, i: e.scalar_tensor_tensor(yh, th, 1.0, yh, ALU.add, ALU.mult), after=[a, b])
            return yh, u, slot

        def split_to(u, ready, hi, lo, slot, after=()):
            a = s.pool(lambda e, i: e.tensor_scalar(hi, u, 1.0, 0.0, ALU.mult, ALU.add), after=[ready, after])
            b = s.dve(lambda e, i: e.tensor_tensor(lo, u, hi, ALU.subtract), after=[a])
            s.keep(f"wide{slot} free", b)
            return b

        def add_to(u, other, ready):
            return s.dve(lambda e, i: e.tensor_tensor(img(u), img(u), other, ALU.add), after=[ready])

        y_ready = {}
        for m in [2, 3, 0, 1]:
            for n in range(2):
                mms = []
                for k in range(CT):
                    mms += three(lambda j: w_cv1[:, j, k, m * P:(m + 1) * P], lambda j: xn_parts[:, k, j, HH[n]])
                bank, mm = unit_group(mms, [s.last("gn1 parts ahead")])
                u, ready, slot = silu(bank, mm, "cv1", m)
                y_ready[m, n] = split_to(img(u), ready, y_half(m, 0, n), y_half(m, 1, n), slot, after=[s.last("y free")])
        s.keep("xn read", mm)

        loaded = load_x(s, lambda i: bass.ds((i + 1) % B, 1))

        def bottleneck(b):
            y0 = HT + b * HT
            c3 = s.dma("c3", lambda e, i, b=b: e.dma_start(w_c3[:, :, :, :, :].rearrange("p a b c d -> p (a b c d)"), w_c3_dram[b]),
                       after=[s.last("w_c3 read")])
            z_ready = {}
            for n in range(2):
                for m in range(HT):
                    mms = []
                    for k in range(HT):
                        for q in range(TAPS):
                            dy, dx = divmod(q, 3)
                            mms += three(lambda j: w_c3[:, j, k, q, m * P:(m + 1) * P],
                                         lambda j: pad_view(y0 - HT + k, j, n * ROWS + dy, dx, ROWS))
                    bank, mm = unit_group(mms, [c3] + [y_ready[y0 + k, nn] for k in range(HT) for nn in range(2)])
                    u, ready, slot = silu(bank, mm, "m1", b * HT + m)
                    z_ready[m, n] = split_to(u, ready, z[:, m, 0, HH[n]], z[:, m, 1, HH[n]], slot, after=[s.last("z free")])
            s.keep("w_c3 read", mm)

            if b == 1:
                group_norm_1(s, loaded)
                s.keep("gn1 parts ahead", *s.kept["gn1 parts"])

            q_ready = {h: [] for h in range(HEADS)}
            k_ready = {h: [] for h in range(HEADS)}
            v_ready = []
            z_all = {n: [z_ready[m, n] for m in range(HT)] for n in range(2)}

            def project(kind, pair, n):
                m = 2 * kind + pair
                mms = []
                for k in range(HT):
                    mms += three(lambda j: w_qkv[:, b, j, k, m * P:(m + 1) * P], lambda j: z[:, k, j, HH[n]])
                bank, mm = unit_group(mms, z_all[n])
                slot = small_turn[0] % 2
                small_turn[0] += 1
                f = wide[:, slot, 0:HALF]
                px = ps_u[:, bank, :]
                free = [s.last(f"wide{slot} free")]
                even, odd = 2 * pair, 2 * pair + 1
                if kind == 0:
                    full = s.act(lambda e, i: e.activation(f, px, ACT.Identity, scale=qkv_unit[:, b, m:m + 1]), after=[mm, free])
                    s.keep(f"U{bank} free", full)
                else:
                    a = s.dve(lambda e, i: e.scalar_tensor_tensor(
                        img(f), img(px), qkv_unit[:, b, m:m + 1], rw[:, b, pair, :].unsqueeze(1).to_broadcast([P, ROWS, W]),
                        ALU.mult, ALU.add), after=[mm, free])
                    s.keep(f"U{bank} free", a)
                    full = s.dve(lambda e, i: e.tensor_tensor(
                        img(f), img(f), rh[:, b, pair, n * ROWS:(n + 1) * ROWS].unsqueeze(2).to_broadcast([P, ROWS, W]), ALU.add), after=[a])
                free_st = [s.last("qk free")]
                last = []
                for h, nat, oth in ((even, slice(0, HD), slice(HD, P)), (odd, slice(HD, P), slice(0, HD))):
                    cols = HH[n]
                    if kind == 0:
                        hi = s.dve(lambda e, i, h=h, nat=nat: e.tensor_copy(q_stack[nat, h, cols], f[nat]), after=[full, free_st])
                        lo = s.dve(lambda e, i, h=h, nat=nat, oth=oth: e.tensor_tensor(q_stack[oth, h, cols], f[nat], q_stack[nat, h, cols], ALU.subtract), after=[hi])
                        dup = s.dve(lambda e, i, h=h, nat=nat: e.tensor_copy(q2_stack[nat, h, cols], q_stack[nat, h, cols]), after=[hi])
                        q_ready[h] += [lo, dup]
                        last += [lo]
                    else:
                        hi = s.act(lambda e, i, h=h, nat=nat: e.activation(k_stack[nat, h, cols], f[nat], ACT.Copy), after=[full, free_st])
                        dup = s.act(lambda e, i, h=h, nat=nat, oth=oth: e.activation(k_stack[oth, h, cols], f[nat], ACT.Copy), after=[full])
                        lo = s.dve(lambda e, i, h=h, nat=nat: e.tensor_tensor(k2_stack[nat, h, cols], f[nat], k_stack[nat, h, cols], ALU.subtract), after=[hi])
                        k_ready[h] += [lo, dup]
                        last += [lo, dup]
                s.keep(f"wide{slot} free", *last)

            def project_v(jj):
                bank = turn[0] % 4
                turn[0] += 1

                def fn(e, i):
                    for q in range(2):
                        px = ps_u[:, bank, q * CH:(q + 1) * CH]
                        j = slice((2 * jj + q) * P, (2 * jj + q + 1) * P)
                        mms = []
                        for k in range(HT):
                            mms += [(z[:, k, a, j], w_qkv[:, b, c, k, 2 * CH:3 * CH]) for a, c in ((0, 0), (0, 1), (1, 0))]
                        for t, (lhsT, rhs) in enumerate(mms):
                            ins = e.matmul(px, lhsT, rhs, start=(t == 0), stop=(t == len(mms) - 1))
                    return ins
                mm = s.pe(fn, after=[z_all[jj // 2], s.last(f"U{bank} free")])
                px = ps_u[:, bank, :].rearrange("p (a d) -> p a d", d=HD)
                ve = v_ext[:, 2 * jj:2 * jj + 2, :, :].rearrange("p j h d -> p (j h) d")
                hi = s.act(lambda e, i: e.activation(ve[:, :, 0:HD], px, ACT.Copy, scale=V_SHIFT), after=[mm, s.last("v free")])
                lo = s.dve(lambda e, i: e.scalar_tensor_tensor(ve[:, :, HD + 1:2 * HD + 1], px, V_SHIFT, ve[:, :, 0:HD], ALU.mult, ALU.subtract), after=[hi])
                s.keep(f"U{bank} free", lo)
                v_ready.append(lo)

            a_turn = [0]

            def max_tile(h, it, n):
                bank = a_turn[0] % 2
                a_turn[0] += 1
                mm = s.pe(lambda e, i: e.matmul(ps_a[:, bank, :], q_stack[:, h, it * P:(it + 1) * P], k_stack[:, h, HH[n]], start=True, stop=True),
                          after=[q_ready[h], k_ready[h], s.last(f"A{bank} free")])
                d = s.dve(lambda e, i: e.reduce_max(row_max[:, h % 2, it, n:n + 1], ps_a[:, bank, :], axis=AX.X),
                          after=[mm, s.last(f"row_max{h % 2} free")])
                s.keep(f"A{bank} free", d)
                return d

            def shifts(h, maxima):
                a = s.dve(lambda e, i: e.tensor_reduce(shift[:, h % 2, 0, :], row_max[:, h % 2, :, :], AX.X, ALU.max), after=[maxima])
                s.keep(f"row_max{h % 2} free", a)
                return s.dve(lambda e, i: e.tensor_scalar(shift16[:, h % 2, :], shift[:, h % 2, 0, :], -1.0 / SHIFT_UNIT, None, ALU.mult),
                             after=[a, s.last(f"shift{h % 2} free")])

            def shift_row(h, ready):
                def fn(e, i):
                    for it in range(JT):
                        ins = e.matmul(ps_a[:, it // 4, (it % 4) * P:(it % 4 + 1) * P],
                                       shift16[:, h % 2, it:it + 1].to_broadcast([P, P]), ident16[:, :], start=True, stop=True)
                    return ins
                mm = s.pe(fn, after=[ready, s.last("A0 free"), s.last("A1 free")])
                s.keep(f"shift{h % 2} free", mm)
                row = slice(HD, HD + 1) if h % 2 == 0 else slice(0, 1)
                got = []
                for n in range(2):
                    c = s.act(lambda e, i, n=n: e.activation(q2_stack[row, h, HH[n]], ps_a[row, n, :], ACT.Copy), after=[mm, s.last("qk free")])
                    s.keep(f"A{n} free", c)
                    got.append(c)
                q_ready[h] += got

            for n in range(2):
                for pair in range(2):
                    project(0, pair, n)
                    project(1, pair, n)
                project_v(2 * n)
                project_v(2 * n + 1)
            maxima = [max_tile(0, it, n) for it in range(JT) for n in range(2)]
            shift_row(0, shifts(0, maxima))

            STEPS = HEADS * 8
            exp_done, lo_done, chunk_lo = {}, {}, {}
            raw_turn = [0]
            transposed = []

            def logits_step(st_):
                h, c, g = st_ // 8, st_ % 8 // 2, st_ % 2
                q0 = c * QC
                pair_bank = turn[0] // 2 % 2
                turn[0] += 2

                def fn(e, i):
                    for jt in range(4):
                        j = slice((4 * g + jt) * P, (4 * g + jt + 1) * P)
                        o = ps_u[:, 2 * pair_bank + jt // 2, (jt % 2) * QC:(jt % 2 + 1) * QC]
                        e.matmul(o, k_stack[:, h, j], q_stack[:, h, q0:q0 + QC], start=True, stop=False)
                        ins = e.matmul(o, k2_stack[:, h, j], q2_stack[:, h, q0:q0 + QC], start=False, stop=True)
                    return ins
                mm = s.pe(fn, after=[q_ready[h], k_ready[h], s.last(f"U{2 * pair_bank} free"), s.last(f"U{2 * pair_bank + 1} free")])
                slot = (st_ // 2) % 2
                w = st_ % 2
                ex = s.act(lambda e, i: e.activation(wide[:, w, :], ps_u[:, 2 * pair_bank:2 * pair_bank + 2, :].rearrange("p a b -> p (a b)"),
                                                     ACT.Exp, scale=1.0 / (ACTIVATION_SCALE ** 2 * HD ** 0.5), bias=exp_top[:, 0:1]),
                           after=[mm, s.last(f"wide{w} free")])
                s.keep(f"U{2 * pair_bank} free", ex)
                s.keep(f"U{2 * pair_bank + 1} free", ex)
                dst = probs[:, slot, 0, 4 * g:4 * g + 4, :].rearrange("p j q -> p (j q)")
                free = s.last(f"probs{slot} free")
                if st_ % 4 == 3:
                    hi = s.act(lambda e, i: e.activation(dst, wide[:, w, :], ACT.Copy), after=[ex, free])
                else:
                    hi = s.pool(lambda e, i: e.tensor_scalar(dst, wide[:, w, :], 1.0, 0.0, ALU.mult, ALU.add), after=[ex, free])
                exp_done[st_] = hi

            def low_step(st_):
                slot, g, w = (st_ // 2) % 2, st_ % 2, st_ % 2
                src = probs[:, slot, 0, 4 * g:4 * g + 4, :].rearrange("p j q -> p (j q)")
                dst = probs[:, slot, 1, 4 * g:4 * g + 4, :].rearrange("p j q -> p (j q)")
                lo = s.dve(lambda e, i: e.tensor_tensor(dst, wide[:, w, :], src, ALU.subtract), after=[exp_done[st_]])
                s.keep(f"wide{w} free", lo)
                lo_done[st_] = lo

            o_turn = [0]
            av_bank = {}

            def av_half(chunk, half):
                h, slot = chunk // 4, chunk % 2
                if half == 0:
                    av_bank[chunk] = o_turn[0] % 2
                    o_turn[0] += 1
                bank = av_bank[chunk]

                def fn(e, i):
                    for jt in range(JT):
                        cols = slice(half * P, (half + 1) * P)
                        o = ps_o[:, bank, half * QC:half * QC + 2 * HD + 1]
                        e.matmul(o, probs[:, slot, 0, jt, cols], v_ext[:, jt, h, 0:2 * HD + 1], start=(jt == 0), stop=False)
                        ins = e.matmul(o[:, 0:HD + 1], probs[:, slot, 1, jt, cols], v_ext[:, jt, h, 0:HD + 1], start=False,
                                       stop=(jt == JT - 1))
                    return ins
                mm = s.pe(fn, after=[lo_done[2 * chunk], lo_done[2 * chunk + 1], v_ready, s.last(f"O{bank} free")])
                if half == 0:
                    return
                s.keep(f"probs{slot} free", mm)
                r = raw_turn[0] % 2
                raw_turn[0] += 1
                src = ps_o[:, bank, :].rearrange("p (a q) -> p a q", a=2)[:, :, 0:2 * HD + 1]
                c = s.act(lambda e, i: e.activation(o_raw[:, r, :, :], src, ACT.Copy), after=[mm, s.last(f"raw{r} free")])
                s.keep(f"O{bank} free", c)
                rc = s.dve(lambda e, i: e.reciprocal(recip[:, r, :], o_raw[:, r, :, HD]), after=[c])
                ad = s.dve(lambda e, i: e.tensor_tensor(o_raw[:, r, :, 0:HD], o_raw[:, r, :, 0:HD], o_raw[:, r, :, HD + 1:2 * HD + 1], ALU.add), after=[c])
                it = chunk % 4 * 2
                par_ = h // 2 % 2
                nr = s.dve(lambda e, i: e.tensor_tensor(o_nat[:, par_, it:it + 2, h % 2 * HD:h % 2 * HD + HD], o_raw[:, r, :, 0:HD],
                                                        recip[:, r, :].unsqueeze(2).to_broadcast([P, 2, HD]), ALU.mult),
                           after=[rc, ad, s.last(f"o_nat{par_} free")])
                s.keep(f"raw{r} free", nr)
                norm_done[chunk] = nr

            norm_done = {}

            def transpose_half(pair, n):
                bank = o_turn[0] % 2
                o_turn[0] += 1

                def fn(e, i):
                    for q in range(4):
                        ins = e.transpose(ps_o[:, bank, q * P:(q + 1) * P], o_nat[:, pair, 4 * n + q, :], ident[:, :])
                    return ins
                need = [norm_done[8 * pair + 4 * hh + 2 * n + cc] for hh in range(2) for cc in range(2)]
                mm = s.pe(fn, after=[need, s.last(f"O{bank} free")])
                if n == 1:
                    s.keep(f"o_nat{pair} free", mm)
                u = qkv_unit[:, b, 4 + pair:5 + pair]
                hi = s.act(lambda e, i: e.activation(z[:, pair, 0, HH[n]], ps_o[:, bank, :], ACT.Copy, scale=u), after=[mm, s.last("z projected")])
                lo = s.dve(lambda e, i: e.scalar_tensor_tensor(z[:, pair, 1, HH[n]], ps_o[:, bank, :], u, z[:, pair, 0, HH[n]], ALU.mult, ALU.subtract), after=[hi])
                s.keep(f"O{bank} free", lo)
                o_ready[pair, n] = lo

            o_ready = {}
            s.keep("z projected", Done(s.sem("tensor"), s.sem("tensor").n))
            if turn[0] % 2:
                turn[0] += 1
            tiles_in_step = [3, 3, 3, 3, 2, 2, 0, 0]
            for st_ in range(STEPS + 5):
                if st_ >= 3 and st_ - 3 < STEPS:
                    k = st_ - 3
                    av_half(k // 2, k % 2)
                if st_ < STEPS:
                    logits_step(st_)
                    h = st_ // 8
                    if h + 1 < HEADS:
                        pos = st_ % 8
                        if pos == 0:
                            tiles = [(it, n) for it in range(JT) for n in range(2)]
                            maxima = []
                        for _ in range(tiles_in_step[pos]):
                            maxima.append(max_tile(h + 1, *tiles.pop(0)))
                        if pos == 6:
                            sh = shifts(h + 1, maxima)
                        if pos == 7:
                            shift_row(h + 1, sh)
                if 1 <= st_ <= STEPS:
                    low_step(st_ - 1)
                if st_ in (21, 22):
                    transpose_half(0, st_ - 21)
            for n in range(2):
                transpose_half(1, n)
            s.keep("qk free", Done(s.sem("tensor"), s.sem("tensor").n))
            s.keep("v free", Done(s.sem("tensor"), s.sem("tensor").n))

            for n in range(2):
                for m in range(HT):
                    mms = []
                    for k in range(HT):
                        mms += three(lambda j: w_m2[:, b, j, k, m * P:(m + 1) * P], lambda j: z[:, k, j, HH[n]])
                    bank, mm = unit_group(mms, [o_ready[0, n], o_ready[1, n]])
                    u, ready, slot = silu(bank, mm, "m2", b * HT + m)
                    a = add_to(u, y_half(y0 + m, 0, n), ready)
                    a = add_to(u, y_half(y0 + m, 1, n), a)
                    t = y0 + HT + m
                    y_ready[t, n] = split_to(img(u), a, y_half(t, 0, n), y_half(t, 1, n), slot, after=[s.last("y free")])
            s.keep("z free", mm)

        for b in range(NB):
            bottleneck(b)

        def cv2_unit(m, n):
            mms = []
            for k in range(YT):
                mms += three(lambda j: w_cv2[:, j, k, m * P:(m + 1) * P], lambda j: y_half(k, j, n))
            bank, mm = unit_group(mms, [y_ready[k, n] for k in range(YT)])
            u, ready, slot = silu(bank, mm, "cv2", m)
            xa = (2 * m + n) % 2

            def fn(e, i):
                src = x[bass.ds(i, 1), m * P:(m + 1) * P, n * ROWS:(n + 1) * ROWS, :].rearrange("b p h w -> p (b h w)")
                return e.dma_start(x_again[:, xa, :], src)
            got = s.dma(f"again{xa}", fn, after=[s.last(f"x_again{xa} free")])
            a = s.dve(lambda e, i: e.tensor_tensor(x1[:, m, HH[n]], u, x_again[:, xa, :], ALU.add),
                      after=[ready, got, s.last("qk free"), s.last("x1 stored")])
            s.keep(f"wide{slot} free", a)
            s.keep(f"x_again{xa} free", a)
            return mm, s.dve(lambda e, i: e.bn_stats(stats[:, 1, m, n, :], x1[:, m, HH[n]]), after=[a])

        ready2 = []
        for m in range(CT):
            for n in range(2):
                mm, stat = cv2_unit(m, n)
            ready2.append(stat)
        s.keep("y free", mm)
        factors = group_norm_stats(s, 1, "gn2", ready2)
        parts = [normalise(s, 1, t, x1[:, t, :], x1_parts[:, t], [], [factors, s.last("probs0 free"), s.last("probs1 free")]) for t in range(CT)]
        s.keep("gn2 factors used", parts[-1])
        def l1_unit_group(m, n):
            mms = []
            for k in range(CT):
                mms += three(lambda j: w_l1[:, j, k, m * P:(m + 1) * P], lambda j: x1_parts[:, k, j, HH[n]])
            bank, mm = unit_group(mms, [parts])
            a = s.dve(lambda e, i: e.scalar_tensor_tensor(x1[:, m, HH[n]], ps_u[:, bank, :], l1_unit[:, m:m + 1], x1[:, m, HH[n]],
                                                          ALU.mult, ALU.add), after=[mm, parts])
            s.keep(f"U{bank} free", a)
            return mm, a

        stored = []
        for m in range(CT):
            for n in range(2):
                mm, a = l1_unit_group(m, n)

            def fn(e, i, m=m):
                return e.dma_start(out[bass.ds(i, 1), m * P:(m + 1) * P, :, :].rearrange("b p h w -> p (b h w)"), x1[:, m, :])
            stored.append(s.dma(f"out{m}", fn, after=[a]))
        s.keep("qk free", *stored)
        s.keep("x1 stored", *stored)
        s.keep("probs0 free", mm)
        s.keep("probs1 free", mm)
        body = s

        block = ctx.enter_context(nc.Block())

        def program(name):
            def run(e):
                setup.emit(name, e, None)
                setup.finals(e)
                for sname, sm_ in body.sems.items():
                    if sname == name or (name == "sync" and sname not in Section.ENGINES):
                        e.sem_inc(sm_.handle, sm_.n)
                with e.Fori(0, B) as i:
                    body.emit(name, e, i)
                if name == "sync":
                    for m in range(CT):
                        e.wait_ge(body.sems[f"out{m}"].handle, (B + 1) * 16)
            return run
        block.sync(program("sync"))
        block.tensor(program("tensor"))
        block.vector(program("vector"))
        block.scalar(program("scalar"))
        block.gpsimd(program("gpsimd"))


_INS = ["x", "L0_conv_cv1_w", "L0_conv_cv1_bn", "L0_conv_cv2_w", "L0_conv_cv2_bn", "L0_conv_m_cv1_w", "L0_conv_m_cv1_bn",
        "L0_conv_m_qkv_w", "L0_conv_m_rw", "L0_conv_m_rh", "L0_conv_m_cv2_w", "L0_conv_m_cv2_bn", "L1_conv_conv",
        "L1_conv_S", "L1_conv_T"]


def kernel(**inputs):
    import numpy as _np
    import concourse.bacc as _bacc
    from concourse import mybir as _mybir
    from concourse.bass_utils import run_bass_kernel_spmd as _run

    nc = _bacc.Bacc("TRN2", target_bir_lowering=False, num_devices=1)
    arrays, args = {}, []
    for name in _INS:
        a = _np.ascontiguousarray(inputs[name])
        arrays[f"in_{name}_dram"] = a
        args.append(nc.dram_tensor(f"in_{name}_dram", a.shape, _mybir.dt.from_np(a.dtype), kind="ExternalInput").ap())
    shape = inputs["x"].shape
    args.append(nc.dram_tensor("out_0_dram", shape, _mybir.dt.float32, kind="ExternalOutput").ap())
    build(nc, *args)
    r = _run(nc, [arrays], core_ids=[0])
    return r.results[0]["out_0_dram"]
```

```python
from contextlib import ExitStack

import concourse.bass as bass
from concourse import mybir
from concourse.alu_op_type import AluOpType as ALU

ACT = mybir.ActivationFunctionType
AX = mybir.AxisListType
F32 = mybir.dt.float32
F16 = mybir.dt.float16
I32 = mybir.dt.int32

P = 128
ACTIVATION_SCALE = 16.0
WEIGHT_TOP = 64.0
WS = WEIGHT_TOP * ACTIVATION_SCALE
V_SHIFT = 2.0 ** -8
SHIFT_UNIT = 1024.0
EXP_TOP = 5.545177444479562
BN_EPS, GN_EPS = 1e-3, 1e-5
R_UNIT = 256.0
WIDES, PROBS = 4, 3
DMA_SCRATCH = 1024


class Done:

    def __init__(self, sem, count, lag=0):
        self.sem, self.count, self.lag = sem, count, lag


class Sem:
    def __init__(self, handle):
        self.handle, self.n = handle, 0


class Later:
    def __init__(self, name):
        self.name = name


def flat(after):
    return [d for a in after for d in (flat(a) if isinstance(a, (list, tuple)) else [a])]


class Section:

    ENGINES = ("tensor", "scalar", "vector", "gpsimd", "sync")

    def __init__(self, nc, ctx, name, loop):
        self.nc, self.ctx, self.name, self.loop = nc, ctx, name, loop
        self.queue = {e: [] for e in self.ENGINES}
        self.sems = {}
        self.kept = {}

    def sem(self, name):
        if name not in self.sems:
            self.sems[name] = Sem(self.ctx.enter_context(self.nc.semaphore(f"{self.name}_{name}")))
        return self.sems[name]

    def do(self, engine, fn, after=(), sem=None, inc=1, bare=False):
        s = self.sem(sem or engine)
        s.n += inc
        self.queue[engine].append((fn, flat(after), s, inc, bare))
        return Done(s, s.n)

    def pe(self, fn, after=()):
        return self.do("tensor", fn, after)

    def act(self, fn, after=()):
        return self.do("scalar", fn, after)

    def dve(self, fn, after=()):
        return self.do("vector", fn, after)

    def pool(self, fn, after=()):
        return self.do("gpsimd", fn, after, bare=True)

    def dma(self, sem, fn, after=()):
        return self.do("sync", fn, after, sem=sem, inc=16, bare=True)

    def keep(self, name, *done):
        self.kept[name] = list(done)

    def last(self, name):
        if name in self.kept:
            return self.kept[name]
        return [Later(name)] if self.loop else []

    def resolve(self, after):
        for a in after:
            if isinstance(a, Later):
                for d in self.kept[a.name]:
                    yield Done(d.sem, d.count, d.lag + 1)
            else:
                yield a

    def emit(self, engine, e, i):
        seen = {}
        for fn, after, s, inc, bare in self.queue[engine]:
            need = {}
            for d in self.resolve(after):
                at = d.count - d.lag * d.sem.n
                if at > seen.get(d.sem, -10**9):
                    seen[d.sem] = need[d.sem] = at
            for d_sem, at in need.items():
                if self.loop:
                    e.wait_ge(d_sem.handle, i * d_sem.n + (d_sem.n + at))
                    if bare:
                        e.sem_inc(self.held.handle, 1)
                else:
                    e.wait_ge(d_sem.handle, at)
            fn(e, i).then_inc(s.handle, inc)

    def finals(self, e):
        for s in self.sems.values():
            e.wait_ge(s.handle, s.n)


def build(nc, x, cv1_w, cv1_bn, cv2_w, cv2_bn, m_cv1_w, m_cv1_bn, m_qkv_w, m_rw, m_rh, m_cv2_w,
          m_cv2_bn, conv, S_logits, T_logits, out):
    B, C, H, W = x.shape
    HW = H * W
    NB, CH = m_cv1_w.shape[0], m_cv1_w.shape[1]
    G = S_logits.shape[1]
    HD = m_rw.shape[3]
    CT, HT, YT = C // P, CH // P, (2 + NB) * CH // P
    HALF = HW // 2
    ROWS = H // 2
    HP, WP = H + 2, W + 2
    TAPS = 9
    JT = HW // P
    VW = 2 * HD + 2
    HEADS = CH // HD
    QC = 2 * P
    GROUP = C // 32
    assert HEADS == 4 and HD == 64 and HW == 1024

    ctx = ExitStack()
    with ctx:
        def sb(name, shape, dt):
            return ctx.enter_context(nc.sbuf_tensor(name, shape, dt))

        w_cv1 = sb("w_cv1", [P, 2, CT, C], F16)
        w_cv2 = sb("w_cv2", [P, 2, YT, C], F16)
        w_l1 = sb("w_l1", [P, 2, CT, C], F16)
        w_qkv = sb("w_qkv", [P, NB, 2, HT, 3 * CH], F16)
        w_m2 = sb("w_m2", [P, NB, 2, HT, CH], F16)
        w_c3 = sb("w_c3", [P, 2, HT, TAPS, CH], F16)
        w_c3_dram = nc.dram_tensor("w_c3_dram", (NB, P, 2 * HT * TAPS * CH), F16, kind="Internal").ap()
        xn = sb("xn", [P, CT, HW], F32)
        xn_parts = xn[:, :, :].rearrange("p t n -> p (t n)").bitcast(F16).rearrange(
            "p (t s n) -> p t s n", t=CT, s=2)
        y_plain = sb("y_plain", [P, HT, 2, HW], F16)
        y_pad = sb("y_pad", [P, YT - HT, 2, HP * WP], F16)
        z = sb("z", [P, HT, 2, HW], F16)
        qk = sb("qk", [P, 2 * HEADS * HW // 2], F32)
        qk16 = qk[:, :].bitcast(F16).rearrange("p (s h n) -> p s h n", s=2, h=HEADS)
        q_stack, k_stack = qk16[:, 0], qk16[:, 1]
        q2_stack = sb("q2_stack", [P, HEADS, HW], F16)
        k2_stack = sb("k2_stack", [P, HEADS, HW], F16)
        x1 = qk[:, :].rearrange("p (t n) -> p t n", t=CT)
        v_ext = sb("v_ext", [P, JT, HEADS, VW], F16)
        probs = sb("probs", [P, PROBS, 2, JT, QC], F16)
        x1_parts = probs[:, :, :, :, :].rearrange("p a b c d -> p (a b c d)")[:, 0:2 * CT * HW].rearrange(
            "p (t s n) -> p t s n", t=CT, s=2)
        wide = sb("wide", [P, WIDES, HW], F32)
        o_nat = sb("o_nat", [P, 2, JT, P], F32)
        x_again = o_nat[:, 0, :, :].rearrange("p a b -> p (a b)").rearrange("p (a n) -> p a n", a=2)
        o_raw = sb("o_raw", [P, 2, 2, 2 * HD + 1], F32)
        ident16 = sb("ident16", [P, P], F16)
        ident = sb("ident", [P, P], F32)
        group_mean = sb("group_mean", [P, P], F32)
        par = {n: sb(f"par_{n}", [P, t, 2], F32) for n, t in
               (("cv1_t", CT), ("cv1_y", CT), ("cv2_t", CT), ("cv2_y", CT), ("m1_t", NB * HT), ("m1_y", NB * HT),
                ("m2_t", NB * HT), ("m2_y", NB * HT))}
        qkv_unit = sb("qkv_unit", [P, NB, 6], F32)
        l1_unit = sb("l1_unit", [P, CT], F32)
        w_r = sb("w_r", [P, NB, HT, P], F16)
        pick = sb("pick", [P, HW], F16)
        row_max = sb("row_max", [P, 2, JT, 2], F32)
        shift = sb("shift", [P, 2, 2, JT], F32)
        shift16 = sb("shift16", [P, 2, JT], F16)
        recip = sb("recip", [P, 2, 2], F32)
        stats = sb("stats", [P, 2, CT, 2, 6], F32)
        mv = sb("mv", [P, 2, CT, 2], F32)
        gn = sb("gn", [P, 2, 8, CT], F32)
        minus_half = sb("minus_half", [P, 16], F32)
        exp_top = sb("exp_top", [P, 1], F32)

        ps_u = ctx.enter_context(nc.psum_tensor("ps_u", [P, 4, HALF], F32))
        ps_a = ctx.enter_context(nc.psum_tensor("ps_a", [P, 2, HALF], F32))
        ps_o = ctx.enter_context(nc.psum_tensor("ps_o", [P, 2, HALF], F32))

        def pad_view(t, part, r0, c0, rows):
            m = y_pad[:, t, part, :].rearrange("p (r c) -> p r c", c=WP)
            return m[:, r0:r0 + rows, c0:c0 + W]

        def y_half(t, part, n):
            if t < HT:
                return y_plain[:, t, part, n * HALF:(n + 1) * HALF].rearrange("p (r c) -> p r c", c=W)
            return pad_view(t - HT, part, 1 + n * ROWS, 1, ROWS)

        def img(ap):
            return ap.rearrange("p (r c) -> p r c", c=W)

        HH = slice(0, HALF), slice(HALF, HW)

        def group_norm_stats(s, slot, tag, source_ready, bank="O0 free", constants=()):
            g = gn[:, slot]
            aggr = [s.do("vector", lambda e, i, t=t: e.bn_aggr(mv[:, slot, t, :], stats[:, slot, t, :, :].rearrange("p a b -> p (a b)")),
                         after=[source_ready[t], s.last(tag + " factors used")], bare=True) for t in range(CT)]
            yield
            mean = s.pe(lambda e, i: e.matmul(ps_o[:, 0, 0:CT], group_mean[:, :], mv[:, slot, :, 0], start=True, stop=True),
                        after=[aggr, constants, s.last(bank)])
            c1 = s.dve(lambda e, i: e.tensor_copy(g[:, 0, :], ps_o[:, 0, 0:CT]), after=[mean])
            c2 = s.dve(lambda e, i: e.tensor_tensor(g[:, 1, :], mv[:, slot, :, 0], g[:, 0, :], ALU.subtract), after=[c1])
            c3 = s.dve(lambda e, i: e.tensor_tensor(g[:, 2, :], g[:, 1, :], g[:, 1, :], ALU.mult), after=[c2])
            c4 = s.dve(lambda e, i: e.tensor_tensor(g[:, 3, :], g[:, 2, :], mv[:, slot, :, 1], ALU.add), after=[c3])
            s.keep(bank, c1)
            yield
            var = s.pe(lambda e, i: e.matmul(ps_o[:, 0, 0:CT], group_mean[:, :], g[:, 3, :], start=True, stop=True),
                       after=[c4, s.last(bank)])
            c5 = s.dve(lambda e, i: e.tensor_scalar(g[:, 4, :], ps_o[:, 0, 0:CT], GN_EPS, None, ALU.add), after=[var])
            s.keep(bank, c5)
            rstd = s.pool(lambda e, i: e.tensor_tensor(g[:, 5, :], g[:, 4, :], minus_half[:, 0:CT], ALU.pow), after=[c5, constants])
            c6 = s.dve(lambda e, i: e.tensor_scalar(g[:, 6, :], g[:, 5, :], ACTIVATION_SCALE, None, ALU.mult), after=[rstd])
            c7 = s.dve(lambda e, i: e.scalar_tensor_tensor(g[:, 7, :], g[:, 6, :], -1.0, g[:, 0, :], ALU.mult, ALU.mult), after=[c6])
            return c7

        wide_turn = [0]

        fixed_wide = [WIDES - 1]

        def next_wide():
            wide_turn[0] += 1
            return fixed_wide[0] if fixed_wide else wide_turn[0] % WIDES

        def normalise(s, slot, t, src, dst, ready, factors):
            w = next_wide()
            g = gn[:, slot]
            f = s.dve(lambda e, i: e.tensor_scalar(wide[:, w, :], src, g[:, 6, t:t + 1], g[:, 7, t:t + 1], ALU.mult, ALU.add),
                      after=[ready, factors, s.last(f"wide{w} free")])
            hi = s.act(lambda e, i: e.activation(dst[:, 0, :], wide[:, w, :], ACT.Copy), after=[f])
            lo = s.dve(lambda e, i: e.tensor_tensor(dst[:, 1, :], wide[:, w, :], dst[:, 0, :], ALU.subtract), after=[hi])
            s.keep(f"wide{w} free", lo)
            return lo

        def load_x(s, batch_of):
            loaded = []
            for t in range(CT):
                def fn(e, i, t=t):
                    src = x[batch_of(i), t * P:(t + 1) * P, :, :].rearrange("b p h w -> p (b h w)")
                    return e.dma_start(xn[:, t, :], src)
                loaded.append(s.dma(f"x{t}", fn, after=[s.last("xn read")]))
            return loaded

        def gn1_stats(s, loaded):
            ready = []
            for t in range(CT):
                for n in range(2):
                    r = s.dve(lambda e, i, t=t, n=n: e.bn_stats(stats[:, 0, t, n, :], xn[:, t, HH[n]]), after=[loaded[t]])
                ready.append(r)
            return ready

        def gn1_apply(s, factors):
            parts = [normalise(s, 0, t, xn[:, t, :], xn_parts[:, t], [], factors) for t in range(CT)]
            s.keep("gn1 factors used", parts[-1])
            s.keep("gn1 parts", *parts)

        turn = [0]

        def unit_group(matmuls, after, width=HALF):
            bank = turn[0] % 4
            turn[0] += 1

            def fn(e, i):
                for k, (lhsT, rhs) in enumerate(matmuls):
                    ins = e.matmul(ps_u[:, bank, :], lhsT, rhs, start=(k == 0), stop=(k == len(matmuls) - 1))
                return ins
            return bank, s.pe(fn, after=[after, s.last(f"U{bank} free")])

        def three(w_of, x_of):
            return [(w_of(0), x_of(0)), (w_of(0), x_of(1)), (w_of(1), x_of(0))]

        def silu(bank, mm, name, t, after=()):
            slot = next_wide()
            th, yh = wide[:, slot, 0:HALF], wide[:, slot, HALF:HW]
            pt, py = par[name + "_t"], par[name + "_y"]
            a = s.act(lambda e, i: e.activation(th, ps_u[:, bank, :], ACT.Tanh, scale=pt[:, t, 0:1], bias=pt[:, t, 1:2]),
                      after=[mm, s.last(f"wide{slot} free")])
            b = s.act(lambda e, i: e.activation(yh, ps_u[:, bank, :], ACT.Identity, scale=py[:, t, 0:1], bias=py[:, t, 1:2]),
                      after=[mm])
            s.keep(f"U{bank} free", b)
            u = s.dve(lambda e, i: e.scalar_tensor_tensor(yh, th, 1.0, yh, ALU.add, ALU.mult), after=[a, b])
            return yh, u, slot

        def split_to(u, ready, hi, lo, slot, after=()):
            a = s.pool(lambda e, i: e.tensor_scalar(hi, u, 1.0, 0.0, ALU.mult, ALU.add), after=[ready, after])
            b = s.dve(lambda e, i: e.tensor_tensor(lo, u, hi, ALU.subtract), after=[a])
            s.keep(f"wide{slot} free", b)
            return b

        def add_to(u, other, ready):
            return s.dve(lambda e, i: e.tensor_tensor(img(u), img(u), other, ALU.add), after=[ready])

        def cv1_steps(parts):
            for m in [2, 3, 0, 1]:
                for n in range(2):
                    mms = []
                    for k in range(CT):
                        mms += three(lambda j: w_cv1[:, j, k, m * P:(m + 1) * P], lambda j: xn_parts[:, k, j, HH[n]])
                    bank, mm = unit_group(mms, parts)
                    u, ready, slot = silu(bank, mm, "cv1", m)
                    s.keep(f"y{m}{n}", split_to(img(u), ready, y_half(m, 0, n), y_half(m, 1, n), slot, after=[s.last("y free")]))
                    s.keep("xn read", mm)
                    yield

        s = Section(nc, ctx, "setup", loop=False)
        SLOT = CH * TAPS
        stage = [qk[:, 0:SLOT],
                 probs[:, :, :, :, :].rearrange("p a b c d -> p (a b c d)")[:, 0:2 * SLOT].bitcast(F32),
                 wide[:, :, :].rearrange("p a b -> p (a b)")[:, 0:SLOT]]
        pads = y_pad[:, :, :, :].rearrange("p a b c -> p (a b c)")
        split = [pads[:, 2 * SLOT * j:2 * SLOT * (j + 1)] for j in range(3)]
        spare = q2_stack[:, :, :].rearrange("p h n -> p (h n)").bitcast(F32)
        spare_used = [0]

        def tmp(*shape):
            size = 1
            for n in shape:
                size *= n
            ap = spare[:, spare_used[0]:spare_used[0] + size]
            spare_used[0] += size
            names = "abcd"[:len(shape)]
            return ap.rearrange(f"p ({' '.join(names)}) -> p {' '.join(names)}", **dict(zip(names[1:], shape[1:]))) if len(shape) > 1 else ap

        def side_by_side(threads, width):
            waiting, running = list(threads), []
            while waiting or running:
                while waiting and len(running) < width:
                    running.append(waiting.pop(0))
                for t in list(running):
                    try:
                        next(t)
                    except StopIteration:
                        running.remove(t)
                yield

        ones = tmp(P)
        m1 = s.pool(lambda e, i: e.memset(ident[:, :], 0.0))
        m2 = s.pool(lambda e, i: e.memset(group_mean[:, :], 1.0 / GROUP))
        m3 = s.pool(lambda e, i: e.memset(minus_half[:, :], -0.5))
        m4 = s.pool(lambda e, i: e.memset(ones, 1.0))
        s.pool(lambda e, i: e.memset(exp_top[:, :], EXP_TOP))
        id32 = s.pool(lambda e, i: e.affine_select(out=ident[:, :], in_=ident[:, :], compare_op=ALU.not_equal, fill=1.0,
                                                   base=0, pattern=[[-1, P]], channel_multiplier=1), after=[m1])
        gm3 = group_mean[:, :].rearrange("p (g q) -> p g q", q=GROUP)
        g1 = s.pool(lambda e, i: e.affine_select(out=gm3, in_=gm3, compare_op=ALU.is_ge, fill=0.0, base=0,
                                                 pattern=[[-GROUP, P // GROUP], [0, GROUP]], channel_multiplier=1), after=[m2])
        g2 = s.pool(lambda e, i: e.affine_select(out=gm3, in_=gm3, compare_op=ALU.is_ge, fill=0.0, base=GROUP - 1,
                                                 pattern=[[GROUP, P // GROUP], [0, GROUP]], channel_multiplier=-1), after=[g1])
        id16 = s.dve(lambda e, i: e.tensor_copy(ident16[:, :], ident[:, :]), after=[id32])
        pk = s.pool(lambda e, i: e.memset(pick[:, :], 0.0))
        pk3 = img(pick[:, :])
        for quarter in range(4):
            pat = [[0, H], [-1, W]] if quarter % 2 == 0 else [[-1, H], [0, W]]
            pk = s.pool(lambda e, i, quarter=quarter, pat=pat: e.affine_select(
                out=pk3, in_=pk3, compare_op=ALU.not_equal, fill=R_UNIT, base=-32 * quarter, pattern=pat,
                channel_multiplier=1), after=[pk])

        bn_raw, got_bn = {}, {}

        def bn_load(name, ap, tiles):
            t = tmp(4, tiles)
            bn_raw[name] = t
            got_bn[name] = s.dma("bn", lambda e, i: e.dma_start(t, ap.rearrange("f (t p) -> p f t", p=P),
                                                                allow_slow_non_contiguous=True))
        bn_load("cv1", cv1_bn, CT)
        bn_load("cv2", cv2_bn, CT)
        for b in range(NB):
            bn_load(f"m1_{b}", m_cv1_bn[b], HT)
            bn_load(f"m2_{b}", m_cv2_bn[b], HT)
        st = tmp(2, CT, G)
        got_st = [s.dma("st", lambda e, i, j=j, src=src: e.dma_start(st[:, j, :, :], src.rearrange("(t p) g -> p t g", p=P)))
                  for j, src in enumerate((S_logits, T_logits))]
        loaded = load_x(s, lambda i: slice(0, 1))
        rwh = tmp(NB, HT, W + H)
        got_r = []
        for b in range(NB):
            for lo_, hi_, src in ((0, W, m_rw), (W, W + H, m_rh)):
                got_r.append(s.dma("r", lambda e, i, b=b, lo_=lo_, hi_=hi_, src=src: e.dma_start(
                    rwh[:, b, :, lo_:hi_], src[b].rearrange("a (t g) d h w -> (g d) (a t) (h w)", g=2))))

        bank_turn = [0]
        row_small = tmp(4, 5)
        slots = [0, 1, 2]
        w_done = []

        def row_factors(slot, w_f32, unit_out, ready, also=None):
            r = row_small[:, slot]
            a = s.dve(lambda e, i: e.tensor_reduce(r[:, 0:1], w_f32, AX.X, ALU.max, apply_absolute_value=True),
                      after=[ready, s.last(f"row_small{slot}")])
            if also is None:
                b = s.dve(lambda e, i: e.tensor_scalar(r[:, 1:2], r[:, 0:1], 2.0 ** -100, None, ALU.max), after=[a])
            else:
                b = s.dve(lambda e, i: e.scalar_tensor_tensor(r[:, 1:2], r[:, 0:1], 2.0 ** -100, also, ALU.max, ALU.max), after=[a])
            c = s.dve(lambda e, i: e.tensor_scalar(unit_out.bitcast(I32), r[:, 1:2].bitcast(I32), 0x7F800000, None,
                                                   ALU.bitwise_and), after=[b])
            d = s.dve(lambda e, i: e.reciprocal(r[:, 2:3], unit_out), after=[c])
            return s.dve(lambda e, i: e.tensor_scalar(r[:, 3:4], r[:, 2:3], WEIGHT_TOP, None, ALU.mult), after=[d])

        def split_scaled(w_f32, w_parts, factor, ready, use_pool=True):
            if use_pool:
                g = s.pool(lambda e, i: e.tensor_scalar(w_f32, w_f32, factor, 0.0, ALU.mult, ALU.add), after=[ready])
            else:
                g = s.act(lambda e, i: e.activation(w_f32, w_f32, ACT.Copy, scale=factor), after=[ready])
            hi = s.act(lambda e, i: e.activation(w_parts[0], w_f32, ACT.Copy), after=[g])
            return s.dve(lambda e, i: e.tensor_tensor(w_parts[1], w_f32, w_parts[0], ALU.subtract), after=[hi])

        def weight_rows(rows, cols, dst_of, unit_out, taps=1, also=None, after=()):
            slot = slots.pop(0)
            n = cols * taps
            wf = stage[slot][:, 0:n]
            wp = [split[slot][:, j * n:(j + 1) * n] for j in range(2)]
            got = s.dma(f"stage{slot}", lambda e, i: e.dma_start(wf, rows), after=[s.last(f"stage{slot} free")])
            yield
            f = row_factors(slot, wf, unit_out, got, also)
            yield
            parts = split_scaled(wf, wp, row_small[:, slot, 3:4], [f, s.last(f"split{slot} free")])
            s.keep(f"stage{slot} free", parts)
            s.keep(f"row_small{slot}", parts)
            yield
            kt = cols // P
            views = [wp[j].rearrange("p (c t) -> p t c", t=taps) for j in range(2)]
            if taps == 1:
                runs = [([views[j][:, 0, k * P:(k + 1) * P] for k in range(k0, min(k0 + 8, kt))],
                         dst_of(j, slice(k0, min(k0 + 8, kt)))) for j in range(2) for k0 in range(0, kt, 8)]
            else:
                runs = [([views[j][:, q, k * P:(k + 1) * P] for q in range(q0, min(q0 + 5, taps))],
                         dst_of(j, k)[:, q0:min(q0 + 5, taps), :]) for j in range(2) for k in range(kt) for q0 in (0, 5)]
            done = []
            for sources, dst in runs:
                bank = bank_turn[0] % 6
                bank_turn[0] += 1
                pt = (ps_u[:, bank, :] if bank < 4 else ps_a[:, bank - 4, :]).bitcast(F16)

                def fn(e, i, sources=sources, pt=pt):
                    for j, src in enumerate(sources):
                        ins = e.transpose(pt[:, j * P:(j + 1) * P], src, ident16[:, :])
                    return ins
                t = s.pe(fn, after=[parts, id16, s.last(f"bank{bank} free")])
                src = pt[:, 0:len(sources) * P].rearrange("p (a b) -> p a b", b=P)
                if bank % 2:
                    d = s.act(lambda e, i, dst=dst, src=src: e.activation(dst, src, ACT.Copy), after=[t, after])
                else:
                    d = s.dve(lambda e, i, dst=dst, src=src: e.tensor_copy(dst, src), after=[t, after])
                s.keep(f"bank{bank} free", d)
                done.append(d)
                yield
            s.keep(f"split{slot} free", *done)
            slots.append(slot)
            w_done.extend(done)
            return done

        unit = {n: tmp(t) for n, t in (("cv1", CT), ("cv2", CT), ("m1", NB * HT), ("m2", NB * HT))}

        r_max = tmp(NB, HT)
        a = s.dve(lambda e, i: e.tensor_reduce(r_max, rwh, AX.X, ALU.max, apply_absolute_value=True), after=[got_r])
        r_ok = s.dve(lambda e, i: e.tensor_scalar(r_max, r_max, 1.0 / R_UNIT, None, ALU.mult), after=[a])

        def r_operand(b, t, ready):
            f = s.dve(lambda e, i: e.reciprocal(r_scale[:, b, t:t + 1], qkv_unit[:, b, 2 + t:3 + t]), after=[ready])
            g = s.dve(lambda e, i: e.tensor_scalar(rwh[:, b, t, :], rwh[:, b, t, :], r_scale[:, b, t:t + 1], WS / R_UNIT,
                                                   ALU.mult, ALU.mult), after=[f])
            hi = s.dve(lambda e, i: e.tensor_copy(r_parts[:, 0, :], rwh[:, b, t, :]), after=[g, s.last("r_parts free")])
            lo = s.dve(lambda e, i: e.tensor_tensor(r_parts[:, 1, :], rwh[:, b, t, :], r_parts[:, 0, :], ALU.subtract), after=[hi])
            pt = ps_o[:, 1, :].bitcast(F16)[:, 0:P]
            mm = s.pe(lambda e, i: e.transpose(pt, r_parts[:, :, :].rearrange("p a b -> p (a b)"), ident16[:, :]),
                      after=[lo, id16, s.last("perm1 free")])
            d = s.dve(lambda e, i: e.tensor_copy(w_r[:, b, t, :], pt), after=[mm])
            s.keep("perm1 free", d)
            s.keep("r_parts free", d)
        r_scale = tmp(NB, HT)
        r_parts = tmp(P // 2).bitcast(F16).rearrange("p (a b) -> p a b", a=2)

        def c3_rows(b, m, state):
            rows = m_cv1_w[b, m * P:(m + 1) * P].rearrange("o c h w -> o (c h w)")
            done = yield from weight_rows(rows, CH, lambda j, k: w_c3[:, j, k, :, m * P:(m + 1) * P],
                                          unit["m1"][:, b * HT + m:b * HT + m + 1], TAPS, after=state["sent"])
            state["done"] += done
            state["left"] -= 1
            if state["left"] == 0:
                state["next"]["sent"] = [s.dma("c3_out", lambda e, i: e.dma_start(
                    w_c3_dram[b], w_c3[:, :, :, :, :].rearrange("p a b c d -> p (a b c d)")), after=[state["done"]])]

        def qkv_rows(b, m):
            rows = m_qkv_w[b, m * P:(m + 1) * P].rearrange("o c h w -> o (c h w)")
            also = r_max[:, b, m - HT:m - HT + 1] if HT <= m < 2 * HT else None
            done = yield from weight_rows(rows, CH, lambda j, k: w_qkv[:, b, j, k, m * P:(m + 1) * P],
                                          qkv_unit[:, b, m:m + 1], also=also)
            if HT <= m < 2 * HT:
                r_operand(b, m - HT, done)

        def plain_rows(w, m, dst, kt, name, t):
            yield from weight_rows(w.rearrange("o c h w -> o (c h w)"), kt * P, lambda j, k: dst[:, j, k, m * P:(m + 1) * P],
                                   unit[name][:, t:t + 1])

        def layer_1():
            st2 = tmp(2, CT, G)
            sm = tmp(6, 2, CT)
            iota_g, key_base, rank, v_unit = tmp(G), tmp(CT), tmp(CT), tmp(CT)
            wl = k2_stack[:, :, :].rearrange("p a b -> p (a b)").bitcast(F32).rearrange("p (t c) -> p t c", t=CT)
            one_hot = z[:, :, :, :].rearrange("p a b c -> p (a b c)").bitcast(F32).rearrange("p (t k) -> p t k", t=CT)
            vx = v_ext[:, :, :, :].rearrange("p a b c -> p (a b c)")
            one_hot16 = vx[:, 0:CT * C].rearrange("p (t k) -> p t k", t=CT)
            iota_k, k_row = x_again[:, 0, :], x_again[:, 1, :]
            yp = y_plain[:, :, :, :].rearrange("p a b c -> p (a b c)")
            s_row, g_row = tmp(C), tmp(C)
            cmp_ = yp[:, 0:2 * C].bitcast(F32)
            wf = yp[:, 2 * C:4 * C].bitcast(F32)
            got_w = [s.dma(f"conv{t}", lambda e, i, t=t: e.dma_start(wl[:, t, :], conv[t * P:(t + 1) * P].rearrange("o c h w -> o (c h w)")))
                     for t in range(CT)]
            i1 = s.pool(lambda e, i: e.iota(iota_g, pattern=[[1, G]], base=-G, channel_multiplier=0,
                                            allow_small_or_imprecise_dtypes=True))
            i2 = s.pool(lambda e, i: e.iota(key_base, pattern=[[P, CT]], base=0, channel_multiplier=1,
                                            allow_small_or_imprecise_dtypes=True))
            i3 = s.pool(lambda e, i: e.iota(iota_k, pattern=[[1, C]], base=0, channel_multiplier=0,
                                            allow_small_or_imprecise_dtypes=True))
            yield

            def bc(ap, n):
                return ap.unsqueeze(3).to_broadcast([P, 2, CT, n])
            a = s.dve(lambda e, i: e.tensor_reduce(sm[:, 0], st[:, :, :, :], AX.X, ALU.max), after=[got_st])
            a = s.dve(lambda e, i: e.tensor_tensor(st[:, :, :, :], st[:, :, :, :], bc(sm[:, 0], G), ALU.subtract), after=[a])
            a = s.act(lambda e, i: e.activation(st2[:, :, :, :], st[:, :, :, :], ACT.Exp), after=[a])
            yield
            a = s.dve(lambda e, i: e.tensor_reduce(sm[:, 1], st2[:, :, :, :], AX.X, ALU.add), after=[a])
            a = s.dve(lambda e, i: e.reciprocal(sm[:, 2], sm[:, 1]), after=[a])
            a = s.dve(lambda e, i: e.tensor_tensor(st2[:, :, :, :], st2[:, :, :, :], bc(sm[:, 2], G), ALU.mult), after=[a])
            gain = s.dve(lambda e, i: e.tensor_reduce(sm[:, 3], st2[:, :, :, :], AX.X, ALU.max), after=[a])
            yield
            a = s.dve(lambda e, i: e.tensor_tensor(st[:, :, :, :], st2[:, :, :, :], bc(sm[:, 3], G), ALU.is_ge), after=[gain])
            a = s.dve(lambda e, i: e.tensor_tensor(st[:, :, :, :], st[:, :, :, :],
                                                   iota_g.unsqueeze(1).unsqueeze(1).to_broadcast([P, 2, CT, G]), ALU.mult), after=[a, i1])
            arg = s.dve(lambda e, i: e.tensor_reduce(sm[:, 4], st[:, :, :, :], AX.X, ALU.min), after=[a])
            key = s.dve(lambda e, i: e.scalar_tensor_tensor(sm[:, 5, 1, :], sm[:, 4, 1, :], float(C), key_base,
                                                            ALU.mult, ALU.add), after=[arg, i2])
            yield
            diag = o_nat[:, 1, 0:CT, :]

            def rows_of(col, ready, dst):
                made = []
                for t in range(CT):
                    made.append(s.dve(lambda e, i, t=t: e.tensor_scalar(diag[:, t, :], ident[:, :], col[:, t:t + 1], None, ALU.mult),
                                      after=[ready, id32, s.last("diag free")]))

                def fn(e, i):
                    for t in range(CT):
                        ins = e.matmul(ps_o[:, 0, t * P:(t + 1) * P], ones, diag[:, t, :], start=True, stop=True)
                    return ins
                mm = s.pe(fn, after=[made, m4, s.last("perm0 free")])
                cp = s.dve(lambda e, i: e.tensor_copy(dst, ps_o[:, 0, :]), after=[mm])
                s.keep("diag free", mm)
                s.keep("perm0 free", cp)
                return cp
            rk = rows_of(sm[:, 5, 1, :], key, k_row)
            yield
            rs = rows_of(sm[:, 4, 0, :], arg, s_row)
            yield
            rg = rows_of(sm[:, 3, 0, :], gain, g_row)
            yield
            hot, free = [], []
            for t in range(CT):
                a = s.dve(lambda e, i, t=t: e.tensor_scalar(cmp_, k_row, sm[:, 5, 1, t:t + 1], None, ALU.is_lt), after=[rk, free])
                a = s.dve(lambda e, i, t=t: e.tensor_reduce(rank[:, t:t + 1], cmp_, AX.X, ALU.add), after=[a])
                free = [a]
                a = s.dve(lambda e, i, t=t: e.tensor_scalar(one_hot[:, t, :], iota_k, rank[:, t:t + 1], None, ALU.is_equal), after=[a, i3])
                hot.append(s.act(lambda e, i, t=t: e.activation(one_hot16[:, t, :], one_hot[:, t, :], ACT.Copy), after=[a]))
                yield
            masked = []
            for t in range(CT):
                a = s.dve(lambda e, i, t=t: e.tensor_scalar(cmp_, s_row, sm[:, 4, 1, t:t + 1], sm[:, 3, 1, t:t + 1], ALU.is_equal, ALU.mult),
                          after=[rs, free])
                a = s.dve(lambda e, i, t=t: e.tensor_tensor(cmp_, cmp_, g_row, ALU.mult), after=[a, rg])
                a = s.dve(lambda e, i, t=t: e.tensor_tensor(wl[:, t, :], wl[:, t, :], cmp_, ALU.mult), after=[a, got_w[t]])
                masked.append(a)
                free = [a]
                yield
            vp = probs[:, :, :, :, :].rearrange("p a b c d -> p (a b c d)")[:, 2 * SLOT:2 * SLOT + 2 * CT * C].rearrange(
                "p (t s c) -> p t s c", t=CT, s=2)
            v_done = []
            for m in range(CT):
                def fn(e, i, m=m):
                    for t in range(CT):
                        ins = e.matmul(ps_o[:, 0, :], one_hot[:, t, m * P:(m + 1) * P], wl[:, t, :], start=(t == 0), stop=(t == CT - 1))
                    return ins
                mm = s.pe(fn, after=[masked, hot, s.last("perm0 free")])
                cp = s.dve(lambda e, i: e.tensor_copy(wf, ps_o[:, 0, :]), after=[mm, s.last("wf free")])
                s.keep("perm0 free", cp)
                f = row_factors(3, wf, v_unit[:, m:m + 1], cp)
                yield
                d = split_scaled(wf, [vp[:, m, 0, :], vp[:, m, 1, :]], row_small[:, 3, 3:4], [f], use_pool=False)
                s.keep("row_small3", d)
                s.keep("wf free", d)
                v_done.append(d)
                yield
            for c in range(CT):
                for j in range(2):
                    def fn(e, i, c=c, j=j):
                        for t in range(CT):
                            ins = e.matmul(ps_o[:, j, :], vp[:, t, j, c * P:(c + 1) * P], one_hot16[:, t, :], start=(t == 0), stop=(t == CT - 1))
                        return ins
                    mm = s.pe(fn, after=[v_done, hot, s.last(f"perm{j} free")])
                    cp = s.act(lambda e, i, c=c, j=j: e.activation(w_l1[:, j, c, :], ps_o[:, j, :], ACT.Copy), after=[mm])
                    s.keep(f"perm{j} free", cp)
                    yield

            def fn(e, i):
                for n in range(CT):
                    for t in range(CT):
                        ins = e.matmul(ps_o[:, 0, n:n + 1], one_hot[:, t, n * P:(n + 1) * P], v_unit[:, t:t + 1], start=(t == 0), stop=(t == CT - 1))
                return ins
            mm = s.pe(fn, after=[v_done, s.last("perm0 free")])
            l1f = s.dve(lambda e, i: e.tensor_scalar(l1_unit[:, :], ps_o[:, 0, 0:CT], 1.0 / WS, None, ALU.mult), after=[mm])
            s.keep("perm0 free", l1f)
            s.keep("layer 1", l1f, mm)
            yield

        def first_norm():
            ready = gn1_stats(s, loaded)
            yield
            factors = yield from group_norm_stats(s, 0, "gn1", ready, "perm0 free", [g2, m3])
            yield
            gn1_apply(s, factors)


        c3_states = [{"sent": [], "done": [], "left": HT} for _ in range(NB + 1)]
        for b in range(NB):
            c3_states[b]["next"] = c3_states[b + 1]
        weights = [plain_rows(cv1_w[m * P:(m + 1) * P], m, w_cv1, CT, "cv1", m) for m in range(CT)]
        for b in range(NB):
            weights += [c3_rows(b, m, c3_states[b]) for m in range(HT)]
            weights += [qkv_rows(b, m) for m in range(6)]
            weights += [plain_rows(m_cv2_w[b, m * P:(m + 1) * P], m, w_m2[:, b], HT, "m2", b * HT + m) for m in range(HT)]
        weights += [plain_rows(cv2_w[m * P:(m + 1) * P], m, w_cv2, YT, "cv2", m) for m in range(CT)]
        for _ in side_by_side([layer_1(), first_norm(), side_by_side(weights, len(slots))], 3):
            pass

        s.dve(lambda e, i: e.tensor_scalar(qkv_unit[:, :, 0:4], qkv_unit[:, :, 0:4], 1.0 / WEIGHT_TOP, None, ALU.mult), after=[w_done])
        s.dve(lambda e, i: e.tensor_scalar(qkv_unit[:, :, 4:6], qkv_unit[:, :, 4:6],
                                           ACTIVATION_SCALE / (WS * V_SHIFT), None, ALU.mult), after=[w_done])

        def bn_factors(name, raw, units, t0, tiles, out_scale):
            t = tmp(4, tiles)
            pt, py = par[name + "_t"][:, t0:t0 + tiles, :], par[name + "_y"][:, t0:t0 + tiles, :]
            a = s.dve(lambda e, i: e.tensor_scalar(t[:, 0, :], raw[:, 3, :], BN_EPS, None, ALU.add), after=[list(got_bn.values())])
            b = s.pool(lambda e, i: e.tensor_tensor(t[:, 1, :], t[:, 0, :], minus_half[:, 0:tiles], ALU.pow), after=[a, m3])
            yield
            c = s.dve(lambda e, i: e.tensor_tensor(t[:, 2, :], t[:, 1, :], raw[:, 0, :], ALU.mult), after=[b])
            d = s.dve(lambda e, i: e.tensor_tensor(t[:, 3, :], t[:, 2, :], raw[:, 2, :], ALU.mult), after=[c])
            f = s.dve(lambda e, i: e.tensor_tensor(t[:, 0, :], raw[:, 1, :], t[:, 3, :], ALU.subtract), after=[d])
            g = s.dve(lambda e, i: e.tensor_tensor(t[:, 1, :], t[:, 2, :], units, ALU.mult), after=[d, w_done])
            yield
            s.dve(lambda e, i: e.tensor_scalar(pt[:, :, 0], t[:, 1, :], 0.5 / WS, None, ALU.mult), after=[g])
            s.dve(lambda e, i: e.tensor_scalar(pt[:, :, 1], t[:, 0, :], 0.5, None, ALU.mult), after=[f])
            s.dve(lambda e, i: e.tensor_scalar(py[:, :, 0], t[:, 1, :], 0.5 * out_scale / WS, None, ALU.mult), after=[g])
            h = s.dve(lambda e, i: e.tensor_scalar(py[:, :, 1], t[:, 0, :], 0.5 * out_scale, None, ALU.mult), after=[f])
            s.keep(f"bn {name} {t0}", h)
            yield

        for _ in side_by_side([bn_factors("cv1", bn_raw["cv1"], unit["cv1"], 0, CT, ACTIVATION_SCALE),
                      bn_factors("cv2", bn_raw["cv2"], unit["cv2"], 0, CT, 1.0)] +
                     [bn_factors(n, bn_raw[f"{n}_{b}"], unit[n][:, b * HT:(b + 1) * HT], b * HT, HT, ACTIVATION_SCALE)
                      for b in range(NB) for n in ("m1", "m2")], 6):
            pass

        read = [s.last("layer 1"), w_done, Done(s.sem("tensor"), s.sem("tensor").n), Done(s.sem("vector"), s.sem("vector").n)]
        zeros = s.pool(lambda e, i: e.memset(y_pad[:, :, :, :], 0.0), after=read)
        k2z = s.pool(lambda e, i: e.memset(k2_stack[:, :, :], 0.0))
        for h in range(HEADS):
            row = HD if h % 2 == 0 else 0
            s.dve(lambda e, i, h=h, row=row: e.memset(k2_stack[row:row + 1, h, :], SHIFT_UNIT), after=[k2z])
        s.pool(lambda e, i: e.memset(q2_stack[:, :, :], 0.0))
        s.dve(lambda e, i: e.memset(v_ext[:, :, :, :], 1.0), after=read)
        for w in range(WIDES):
            s.keep(f"wide{w} free", *read)
        for q in range(4):
            s.keep(f"U{q} free", *read)
        fixed_wide.clear()
        s.keep("y free", zeros, *flat([s.last("layer 1")]))
        for _ in cv1_steps(s.kept["gn1 parts"] + s.last("bn cv1 0")):
            pass
        setup = s

        s = Section(nc, ctx, "batch", loop=True)
        s.held = Sem(ctx.enter_context(nc.semaphore("held")))
        loaded = load_x(s, lambda i: bass.ds((i + 1) % B, 1))

        norm_ahead = {}

        def bottleneck(b):
            y0 = HT + b * HT
            c3 = s.dma("c3", lambda e, i, b=b: e.dma_start(w_c3[:, :, :, :, :].rearrange("p a b c d -> p (a b c d)"), w_c3_dram[b]),
                       after=[s.last("w_c3 read")])
            z_ready = {}
            for n in range(2):
                for m in range(HT):
                    mms = []
                    for k in range(HT):
                        for q in range(TAPS):
                            dy, dx = divmod(q, 3)
                            mms += three(lambda j: w_c3[:, j, k, q, m * P:(m + 1) * P],
                                         lambda j: pad_view(y0 - HT + k, j, n * ROWS + dy, dx, ROWS))
                    bank, mm = unit_group(mms, [c3] + [s.last(f"y{y0 + k}{nn}") for k in range(HT) for nn in range(2)])
                    u, ready, slot = silu(bank, mm, "m1", b * HT + m)
                    z_ready[m, n] = split_to(u, ready, z[:, m, 0, HH[n]], z[:, m, 1, HH[n]], slot, after=[s.last("z free")])
                    if b == 0 and (n, m) == (0, 0):
                        norm_ahead["ready"] = gn1_stats(s, loaded)
                    if b == 1 and "steps" in norm_ahead:
                        norm_ahead["factors"] = next(norm_ahead["steps"], None)
                    if b == 1 and (n, m) == (0, 0):
                        norm_ahead["steps"] = group_norm_stats(s, 0, "gn1", norm_ahead["ready"])
                        next(norm_ahead["steps"])
            if b == 1:
                for _ in norm_ahead["steps"]:
                    pass
                gn1_apply(s, [Done(s.sem("vector"), s.sem("vector").n)])
            s.keep("w_c3 read", mm)

            q_ready = {h: [] for h in range(HEADS)}
            k_ready = {h: [] for h in range(HEADS)}
            v_ready = []
            z_all = {n: [z_ready[m, n] for m in range(HT)] for n in range(2)}

            def project(kind, pair, n):
                m = 2 * kind + pair
                mms = []
                for k in range(HT):
                    mms += three(lambda j: w_qkv[:, b, j, k, m * P:(m + 1) * P], lambda j: z[:, k, j, HH[n]])
                if kind == 1:
                    mms.append((w_r[:, b, pair, :], pick[:, HH[n]]))
                bank, mm = unit_group(mms, z_all[n])
                slot = next_wide()
                f = wide[:, slot, 0:HALF]
                px = ps_u[:, bank, :]
                free = [s.last(f"wide{slot} free")]
                even, odd = 2 * pair, 2 * pair + 1
                full = s.act(lambda e, i: e.activation(f, px, ACT.Identity, scale=qkv_unit[:, b, m:m + 1]), after=[mm, free])
                s.keep(f"U{bank} free", full)
                free_st = [s.last("qk free")]
                last = []
                for h, nat, oth in ((even, slice(0, HD), slice(HD, P)), (odd, slice(HD, P), slice(0, HD))):
                    cols = HH[n]
                    if kind == 0:
                        hi = s.act(lambda e, i, h=h, nat=nat: e.activation(q_stack[nat, h, cols], f[nat], ACT.Copy), after=[full, free_st])
                        lo = s.dve(lambda e, i, h=h, nat=nat, oth=oth: e.tensor_tensor(q_stack[oth, h, cols], f[nat], q_stack[nat, h, cols], ALU.subtract), after=[hi])
                        dup = s.dve(lambda e, i, h=h, nat=nat: e.tensor_copy(q2_stack[nat, h, cols], q_stack[nat, h, cols]), after=[hi])
                        q_ready[h] += [lo, dup]
                        last += [lo]
                    else:
                        hi = s.act(lambda e, i, h=h, nat=nat: e.activation(k_stack[nat, h, cols], f[nat], ACT.Copy), after=[full, free_st])
                        dup = s.act(lambda e, i, h=h, nat=nat, oth=oth: e.activation(k_stack[oth, h, cols], f[nat], ACT.Copy), after=[full])
                        lo = s.dve(lambda e, i, h=h, nat=nat: e.tensor_tensor(k2_stack[nat, h, cols], f[nat], k_stack[nat, h, cols], ALU.subtract), after=[hi])
                        k_ready[h] += [lo, dup]
                        last += [lo, dup]
                s.keep(f"wide{slot} free", *last)

            def project_v(jj):
                bank = turn[0] % 4
                turn[0] += 1

                def fn(e, i):
                    for q in range(2):
                        px = ps_u[:, bank, q * CH:(q + 1) * CH]
                        j = slice((2 * jj + q) * P, (2 * jj + q + 1) * P)
                        mms = []
                        for k in range(HT):
                            mms += [(z[:, k, a, j], w_qkv[:, b, c, k, 2 * CH:3 * CH]) for a, c in ((0, 0), (0, 1), (1, 0))]
                        for t, (lhsT, rhs) in enumerate(mms):
                            ins = e.matmul(px, lhsT, rhs, start=(t == 0), stop=(t == len(mms) - 1))
                    return ins
                mm = s.pe(fn, after=[z_all[jj // 2], s.last(f"U{bank} free")])
                px = ps_u[:, bank, :].rearrange("p (a d) -> p a d", d=HD)
                ve = v_ext[:, 2 * jj:2 * jj + 2, :, :].rearrange("p j h d -> p (j h) d")
                hi = s.act(lambda e, i: e.activation(ve[:, :, 0:HD], px, ACT.Copy, scale=V_SHIFT), after=[mm, s.last("v free")])
                lo = s.dve(lambda e, i: e.scalar_tensor_tensor(ve[:, :, HD + 1:2 * HD + 1], px, V_SHIFT, ve[:, :, 0:HD], ALU.mult, ALU.subtract), after=[hi])
                s.keep(f"U{bank} free", lo)
                v_ready.append(lo)

            a_turn = [0]

            def max_tile(h, it, n):
                bank = a_turn[0] % 2
                a_turn[0] += 1
                mm = s.pe(lambda e, i: e.matmul(ps_a[:, bank, :], q_stack[:, h, it * P:(it + 1) * P], k_stack[:, h, HH[n]], start=True, stop=True),
                          after=[q_ready[h], k_ready[h], s.last(f"A{bank} free")])
                d = s.dve(lambda e, i: e.reduce_max(row_max[:, h % 2, it, n:n + 1], ps_a[:, bank, :], axis=AX.X),
                          after=[mm, s.last(f"row_max{h % 2} free")])
                s.keep(f"A{bank} free", d)
                return d

            def shifts(h, maxima):
                a = s.dve(lambda e, i: e.tensor_reduce(shift[:, h % 2, 0, :], row_max[:, h % 2, :, :], AX.X, ALU.max), after=[maxima])
                s.keep(f"row_max{h % 2} free", a)
                return s.dve(lambda e, i: e.tensor_scalar(shift16[:, h % 2, :], shift[:, h % 2, 0, :], -1.0 / SHIFT_UNIT, None, ALU.mult),
                             after=[a, s.last(f"shift{h % 2} free")])

            def shift_row(h, ready):
                def fn(e, i):
                    for it in range(JT):
                        ins = e.matmul(ps_a[:, it // 4, (it % 4) * P:(it % 4 + 1) * P],
                                       shift16[:, h % 2, it:it + 1].to_broadcast([P, P]), ident16[:, :], start=True, stop=True)
                    return ins
                mm = s.pe(fn, after=[ready, s.last("A0 free"), s.last("A1 free")])
                s.keep(f"shift{h % 2} free", mm)
                row = slice(HD, HD + 1) if h % 2 == 0 else slice(0, 1)
                got = []
                for n in range(2):
                    c = s.act(lambda e, i, n=n: e.activation(q2_stack[row, h, HH[n]], ps_a[row, n, :], ACT.Copy), after=[mm, s.last("qk free")])
                    s.keep(f"A{n} free", c)
                    got.append(c)
                q_ready[h] += got

            for pair in range(2):
                project(0, pair, 0)
                project(1, pair, 0)
            project_v(0)
            project_v(1)
            project(0, 0, 1)
            project(1, 0, 1)
            tiles = [(it, n) for it in range(JT) for n in range(2)]
            maxima = []

            def take_maxima(h, count):
                for _ in range(count):
                    maxima.append(max_tile(h, *tiles.pop(0)))
            for piece in (lambda: project(0, 1, 1), lambda: project(1, 1, 1), lambda: project_v(2), lambda: project_v(3)):
                piece()
                take_maxima(0, 4)
            shift_row(0, shifts(0, maxima))

            STEPS = HEADS * 8
            exp_done, lo_done, chunk_lo = {}, {}, {}
            raw_turn = [0]
            transposed = []

            def logits_step(st_):
                h, c, g = st_ // 8, st_ % 8 // 2, st_ % 2
                q0 = c * QC
                pair_bank = turn[0] // 2 % 2
                turn[0] += 2

                def fn(e, i):
                    for jt in range(4):
                        j = slice((4 * g + jt) * P, (4 * g + jt + 1) * P)
                        o = ps_u[:, 2 * pair_bank + jt // 2, (jt % 2) * QC:(jt % 2 + 1) * QC]
                        e.matmul(o, k_stack[:, h, j], q_stack[:, h, q0:q0 + QC], start=True, stop=False)
                        ins = e.matmul(o, k2_stack[:, h, j], q2_stack[:, h, q0:q0 + QC], start=False, stop=True)
                    return ins
                mm = s.pe(fn, after=[q_ready[h], k_ready[h], s.last(f"U{2 * pair_bank} free"), s.last(f"U{2 * pair_bank + 1} free")])
                slot = (st_ // 2) % PROBS
                w = next_wide()
                ex = s.act(lambda e, i: e.activation(wide[:, w, :], ps_u[:, 2 * pair_bank:2 * pair_bank + 2, :].rearrange("p a b -> p (a b)"),
                                                     ACT.Exp, scale=1.0 / (ACTIVATION_SCALE ** 2 * HD ** 0.5), bias=exp_top[:, 0:1]),
                           after=[mm, s.last(f"wide{w} free")])
                s.keep(f"U{2 * pair_bank} free", ex)
                s.keep(f"U{2 * pair_bank + 1} free", ex)
                free = s.last(f"probs{slot} free")
                dst = [probs[:, slot, part, 4 * g:4 * g + 4, :].rearrange("p j q -> p (j q)") for part in range(2)]
                hi_a = s.act(lambda e, i: e.activation(dst[0][:, HH[0]], wide[:, w, HH[0]], ACT.Copy), after=[ex, free])
                hi_b = s.pool(lambda e, i: e.tensor_scalar(dst[0][:, HH[1]], wide[:, w, HH[1]], 1.0, 0.0, ALU.mult, ALU.add), after=[ex, free])
                lo_b = s.pool(lambda e, i: e.tensor_tensor(dst[1][:, HH[1]], wide[:, w, HH[1]], dst[0][:, HH[1]], ALU.subtract), after=[hi_b])
                exp_done[st_] = (w, dst, hi_a, lo_b)

            def low_step(st_):
                w, dst, hi_a, lo_b = exp_done[st_]
                lo = s.dve(lambda e, i: e.tensor_tensor(dst[1][:, HH[0]], wide[:, w, HH[0]], dst[0][:, HH[0]], ALU.subtract), after=[hi_a])
                s.keep(f"wide{w} free", lo, lo_b)
                lo_done[st_] = [lo, lo_b]

            o_turn = [0]
            av_bank = {}

            def av_half(chunk, half):
                h, slot = chunk // 4, chunk % PROBS
                if half == 0:
                    av_bank[chunk] = o_turn[0] % 2
                    o_turn[0] += 1
                bank = av_bank[chunk]

                def fn(e, i):
                    for jt in range(JT):
                        cols = slice(half * P, (half + 1) * P)
                        o = ps_o[:, bank, half * QC:half * QC + 2 * HD + 1]
                        e.matmul(o, probs[:, slot, 0, jt, cols], v_ext[:, jt, h, 0:2 * HD + 1], start=(jt == 0), stop=False)
                        ins = e.matmul(o[:, 0:HD + 1], probs[:, slot, 1, jt, cols], v_ext[:, jt, h, 0:HD + 1], start=False,
                                       stop=(jt == JT - 1))
                    return ins
                mm = s.pe(fn, after=[lo_done[2 * chunk], lo_done[2 * chunk + 1], v_ready, s.last(f"O{bank} free")])
                if half == 0:
                    return
                s.keep(f"probs{slot} free", mm)
                r = raw_turn[0] % 2
                raw_turn[0] += 1
                src = ps_o[:, bank, :].rearrange("p (a q) -> p a q", a=2)[:, :, 0:2 * HD + 1]
                c = s.act(lambda e, i: e.activation(o_raw[:, r, :, :], src, ACT.Copy), after=[mm, s.last(f"raw{r} free")])
                s.keep(f"O{bank} free", c)
                rc = s.dve(lambda e, i: e.reciprocal(recip[:, r, :], o_raw[:, r, :, HD]), after=[c])
                ad = s.dve(lambda e, i: e.tensor_tensor(o_raw[:, r, :, 0:HD], o_raw[:, r, :, 0:HD], o_raw[:, r, :, HD + 1:2 * HD + 1], ALU.add), after=[c])
                it = chunk % 4 * 2
                par_ = h // 2 % 2
                nr = s.dve(lambda e, i: e.tensor_tensor(o_nat[:, par_, it:it + 2, h % 2 * HD:h % 2 * HD + HD], o_raw[:, r, :, 0:HD],
                                                        recip[:, r, :].unsqueeze(2).to_broadcast([P, 2, HD]), ALU.mult),
                           after=[rc, ad, s.last(f"o_nat{par_} free")])
                s.keep(f"raw{r} free", nr)
                norm_done[chunk] = nr

            norm_done = {}

            def transpose_half(pair, n):
                bank = o_turn[0] % 2
                o_turn[0] += 1

                def fn(e, i):
                    for q in range(4):
                        ins = e.transpose(ps_o[:, bank, q * P:(q + 1) * P], o_nat[:, pair, 4 * n + q, :], ident[:, :])
                    return ins
                need = [norm_done[8 * pair + 4 * hh + 2 * n + cc] for hh in range(2) for cc in range(2)]
                mm = s.pe(fn, after=[need, s.last(f"O{bank} free")])
                if n == 1:
                    s.keep(f"o_nat{pair} free", mm)
                u = qkv_unit[:, b, 4 + pair:5 + pair]
                hi = s.act(lambda e, i: e.activation(z[:, pair, 0, HH[n]], ps_o[:, bank, :], ACT.Copy, scale=u), after=[mm, s.last("z projected")])
                lo = s.dve(lambda e, i: e.scalar_tensor_tensor(z[:, pair, 1, HH[n]], ps_o[:, bank, :], u, z[:, pair, 0, HH[n]], ALU.mult, ALU.subtract), after=[hi])
                s.keep(f"O{bank} free", lo)
                o_ready[pair, n] = lo

            o_ready = {}
            s.keep("z projected", Done(s.sem("tensor"), s.sem("tensor").n))
            if turn[0] % 2:
                turn[0] += 1
            per_step = [3, 3, 3, 3, 2, 2] + [2] * 16
            ahead = {}
            tail = {}

            def second_conv(m, n):
                mms = []
                for k in range(HT):
                    mms += three(lambda j: w_m2[:, b, j, k, m * P:(m + 1) * P], lambda j: z[:, k, j, HH[n]])
                bank, mm = unit_group(mms, [o_ready[0, n], o_ready[1, n]])
                u, ready, slot = silu(bank, mm, "m2", b * HT + m)
                a = add_to(u, y_half(y0 + m, 0, n), ready)
                a = add_to(u, y_half(y0 + m, 1, n), a)
                t = y0 + HT + m
                s.keep(f"y{t}{n}", split_to(img(u), a, y_half(t, 0, n), y_half(t, 1, n), slot, after=[s.last("y free")]))
                s.keep("z free", mm)

            tail[STEPS + 2] = lambda: transpose_half(1, 0)
            tail[STEPS + 4] = lambda: second_conv(0, 0)
            tail[STEPS + 5] = lambda: second_conv(1, 0)
            for st_ in range(STEPS + LAG + 2):
                pos, h = st_ % 8, st_ // 8
                if pos == 7 and h + 1 < HEADS:
                    shift_row(h + 1, shifts(h + 1, ahead[h + 1]))
                count = per_step[st_] if st_ < len(per_step) else 0
                for half_step in range(2):
                    if half_step == 0 and LAG <= st_ < STEPS + LAG:
                        k = st_ - LAG
                        av_half(k // 2, k % 2)
                    if half_step == 1 and st_ < STEPS:
                        logits_step(st_)
                        if st_ >= 1:
                            low_step(st_ - 1)
                    if half_step == 1 and st_ == STEPS:
                        low_step(st_ - 1)
                    for _ in range(count - count // 2 if half_step else count // 2):
                        head = 1 + sum(len(v) for v in ahead.values()) // (2 * JT)
                        done = ahead.setdefault(head, [])
                        done.append(max_tile(head, len(done) // 2, len(done) % 2))
                if st_ in (8 * 2 + LAG + 2, 8 * 2 + LAG + 3):
                    transpose_half(0, st_ - (8 * 2 + LAG + 2))
                if st_ in tail:
                    tail[st_]()
            s.keep("qk free", Done(s.sem("tensor"), s.sem("tensor").n))
            s.keep("v free", Done(s.sem("tensor"), s.sem("tensor").n))
            if b == NB - 1:
                early_cv2.extend(cv2_begin(m, n) for m, n in CV2_ORDER[:2])
            transpose_half(1, 1)
            second_conv(0, 1)
            second_conv(1, 1)

        LAG = 4
        early_cv2 = []
        CV2_ORDER = [(m, n) for m in range(CT) for n in range(2)]

        def cv2_begin(m, n):
            bank = turn[0] % 4
            turn[0] += 1
            mms = []
            for k in range(YT - HT):
                mms += three(lambda j: w_cv2[:, j, k, m * P:(m + 1) * P], lambda j: y_half(k, j, n))

            def fn(e, i):
                for t, (lhsT, rhs) in enumerate(mms):
                    ins = e.matmul(ps_u[:, bank, :], lhsT, rhs, start=(t == 0), stop=False)
                return ins
            s.pe(fn, after=[s.last(f"y{k}{n}") for k in range(YT - HT)] + [s.last(f"U{bank} free")])
            return bank

        def cv2_end(m, n, bank):
            mms = []
            for k in range(YT - HT, YT):
                mms += three(lambda j: w_cv2[:, j, k, m * P:(m + 1) * P], lambda j: y_half(k, j, n))

            def fn(e, i):
                for t, (lhsT, rhs) in enumerate(mms):
                    ins = e.matmul(ps_u[:, bank, :], lhsT, rhs, start=False, stop=(t == len(mms) - 1))
                return ins
            return s.pe(fn, after=[s.last(f"y{k}{n}") for k in range(YT - HT, YT)])

        for b in range(NB):
            bottleneck(b)

        def cv2_unit(m, n):
            bank = early_cv2.pop(0) if early_cv2 else cv2_begin(m, n)
            mm = cv2_end(m, n, bank)
            u, ready, slot = silu(bank, mm, "cv2", m)
            xa = (2 * m + n) % 2

            def fn(e, i):
                src = x[bass.ds(i, 1), m * P:(m + 1) * P, n * ROWS:(n + 1) * ROWS, :].rearrange("b p h w -> p (b h w)")
                return e.dma_start(x_again[:, xa, :], src)
            got = s.dma(f"again{xa}", fn, after=[s.last(f"x_again{xa} free"), s.last("o_nat0 free")])
            a = s.dve(lambda e, i: e.tensor_tensor(x1[:, m, HH[n]], u, x_again[:, xa, :], ALU.add),
                      after=[ready, got, s.last("qk free"), s.last("x1 stored")])
            s.keep(f"wide{slot} free", a)
            s.keep(f"x_again{xa} free", a)
            x_again_read.append(a)
            return mm, s.dve(lambda e, i: e.bn_stats(stats[:, 1, m, n, :], x1[:, m, HH[n]]), after=[a])

        ready2, x_again_read = [], []
        for m, n in CV2_ORDER:
            mm, stat = cv2_unit(m, n)
            if n == 1:
                ready2.append(stat)
        s.keep("y free", mm)
        s.keep("o_nat0 free", *x_again_read)

        s.keep("gn2 ready", *ready2)
        gn2 = group_norm_stats(s, 1, "gn2", ready2)
        next(gn2)
        ahead_cv1 = cv1_steps(s.kept["gn1 parts"])
        next(ahead_cv1)
        next(gn2)
        next(ahead_cv1)
        next(ahead_cv1)
        next(gn2, None)
        factors = Done(s.sem("vector"), s.sem("vector").n)
        parts = []
        for t in range(CT):
            parts.append(normalise(s, 1, t, x1[:, t, :], x1_parts[:, t], [], [factors, [s.last(f"probs{q} free") for q in range(PROBS)]]))
            next(ahead_cv1)
        for _ in ahead_cv1:
            pass
        s.keep("gn2 factors used", parts[-1])

        def l1_unit_group(m, n):
            mms = []
            for k in range(CT):
                mms += three(lambda j: w_l1[:, j, k, m * P:(m + 1) * P], lambda j: x1_parts[:, k, j, HH[n]])
            bank, mm = unit_group(mms, [parts])
            a = s.dve(lambda e, i: e.scalar_tensor_tensor(x1[:, m, HH[n]], ps_u[:, bank, :], l1_unit[:, m:m + 1], x1[:, m, HH[n]],
                                                          ALU.mult, ALU.add), after=[mm, parts])
            s.keep(f"U{bank} free", a)
            return mm, a

        stored = []
        for m in range(CT):
            for n in range(2):
                mm, a = l1_unit_group(m, n)

            def fn(e, i, m=m):
                return e.dma_start(out[bass.ds(i, 1), m * P:(m + 1) * P, :, :].rearrange("b p h w -> p (b h w)"), x1[:, m, :])
            stored.append(s.dma(f"out{m}", fn, after=[a]))
        s.keep("qk free", *stored)
        s.keep("x1 stored", *stored)
        for q in range(PROBS):
            s.keep(f"probs{q} free", mm)
        body = s

        block = ctx.enter_context(nc.Block())

        def program(name):
            def run(e):
                setup.emit(name, e, None)
                setup.finals(e)
                for sname, sm_ in body.sems.items():
                    if sname == name or (name == "sync" and sname not in Section.ENGINES):
                        e.sem_inc(sm_.handle, sm_.n)
                with e.Fori(0, B) as i:
                    body.emit(name, e, i)
                if name == "sync":
                    for m in range(CT):
                        e.wait_ge(body.sems[f"out{m}"].handle, (B + 1) * 16)
            return run
        block.sync(program("sync"))
        block.tensor(program("tensor"))
        block.vector(program("vector"))
        block.scalar(program("scalar"))
        block.gpsimd(program("gpsimd"))


_INS = ["x", "L0_conv_cv1_w", "L0_conv_cv1_bn", "L0_conv_cv2_w", "L0_conv_cv2_bn", "L0_conv_m_cv1_w", "L0_conv_m_cv1_bn",
        "L0_conv_m_qkv_w", "L0_conv_m_rw", "L0_conv_m_rh", "L0_conv_m_cv2_w", "L0_conv_m_cv2_bn", "L1_conv_conv",
        "L1_conv_S", "L1_conv_T"]


def kernel(**inputs):
    import numpy as _np
    import concourse.bacc as _bacc
    from concourse import mybir as _mybir
    from concourse.bass_utils import run_bass_kernel_spmd as _run

    nc = _bacc.Bacc("TRN2", target_bir_lowering=False, num_devices=1, dynamic_dma_scratch_size=DMA_SCRATCH)
    arrays, args = {}, []
    for name in _INS:
        a = _np.ascontiguousarray(inputs[name])
        arrays[f"in_{name}_dram"] = a
        args.append(nc.dram_tensor(f"in_{name}_dram", a.shape, _mybir.dt.from_np(a.dtype), kind="ExternalInput").ap())
    shape = inputs["x"].shape
    args.append(nc.dram_tensor("out_0_dram", shape, _mybir.dt.float32, kind="ExternalOutput").ap())
    build(nc, *args)
    r = _run(nc, [arrays], core_ids=[0])
    return r.results[0]["out_0_dram"]
```

```python
from contextlib import ExitStack

import concourse.bass as bass
from concourse import mybir
from concourse.alu_op_type import AluOpType as ALU

ACT = mybir.ActivationFunctionType
AX = mybir.AxisListType
F32 = mybir.dt.float32
F16 = mybir.dt.float16
I32 = mybir.dt.int32

P = 128
ACTIVATION_SCALE = 16.0
WEIGHT_TOP = 64.0
WS = WEIGHT_TOP * ACTIVATION_SCALE
V_SHIFT = 2.0 ** -8
SHIFT_UNIT = 1024.0
EXP_TOP = 5.545177444479562
BN_EPS, GN_EPS = 1e-3, 1e-5
R_UNIT = 256.0
WIDES, PROBS = 4, 3
DMA_SCRATCH = 1024


class Done:

    def __init__(self, sem, count, lag=0):
        self.sem, self.count, self.lag = sem, count, lag


class Sem:
    def __init__(self, handle):
        self.handle, self.n = handle, 0


class Later:
    def __init__(self, name):
        self.name = name


def flat(after):
    return [d for a in after for d in (flat(a) if isinstance(a, (list, tuple)) else [a])]


class Section:

    ENGINES = ("tensor", "scalar", "vector", "gpsimd", "sync")

    def __init__(self, nc, ctx, name, loop):
        self.nc, self.ctx, self.name, self.loop = nc, ctx, name, loop
        self.queue = {e: [] for e in self.ENGINES}
        self.sems = {}
        self.kept = {}

    def sem(self, name):
        if name not in self.sems:
            self.sems[name] = Sem(self.ctx.enter_context(self.nc.semaphore(f"{self.name}_{name}")))
        return self.sems[name]

    def do(self, engine, fn, after=(), sem=None, inc=1, bare=False):
        s = self.sem(sem or engine)
        s.n += inc
        self.queue[engine].append((fn, flat(after), s, inc, bare))
        return Done(s, s.n)

    def pe(self, fn, after=()):
        return self.do("tensor", fn, after)

    def act(self, fn, after=()):
        return self.do("scalar", fn, after)

    def dve(self, fn, after=()):
        return self.do("vector", fn, after)

    def pool(self, fn, after=()):
        return self.do("gpsimd", fn, after, bare=True)

    def dma(self, sem, fn, after=()):
        return self.do("sync", fn, after, sem=sem, inc=16, bare=True)

    def keep(self, name, *done):
        self.kept[name] = list(done)

    def last(self, name):
        if name in self.kept:
            return self.kept[name]
        return [Later(name)] if self.loop else []

    def resolve(self, after):
        for a in after:
            if isinstance(a, Later):
                for d in self.kept[a.name]:
                    yield Done(d.sem, d.count, d.lag + 1)
            else:
                yield a

    def emit(self, engine, e, i):
        seen = {}
        for fn, after, s, inc, bare in self.queue[engine]:
            need = {}
            for d in self.resolve(after):
                at = d.count - d.lag * d.sem.n
                if at > seen.get(d.sem, -10**9):
                    seen[d.sem] = need[d.sem] = at
            for d_sem, at in need.items():
                if self.loop:
                    e.wait_ge(d_sem.handle, i * d_sem.n + (d_sem.n + at))
                    if bare:
                        e.sem_inc(self.held.handle, 1)
                else:
                    e.wait_ge(d_sem.handle, at)
            fn(e, i).then_inc(s.handle, inc)

    def finals(self, e):
        for s in self.sems.values():
            e.wait_ge(s.handle, s.n)


def build(nc, x, cv1_w, cv1_bn, cv2_w, cv2_bn, m_cv1_w, m_cv1_bn, m_qkv_w, m_rw, m_rh, m_cv2_w,
          m_cv2_bn, conv, S_logits, T_logits, out):
    B, C, H, W = x.shape
    HW = H * W
    NB, CH = m_cv1_w.shape[0], m_cv1_w.shape[1]
    G = S_logits.shape[1]
    HD = m_rw.shape[3]
    CT, HT, YT = C // P, CH // P, (2 + NB) * CH // P
    HALF = HW // 2
    ROWS = H // 2
    HP, WP = H + 2, W + 2
    TAPS = 9
    JT = HW // P
    VW = 2 * HD + 2
    HEADS = CH // HD
    QC = 2 * P
    GROUP = C // 32
    assert HEADS == 4 and HD == 64 and HW == 1024

    ctx = ExitStack()
    with ctx:
        def sb(name, shape, dt):
            return ctx.enter_context(nc.sbuf_tensor(name, shape, dt))

        w_cv1 = sb("w_cv1", [P, 2, CT, C], F16)
        w_cv2 = sb("w_cv2", [P, 2, YT, C], F16)
        w_l1 = sb("w_l1", [P, 2, CT, C], F16)
        w_qkv = sb("w_qkv", [P, NB, 2, HT, 3 * CH], F16)
        w_m2 = sb("w_m2", [P, NB, 2, HT, CH], F16)
        w_c3 = sb("w_c3", [P, 2, HT, TAPS, CH], F16)
        w_c3_dram = nc.dram_tensor("w_c3_dram", (NB, P, 2 * HT * TAPS * CH), F16, kind="Internal").ap()
        xn = sb("xn", [P, CT, HW], F32)
        xn_parts = xn[:, :, :].rearrange("p t n -> p (t n)").bitcast(F16).rearrange(
            "p (t s n) -> p t s n", t=CT, s=2)
        y_plain = sb("y_plain", [P, HT, 2, HW], F16)
        y_pad = sb("y_pad", [P, YT - HT, 2, HP * WP], F16)
        z = sb("z", [P, HT, 2, HW], F16)
        qk = sb("qk", [P, 2 * HEADS * HW // 2], F32)
        qk16 = qk[:, :].bitcast(F16).rearrange("p (s h n) -> p s h n", s=2, h=HEADS)
        q_stack, k_stack = qk16[:, 0], qk16[:, 1]
        q2_stack = sb("q2_stack", [P, HEADS, HW], F16)
        k2_stack = sb("k2_stack", [P, HEADS, HW], F16)
        x1 = qk[:, :].rearrange("p (t n) -> p t n", t=CT)
        v_ext = sb("v_ext", [P, JT, HEADS, VW], F16)
        probs = sb("probs", [P, PROBS, 2, JT, QC], F16)
        x1_parts = probs[:, :, :, :, :].rearrange("p a b c d -> p (a b c d)")[:, 0:2 * CT * HW].rearrange(
            "p (t s n) -> p t s n", t=CT, s=2)
        wide = sb("wide", [P, WIDES, HW], F32)
        o_nat = sb("o_nat", [P, 2, JT, P], F32)
        x_again = o_nat[:, 0, :, :].rearrange("p a b -> p (a b)").rearrange("p (a n) -> p a n", a=2)
        ident16 = sb("ident16", [P, P], F16)
        ident = sb("ident", [P, P], F32)
        group_mean = sb("group_mean", [P, P], F32)
        par = {n: sb(f"par_{n}", [P, t, 2], F32) for n, t in
               (("cv1_t", CT), ("cv1_y", CT), ("cv2_t", CT), ("cv2_y", CT), ("m1_t", NB * HT), ("m1_y", NB * HT),
                ("m2_t", NB * HT), ("m2_y", NB * HT))}
        qkv_unit = sb("qkv_unit", [P, NB, 6], F32)
        l1_unit = sb("l1_unit", [P, CT], F32)
        w_r = sb("w_r", [P, NB, HT, P], F16)
        pick = sb("pick", [P, HW], F16)
        row_max = sb("row_max", [P, 2, JT, 2], F32)
        shift = sb("shift", [P, 2, 2, JT], F32)
        shift16 = sb("shift16", [P, 2, JT], F16)
        recip = sb("recip", [P, 2, 2], F32)
        stats = sb("stats", [P, 2, CT, 2, 6], F32)
        mv = sb("mv", [P, 2, CT, 2], F32)
        gn = sb("gn", [P, 2, 8, CT], F32)
        minus_half = sb("minus_half", [P, 16], F32)
        exp_top = sb("exp_top", [P, 1], F32)

        ps_u = ctx.enter_context(nc.psum_tensor("ps_u", [P, 4, HALF], F32))
        ps_a = ctx.enter_context(nc.psum_tensor("ps_a", [P, 2, HALF], F32))
        ps_o = ctx.enter_context(nc.psum_tensor("ps_o", [P, 2, HALF], F32))

        def pad_view(t, part, r0, c0, rows):
            m = y_pad[:, t, part, :].rearrange("p (r c) -> p r c", c=WP)
            return m[:, r0:r0 + rows, c0:c0 + W]

        def y_half(t, part, n):
            if t < HT:
                return y_plain[:, t, part, n * HALF:(n + 1) * HALF].rearrange("p (r c) -> p r c", c=W)
            return pad_view(t - HT, part, 1 + n * ROWS, 1, ROWS)

        def img(ap):
            return ap.rearrange("p (r c) -> p r c", c=W)

        HH = slice(0, HALF), slice(HALF, HW)

        def group_norm_stats(s, slot, tag, source_ready, bank="O0 free", constants=()):
            g = gn[:, slot]
            aggr = [s.do("vector", lambda e, i, t=t: e.bn_aggr(mv[:, slot, t, :], stats[:, slot, t, :, :].rearrange("p a b -> p (a b)")),
                         after=[source_ready[t], s.last(tag + " factors used")], bare=True) for t in range(CT)]
            yield
            mean = s.pe(lambda e, i: e.matmul(ps_o[:, 0, 0:CT], group_mean[:, :], mv[:, slot, :, 0], start=True, stop=True),
                        after=[aggr, constants, s.last(bank)])
            c1 = s.dve(lambda e, i: e.tensor_copy(g[:, 0, :], ps_o[:, 0, 0:CT]), after=[mean])
            c2 = s.dve(lambda e, i: e.tensor_tensor(g[:, 1, :], mv[:, slot, :, 0], g[:, 0, :], ALU.subtract), after=[c1])
            c3 = s.dve(lambda e, i: e.tensor_tensor(g[:, 2, :], g[:, 1, :], g[:, 1, :], ALU.mult), after=[c2])
            c4 = s.dve(lambda e, i: e.tensor_tensor(g[:, 3, :], g[:, 2, :], mv[:, slot, :, 1], ALU.add), after=[c3])
            s.keep(bank, c1)
            yield
            var = s.pe(lambda e, i: e.matmul(ps_o[:, 0, 0:CT], group_mean[:, :], g[:, 3, :], start=True, stop=True),
                       after=[c4, s.last(bank)])
            c5 = s.dve(lambda e, i: e.tensor_scalar(g[:, 4, :], ps_o[:, 0, 0:CT], GN_EPS, None, ALU.add), after=[var])
            s.keep(bank, c5)
            rstd = s.pool(lambda e, i: e.tensor_tensor(g[:, 5, :], g[:, 4, :], minus_half[:, 0:CT], ALU.pow), after=[c5, constants])
            c6 = s.dve(lambda e, i: e.tensor_scalar(g[:, 6, :], g[:, 5, :], ACTIVATION_SCALE, None, ALU.mult), after=[rstd])
            c7 = s.dve(lambda e, i: e.scalar_tensor_tensor(g[:, 7, :], g[:, 6, :], -1.0, g[:, 0, :], ALU.mult, ALU.mult), after=[c6])
            return c7

        wide_turn = [0]

        fixed_wide = [WIDES - 1]

        def next_wide():
            wide_turn[0] += 1
            return fixed_wide[0] if fixed_wide else wide_turn[0] % WIDES

        def normalise(s, *what, **how):
            thread = normalise_thread(s, *what, **how)
            while True:
                try:
                    next(thread)
                except StopIteration as end:
                    return end.value

        def normalise_thread(s, slot, t, src, dst, ready, factors, in_place=False):
            w = next_wide()
            g = gn[:, slot]
            f = s.pool(lambda e, i: e.tensor_scalar(wide[:, w, :], src, g[:, 6, t:t + 1], g[:, 7, t:t + 1], ALU.mult, ALU.add),
                       after=[ready, factors, s.last(f"wide{w} free")])
            yield
            if in_place:
                hi = s.act(lambda e, i: e.activation(dst[:, 0, :], wide[:, w, :], ACT.Copy), after=[f])
            else:
                hi = s.act(lambda e, i: e.activation(dst[:, 0, :], src, ACT.Identity, scale=g[:, 6, t:t + 1], bias=g[:, 7, t:t + 1]),
                           after=[ready, factors])
            yield
            lo = s.dve(lambda e, i: e.tensor_tensor(dst[:, 1, :], wide[:, w, :], dst[:, 0, :], ALU.subtract), after=[f, hi])
            s.keep(f"wide{w} free", lo)
            return lo

        def load_x(s, batch_of):
            loaded = []
            for t in range(CT):
                def fn(e, i, t=t):
                    src = x[batch_of(i), t * P:(t + 1) * P, :, :].rearrange("b p h w -> p (b h w)")
                    return e.dma_start(xn[:, t, :], src)
                loaded.append(s.dma(f"x{t}", fn, after=[s.last("xn read")]))
            return loaded

        def gn1_stats(s, loaded):
            ready = []
            for t in range(CT):
                for n in range(2):
                    r = s.dve(lambda e, i, t=t, n=n: e.bn_stats(stats[:, 0, t, n, :], xn[:, t, HH[n]]), after=[loaded[t]])
                ready.append(r)
            return ready

        turn = [0]

        def unit_bank():
            turn[0] += 1
            return (turn[0] - 1) % 4

        def unit_part(bank, matmuls, after, start=True, stop=True):
            def fn(e, i):
                for k, (lhsT, rhs) in enumerate(matmuls):
                    ins = e.matmul(ps_u[:, bank, :], lhsT, rhs, start=start and k == 0, stop=stop and k == len(matmuls) - 1)
                return ins
            return s.pe(fn, after=[after, s.last(f"U{bank} free") if start else []])

        def unit_group(matmuls, after):
            bank = unit_bank()
            return bank, unit_part(bank, matmuls, after)

        def three(w_of, x_of):
            return [(w_of(0), x_of(0)), (w_of(0), x_of(1)), (w_of(1), x_of(0))]

        def silu_halves(bank, mm, name, t):
            slot = next_wide()
            th, yh = wide[:, slot, 0:HALF], wide[:, slot, HALF:HW]
            pt, py = par[name + "_t"], par[name + "_y"]
            a = s.act(lambda e, i: e.activation(th, ps_u[:, bank, :], ACT.Tanh, scale=pt[:, t, 0:1], bias=pt[:, t, 1:2]),
                      after=[mm, s.last(f"wide{slot} free")])
            b = s.act(lambda e, i: e.activation(yh, ps_u[:, bank, :], ACT.Identity, scale=py[:, t, 0:1], bias=py[:, t, 1:2]),
                      after=[mm])
            s.keep(f"U{bank} free", b)
            return th, yh, [a, b], slot

        def silu_product(th, yh, halves):
            return s.dve(lambda e, i: e.scalar_tensor_tensor(yh, th, 1.0, yh, ALU.add, ALU.mult), after=[halves])

        def silu(bank, mm, name, t):
            th, yh, halves, slot = silu_halves(bank, mm, name, t)
            return yh, silu_product(th, yh, halves), slot

        def split_hi(u, ready, hi, after=()):
            return s.pool(lambda e, i: e.tensor_scalar(hi, u, 1.0, 0.0, ALU.mult, ALU.add), after=[ready, after])

        def split_lo(u, ready, hi, lo, slot):
            b = s.dve(lambda e, i: e.tensor_tensor(lo, u, hi, ALU.subtract), after=[ready])
            s.keep(f"wide{slot} free", b)
            return b

        def split_to(u, ready, hi, lo, slot, after=()):
            return split_lo(u, split_hi(u, ready, hi, after), hi, lo, slot)

        def add_to(u, other, ready):
            return s.dve(lambda e, i: e.tensor_tensor(img(u), img(u), other, ALU.add), after=[ready])

        def cv1_steps(parts):
            for m in [2, 3, 0, 1]:
                for n in range(2):
                    mms = []
                    for k in range(CT):
                        mms += three(lambda j: w_cv1[:, j, k, m * P:(m + 1) * P], lambda j: xn_parts[:, k, j, HH[n]])
                    bank, mm = unit_group(mms, parts)
                    u, ready, slot = silu(bank, mm, "cv1", m)
                    s.keep(f"y{m}{n}", split_to(img(u), ready, y_half(m, 0, n), y_half(m, 1, n), slot, after=[s.last("y free")]))
                    s.keep("xn read", mm)
                    yield

        s = Section(nc, ctx, "setup", loop=False)
        SLOT = CH * TAPS
        stage = [qk[:, 0:SLOT],
                 probs[:, :, :, :, :].rearrange("p a b c d -> p (a b c d)")[:, 0:2 * SLOT].bitcast(F32),
                 wide[:, :, :].rearrange("p a b -> p (a b)")[:, 0:SLOT]]
        pads = y_pad[:, :, :, :].rearrange("p a b c -> p (a b c)")
        split = [pads[:, 2 * SLOT * j:2 * SLOT * (j + 1)] for j in range(3)]
        spare = q2_stack[:, :, :].rearrange("p h n -> p (h n)").bitcast(F32)
        spare_used = [0]

        def tmp(*shape):
            size = 1
            for n in shape:
                size *= n
            ap = spare[:, spare_used[0]:spare_used[0] + size]
            spare_used[0] += size
            names = "abcd"[:len(shape)]
            return ap.rearrange(f"p ({' '.join(names)}) -> p {' '.join(names)}", **dict(zip(names[1:], shape[1:]))) if len(shape) > 1 else ap

        def side_by_side(threads, width):
            waiting, running = list(threads), []
            while waiting or running:
                while waiting and len(running) < width:
                    running.append(waiting.pop(0))
                for t in list(running):
                    try:
                        next(t)
                    except StopIteration:
                        running.remove(t)
                yield

        ones = tmp(P)
        m1 = s.pool(lambda e, i: e.memset(ident[:, :], 0.0))
        m2 = s.pool(lambda e, i: e.memset(group_mean[:, :], 1.0 / GROUP))
        m3 = s.pool(lambda e, i: e.memset(minus_half[:, :], -0.5))
        m4 = s.pool(lambda e, i: e.memset(ones, 1.0))
        s.pool(lambda e, i: e.memset(exp_top[:, :], EXP_TOP))
        id32 = s.pool(lambda e, i: e.affine_select(out=ident[:, :], in_=ident[:, :], compare_op=ALU.not_equal, fill=1.0,
                                                   base=0, pattern=[[-1, P]], channel_multiplier=1), after=[m1])
        gm3 = group_mean[:, :].rearrange("p (g q) -> p g q", q=GROUP)
        g1 = s.pool(lambda e, i: e.affine_select(out=gm3, in_=gm3, compare_op=ALU.is_ge, fill=0.0, base=0,
                                                 pattern=[[-GROUP, P // GROUP], [0, GROUP]], channel_multiplier=1), after=[m2])
        g2 = s.pool(lambda e, i: e.affine_select(out=gm3, in_=gm3, compare_op=ALU.is_ge, fill=0.0, base=GROUP - 1,
                                                 pattern=[[GROUP, P // GROUP], [0, GROUP]], channel_multiplier=-1), after=[g1])
        id16 = s.dve(lambda e, i: e.tensor_copy(ident16[:, :], ident[:, :]), after=[id32])
        pk = s.pool(lambda e, i: e.memset(pick[:, :], 0.0))
        pk3 = img(pick[:, :])
        for quarter in range(4):
            pat = [[0, H], [-1, W]] if quarter % 2 == 0 else [[-1, H], [0, W]]
            pk = s.pool(lambda e, i, quarter=quarter, pat=pat: e.affine_select(
                out=pk3, in_=pk3, compare_op=ALU.not_equal, fill=R_UNIT, base=-32 * quarter, pattern=pat,
                channel_multiplier=1), after=[pk])

        bn_raw, got_bn = {}, {}

        def bn_load(name, ap, tiles):
            t = tmp(4, tiles)
            bn_raw[name] = t
            got_bn[name] = s.dma("bn", lambda e, i: e.dma_start(t, ap.rearrange("f (t p) -> p f t", p=P),
                                                                allow_slow_non_contiguous=True))
        bn_load("cv1", cv1_bn, CT)
        bn_load("cv2", cv2_bn, CT)
        for b in range(NB):
            bn_load(f"m1_{b}", m_cv1_bn[b], HT)
            bn_load(f"m2_{b}", m_cv2_bn[b], HT)
        st = tmp(2, CT, G)
        got_st = [s.dma("st", lambda e, i, j=j, src=src: e.dma_start(st[:, j, :, :], src.rearrange("(t p) g -> p t g", p=P)))
                  for j, src in enumerate((S_logits, T_logits))]
        loaded = load_x(s, lambda i: slice(0, 1))
        rwh = tmp(NB, HT, W + H)
        got_r = []
        for b in range(NB):
            for lo_, hi_, src in ((0, W, m_rw), (W, W + H, m_rh)):
                got_r.append(s.dma("r", lambda e, i, b=b, lo_=lo_, hi_=hi_, src=src: e.dma_start(
                    rwh[:, b, :, lo_:hi_], src[b].rearrange("a (t g) d h w -> (g d) (a t) (h w)", g=2))))

        bank_turn = [0]
        SMALLS = 6
        row_small = tmp(SMALLS + 1, 5)
        w_done = []

        def row_factors(slot, w_f32, unit_out, ready, also=None):
            r = row_small[:, slot]
            a = s.dve(lambda e, i: e.tensor_reduce(r[:, 0:1], w_f32, AX.X, ALU.max, apply_absolute_value=True),
                      after=[ready, s.last(f"row_small{slot}")])
            yield
            if also is None:
                b = s.dve(lambda e, i: e.tensor_scalar(r[:, 1:2], r[:, 0:1], 2.0 ** -100, None, ALU.max), after=[a])
            else:
                b = s.dve(lambda e, i: e.scalar_tensor_tensor(r[:, 1:2], r[:, 0:1], 2.0 ** -100, also, ALU.max, ALU.max), after=[a])
            yield
            c = s.dve(lambda e, i: e.tensor_scalar(unit_out.bitcast(I32), r[:, 1:2].bitcast(I32), 0x7F800000, None,
                                                   ALU.bitwise_and), after=[b])
            yield
            d = s.dve(lambda e, i: e.reciprocal(r[:, 2:3], unit_out), after=[c])
            yield
            return s.dve(lambda e, i: e.tensor_scalar(r[:, 3:4], r[:, 2:3], WEIGHT_TOP, None, ALU.mult), after=[d])

        def split_scaled(w_f32, w_parts, factor, ready, use_pool=True):
            if use_pool:
                g = s.pool(lambda e, i: e.tensor_scalar(w_f32, w_f32, factor, 0.0, ALU.mult, ALU.add), after=[ready])
            else:
                g = s.act(lambda e, i: e.activation(w_f32, w_f32, ACT.Copy, scale=factor), after=[ready])
            yield
            hi = s.act(lambda e, i: e.activation(w_parts[0], w_f32, ACT.Copy), after=[g])
            yield
            return s.dve(lambda e, i: e.tensor_tensor(w_parts[1], w_f32, w_parts[0], ALU.subtract), after=[hi])

        def claim(free, size):
            for q in list(free):
                pair = [q - q % 2, q - q % 2 + 1]
                if size <= SLOT // 2:
                    free.remove(q)
                    return [q]
                if all(k in free for k in pair):
                    for k in pair:
                        free.remove(k)
                    return pair

        free_stage, free_split = list(range(SMALLS)), list(range(SMALLS))

        class Rows:

            def __init__(self, rows, cols, dst_of, unit_out, taps=1, also=None, after=lambda: [], then=lambda done: ()):
                self.rows, self.cols, self.dst_of, self.unit_out = rows, cols, dst_of, unit_out
                self.taps, self.also, self.after, self.then = taps, also, after, then
                self.size = cols * taps

            def load(self):
                self.stage = claim(free_stage, self.size)
                if self.stage is None:
                    return False
                q = self.stage[0]
                wf = self.wf = stage[q // 2][:, q % 2 * (SLOT // 2):q % 2 * (SLOT // 2) + self.size]
                self.got = s.dma(f"stage{q}", lambda e, i: e.dma_start(wf, self.rows), after=[s.last(f"stage{k} free") for k in self.stage])
                return True

            def compute(self, own):
                q, n = own[0], self.size
                base = split[q // 2][:, q % 2 * SLOT:]
                wp = [base[:, j * n:(j + 1) * n] for j in range(2)]
                f = yield from row_factors(q, self.wf, self.unit_out, self.got, self.also)
                yield
                parts = yield from split_scaled(self.wf, wp, row_small[:, q, 3:4], [f, [s.last(f"split{k} free") for k in own]])
                for k in self.stage:
                    s.keep(f"stage{k} free", parts)
                free_stage.extend(self.stage)
                s.keep(f"row_small{q}", parts)
                yield
                kt = self.cols // P
                views = [wp[j].rearrange("p (c t) -> p t c", t=self.taps) for j in range(2)]
                if self.taps == 1:
                    runs = [([views[j][:, 0, k * P:(k + 1) * P] for k in range(k0, min(k0 + 8, kt))],
                             self.dst_of(j, slice(k0, min(k0 + 8, kt)))) for j in range(2) for k0 in range(0, kt, 8)]
                else:
                    runs = [([views[j][:, t, k * P:(k + 1) * P] for t in range(t0, min(t0 + 5, self.taps))],
                             self.dst_of(j, k)[:, t0:min(t0 + 5, self.taps), :]) for j in range(2) for k in range(kt) for t0 in (0, 5)]
                done = []
                for sources, dst in runs:
                    bank = bank_turn[0] % 6
                    bank_turn[0] += 1
                    pt = (ps_u[:, bank, :] if bank < 4 else ps_a[:, bank - 4, :]).bitcast(F16)

                    def fn(e, i, sources=sources, pt=pt):
                        for j, src in enumerate(sources):
                            ins = e.transpose(pt[:, j * P:(j + 1) * P], src, ident16[:, :])
                        return ins
                    t = s.pe(fn, after=[parts, id16, s.last(f"bank{bank} free")])
                    src = pt[:, 0:len(sources) * P].rearrange("p (a b) -> p a b", b=P)
                    if bank % 2:
                        d = s.act(lambda e, i, dst=dst, src=src: e.activation(dst, src, ACT.Copy), after=[t, self.after()])
                    else:
                        d = s.dve(lambda e, i, dst=dst, src=src: e.tensor_copy(dst, src), after=[t, self.after()])
                    s.keep(f"bank{bank} free", d)
                    done.append(d)
                    yield
                for k in own:
                    s.keep(f"split{k} free", *done)
                free_split.extend(own)
                w_done.extend(done)
                yield from self.then(done)

        def weight_threads(tiles):
            STAGGER = 3
            to_load, loaded_, running, wait = list(tiles), [], [], 0
            while to_load or loaded_ or running:
                while to_load and to_load[0].load():
                    loaded_.append(to_load.pop(0))
                own = claim(free_split, loaded_[0].size) if loaded_ and wait <= 0 else None
                if own:
                    running.append(loaded_.pop(0).compute(own))
                    wait = STAGGER
                wait -= 1
                for t in list(running):
                    if next(t, t) is t:
                        running.remove(t)
                yield

        unit = {n: tmp(t) for n, t in (("cv1", CT), ("cv2", CT), ("m1", NB * HT), ("m2", NB * HT))}

        r_max = tmp(NB, HT)
        a = s.dve(lambda e, i: e.tensor_reduce(r_max, rwh, AX.X, ALU.max, apply_absolute_value=True), after=[got_r])
        s.dve(lambda e, i: e.tensor_scalar(r_max, r_max, 1.0 / R_UNIT, None, ALU.mult), after=[a])

        def r_operand(b, t, ready):
            f = s.dve(lambda e, i: e.reciprocal(r_scale[:, b, t:t + 1], qkv_unit[:, b, 2 + t:3 + t]), after=[ready])
            yield
            g = s.dve(lambda e, i: e.tensor_scalar(rwh[:, b, t, :], rwh[:, b, t, :], r_scale[:, b, t:t + 1], WS / R_UNIT,
                                                   ALU.mult, ALU.mult), after=[f])
            yield
            hi = s.dve(lambda e, i: e.tensor_copy(r_parts[:, 0, :], rwh[:, b, t, :]), after=[g, s.last("r_parts free")])
            yield
            lo = s.dve(lambda e, i: e.tensor_tensor(r_parts[:, 1, :], rwh[:, b, t, :], r_parts[:, 0, :], ALU.subtract), after=[hi])
            pt = ps_o[:, 1, :].bitcast(F16)[:, 0:P]
            yield
            mm = s.pe(lambda e, i: e.transpose(pt, r_parts[:, :, :].rearrange("p a b -> p (a b)"), ident16[:, :]),
                      after=[lo, id16, s.last("perm1 free")])
            yield
            d = s.dve(lambda e, i: e.tensor_copy(w_r[:, b, t, :], pt), after=[mm])
            s.keep("perm1 free", d)
            s.keep("r_parts free", d)
        r_scale = tmp(NB, HT)
        r_parts = tmp(P // 2).bitcast(F16).rearrange("p (a b) -> p a b", a=2)

        c3_sent = {NB: []}
        c3_made = {b: [] for b in range(NB)}

        def c3_rows(b, m):
            def then(done):
                c3_made[b] += done
                if m == HT - 1:
                    c3_sent[b] = [s.dma("c3_out", lambda e, i: e.dma_start(
                        w_c3_dram[b], w_c3[:, :, :, :, :].rearrange("p a b c d -> p (a b c d)")), after=[c3_made[b]])]
                return ()
            return Rows(m_cv1_w[b, m * P:(m + 1) * P].rearrange("o c h w -> o (c h w)"), CH,
                        lambda j, k: w_c3[:, j, k, :, m * P:(m + 1) * P], unit["m1"][:, b * HT + m:b * HT + m + 1], TAPS,
                        after=lambda: c3_sent[b + 1], then=then)

        def qkv_rows(b, m):
            is_k = HT <= m < 2 * HT
            return Rows(m_qkv_w[b, m * P:(m + 1) * P].rearrange("o c h w -> o (c h w)"), CH,
                        lambda j, k: w_qkv[:, b, j, k, m * P:(m + 1) * P], qkv_unit[:, b, m:m + 1],
                        also=r_max[:, b, m - HT:m - HT + 1] if is_k else None,
                        then=(lambda done: r_operand(b, m - HT, done)) if is_k else (lambda done: ()))

        def plain_rows(w, m, dst, kt, name, t):
            return Rows(w.rearrange("o c h w -> o (c h w)"), kt * P, lambda j, k: dst[:, j, k, m * P:(m + 1) * P],
                        unit[name][:, t:t + 1])

        def layer_1():
            st2 = tmp(2, CT, G)
            sm = tmp(6, 2, CT)
            iota_g, key_base, rank, v_unit = tmp(G), tmp(CT), tmp(CT), tmp(CT)
            wl = k2_stack[:, :, :].rearrange("p a b -> p (a b)").bitcast(F32).rearrange("p (t c) -> p t c", t=CT)
            one_hot = z[:, :, :, :].rearrange("p a b c -> p (a b c)").bitcast(F32).rearrange("p (t k) -> p t k", t=CT)
            vx = v_ext[:, :, :, :].rearrange("p a b c -> p (a b c)")
            one_hot16 = vx[:, 0:CT * C].rearrange("p (t k) -> p t k", t=CT)
            iota_k, k_row = x_again[:, 0, :], x_again[:, 1, :]
            yp = y_plain[:, :, :, :].rearrange("p a b c -> p (a b c)")
            s_row, g_row = tmp(C), tmp(C)
            cmp_ = yp[:, 0:2 * C].bitcast(F32)
            wf = yp[:, 2 * C:4 * C].bitcast(F32)
            got_w = [s.dma(f"conv{t}", lambda e, i, t=t: e.dma_start(wl[:, t, :], conv[t * P:(t + 1) * P].rearrange("o c h w -> o (c h w)")))
                     for t in range(CT)]
            i1 = s.pool(lambda e, i: e.iota(iota_g, pattern=[[1, G]], base=-G, channel_multiplier=0,
                                            allow_small_or_imprecise_dtypes=True))
            i2 = s.pool(lambda e, i: e.iota(key_base, pattern=[[P, CT]], base=0, channel_multiplier=1,
                                            allow_small_or_imprecise_dtypes=True))
            i3 = s.pool(lambda e, i: e.iota(iota_k, pattern=[[1, C]], base=0, channel_multiplier=0,
                                            allow_small_or_imprecise_dtypes=True))
            yield

            def bc(ap, n):
                return ap.unsqueeze(3).to_broadcast([P, 2, CT, n])
            a = s.dve(lambda e, i: e.tensor_reduce(sm[:, 0], st[:, :, :, :], AX.X, ALU.max), after=[got_st])
            yield
            a = s.dve(lambda e, i: e.tensor_tensor(st[:, :, :, :], st[:, :, :, :], bc(sm[:, 0], G), ALU.subtract), after=[a])
            yield
            a = s.act(lambda e, i: e.activation(st2[:, :, :, :], st[:, :, :, :], ACT.Exp), after=[a])
            yield
            yield
            a = s.dve(lambda e, i: e.tensor_reduce(sm[:, 1], st2[:, :, :, :], AX.X, ALU.add), after=[a])
            yield
            a = s.dve(lambda e, i: e.reciprocal(sm[:, 2], sm[:, 1]), after=[a])
            yield
            a = s.dve(lambda e, i: e.tensor_tensor(st2[:, :, :, :], st2[:, :, :, :], bc(sm[:, 2], G), ALU.mult), after=[a])
            yield
            gain = s.dve(lambda e, i: e.tensor_reduce(sm[:, 3], st2[:, :, :, :], AX.X, ALU.max), after=[a])
            yield
            yield
            a = s.dve(lambda e, i: e.tensor_tensor(st[:, :, :, :], st2[:, :, :, :], bc(sm[:, 3], G), ALU.is_ge), after=[gain])
            yield
            a = s.dve(lambda e, i: e.tensor_tensor(st[:, :, :, :], st[:, :, :, :],
                                                   iota_g.unsqueeze(1).unsqueeze(1).to_broadcast([P, 2, CT, G]), ALU.mult), after=[a, i1])
            yield
            arg = s.dve(lambda e, i: e.tensor_reduce(sm[:, 4], st[:, :, :, :], AX.X, ALU.min), after=[a])
            yield
            key = s.dve(lambda e, i: e.scalar_tensor_tensor(sm[:, 5, 1, :], sm[:, 4, 1, :], float(C), key_base,
                                                            ALU.mult, ALU.add), after=[arg, i2])
            yield
            diag = o_nat[:, 1, 0:CT, :]

            def rows_of(col, ready, dst):
                made = []
                for t in range(CT):
                    made.append(s.dve(lambda e, i, t=t: e.tensor_scalar(diag[:, t, :], ident[:, :], col[:, t:t + 1], None, ALU.mult),
                                      after=[ready, id32, s.last("diag free")]))

                def fn(e, i):
                    for t in range(CT):
                        ins = e.matmul(ps_o[:, 0, t * P:(t + 1) * P], ones, diag[:, t, :], start=True, stop=True)
                    return ins
                yield
                mm = s.pe(fn, after=[made, m4, s.last("perm0 free")])
                yield
                cp = s.dve(lambda e, i: e.tensor_copy(dst, ps_o[:, 0, :]), after=[mm])
                s.keep("diag free", mm)
                s.keep("perm0 free", cp)
                return cp
            rk = yield from rows_of(sm[:, 5, 1, :], key, k_row)
            yield
            rs = yield from rows_of(sm[:, 4, 0, :], arg, s_row)
            yield
            rg = yield from rows_of(sm[:, 3, 0, :], gain, g_row)
            yield
            hot, free = [], []
            for t in range(CT):
                yield
                a = s.dve(lambda e, i, t=t: e.tensor_scalar(cmp_, k_row, sm[:, 5, 1, t:t + 1], None, ALU.is_lt), after=[rk, free])
                yield
                a = s.dve(lambda e, i, t=t: e.tensor_reduce(rank[:, t:t + 1], cmp_, AX.X, ALU.add), after=[a])
                free = [a]
                yield
                a = s.dve(lambda e, i, t=t: e.tensor_scalar(one_hot[:, t, :], iota_k, rank[:, t:t + 1], None, ALU.is_equal), after=[a, i3])
                hot.append(s.act(lambda e, i, t=t: e.activation(one_hot16[:, t, :], one_hot[:, t, :], ACT.Copy), after=[a]))
                yield
            masked = []
            for t in range(CT):
                yield
                a = s.dve(lambda e, i, t=t: e.tensor_scalar(cmp_, s_row, sm[:, 4, 1, t:t + 1], sm[:, 3, 1, t:t + 1], ALU.is_equal, ALU.mult),
                          after=[rs, free])
                yield
                a = s.dve(lambda e, i, t=t: e.tensor_tensor(cmp_, cmp_, g_row, ALU.mult), after=[a, rg])
                yield
                a = s.dve(lambda e, i, t=t: e.tensor_tensor(wl[:, t, :], wl[:, t, :], cmp_, ALU.mult), after=[a, got_w[t]])
                masked.append(a)
                free = [a]
                yield
            vp = probs[:, :, :, :, :].rearrange("p a b c d -> p (a b c d)")[:, 2 * SLOT:2 * SLOT + 2 * CT * C].rearrange(
                "p (t s c) -> p t s c", t=CT, s=2)
            v_done = []
            for m in range(CT):
                def fn(e, i, m=m):
                    for t in range(CT):
                        ins = e.matmul(ps_o[:, 0, :], one_hot[:, t, m * P:(m + 1) * P], wl[:, t, :], start=(t == 0), stop=(t == CT - 1))
                    return ins
                mm = s.pe(fn, after=[masked, hot, s.last("perm0 free")])
                cp = s.dve(lambda e, i: e.tensor_copy(wf, ps_o[:, 0, :]), after=[mm, s.last("wf free")])
                s.keep("perm0 free", cp)
                f = yield from row_factors(SMALLS, wf, v_unit[:, m:m + 1], cp)
                yield
                d = yield from split_scaled(wf, [vp[:, m, 0, :], vp[:, m, 1, :]], row_small[:, SMALLS, 3:4], [f], use_pool=False)
                s.keep(f"row_small{SMALLS}", d)
                s.keep("wf free", d)
                v_done.append(d)
                yield
            for c in range(CT):
                for j in range(2):
                    def fn(e, i, c=c, j=j):
                        for t in range(CT):
                            ins = e.matmul(ps_o[:, j, :], vp[:, t, j, c * P:(c + 1) * P], one_hot16[:, t, :], start=(t == 0), stop=(t == CT - 1))
                        return ins
                    mm = s.pe(fn, after=[v_done, hot, s.last(f"perm{j} free")])
                    cp = s.act(lambda e, i, c=c, j=j: e.activation(w_l1[:, j, c, :], ps_o[:, j, :], ACT.Copy), after=[mm])
                    s.keep(f"perm{j} free", cp)
                    yield

            def fn(e, i):
                for n in range(CT):
                    for t in range(CT):
                        ins = e.matmul(ps_o[:, 0, n:n + 1], one_hot[:, t, n * P:(n + 1) * P], v_unit[:, t:t + 1], start=(t == 0), stop=(t == CT - 1))
                return ins
            mm = s.pe(fn, after=[v_done, s.last("perm0 free")])
            l1f = s.dve(lambda e, i: e.tensor_scalar(l1_unit[:, :], ps_o[:, 0, 0:CT], 1.0 / WS, None, ALU.mult), after=[mm])
            s.keep("perm0 free", l1f)
            s.keep("layer 1", l1f, mm)
            yield

        def first_norm():
            ready = gn1_stats(s, loaded)
            yield
            factors = yield from group_norm_stats(s, 0, "gn1", ready, "perm0 free", [g2, m3])
            yield
            parts = []
            for t in range(CT):
                parts.append((yield from normalise_thread(s, 0, t, xn[:, t, :], xn_parts[:, t], [], factors, in_place=True)))
                yield
            s.keep("gn1 factors used", parts[-1])
            s.keep("gn1 parts", *parts)


        def bn_factors(name, raw, units, t0, tiles, out_scale):
            t = tmp(4, tiles)
            pt, py = par[name + "_t"][:, t0:t0 + tiles, :], par[name + "_y"][:, t0:t0 + tiles, :]
            a = s.dve(lambda e, i: e.tensor_scalar(t[:, 0, :], raw[:, 3, :], BN_EPS, None, ALU.add), after=[list(got_bn.values())])
            b = s.pool(lambda e, i: e.tensor_tensor(t[:, 1, :], t[:, 0, :], minus_half[:, 0:tiles], ALU.pow), after=[a, m3])
            yield
            c = s.dve(lambda e, i: e.tensor_tensor(t[:, 2, :], t[:, 1, :], raw[:, 0, :], ALU.mult), after=[b])
            d = s.dve(lambda e, i: e.tensor_tensor(t[:, 3, :], t[:, 2, :], raw[:, 2, :], ALU.mult), after=[c])
            f = s.dve(lambda e, i: e.tensor_tensor(t[:, 0, :], raw[:, 1, :], t[:, 3, :], ALU.subtract), after=[d])
            yield
            g = s.dve(lambda e, i: e.tensor_tensor(t[:, 1, :], t[:, 2, :], units, ALU.mult), after=[d, w_done])
            s.dve(lambda e, i: e.tensor_scalar(pt[:, :, 0], t[:, 1, :], 0.5 / WS, None, ALU.mult), after=[g])
            s.dve(lambda e, i: e.tensor_scalar(pt[:, :, 1], t[:, 0, :], 0.5, None, ALU.mult), after=[f])
            s.dve(lambda e, i: e.tensor_scalar(py[:, :, 0], t[:, 1, :], 0.5 * out_scale / WS, None, ALU.mult), after=[g])
            h = s.dve(lambda e, i: e.tensor_scalar(py[:, :, 1], t[:, 0, :], 0.5 * out_scale, None, ALU.mult), after=[f])
            s.keep(f"bn {name} {t0}", h)

        bns = [bn_factors("cv1", bn_raw["cv1"], unit["cv1"], 0, CT, ACTIVATION_SCALE),
               bn_factors("cv2", bn_raw["cv2"], unit["cv2"], 0, CT, 1.0)]
        bns += [bn_factors(n, bn_raw[f"{n}_{b}"], unit[n][:, b * HT:(b + 1) * HT], b * HT, HT, ACTIVATION_SCALE)
                for b in range(NB) for n in ("m1", "m2")]

        def bn_beginnings():
            for _ in range(2):
                for t in bns:
                    next(t)
                    yield

        weights = [c3_rows(NB - 1, m) for m in range(HT)]
        weights += [plain_rows(cv1_w[m * P:(m + 1) * P], m, w_cv1, CT, "cv1", m) for m in range(CT)]
        for b in reversed(range(NB - 1)):
            weights += [c3_rows(b, m) for m in range(HT)]
        for b in range(NB):
            weights += [qkv_rows(b, m) for m in range(6)]
            weights += [plain_rows(m_cv2_w[b, m * P:(m + 1) * P], m, w_m2[:, b], HT, "m2", b * HT + m) for m in range(HT)]
        weights += [plain_rows(cv2_w[m * P:(m + 1) * P], m, w_cv2, YT, "cv2", m) for m in range(CT)]
        for _ in side_by_side([weight_threads(weights), first_norm(), layer_1(), bn_beginnings()], 4):
            pass

        read = [s.last("layer 1"), w_done, Done(s.sem("tensor"), s.sem("tensor").n), Done(s.sem("vector"), s.sem("vector").n)]
        pad_maps = y_pad[:, :, :, :].rearrange("p t s (r c) -> p (t s) r c", c=WP)
        zeros = read
        for edge in (pad_maps[:, :, 0, :], pad_maps[:, :, HP - 1, :], pad_maps[:, :, :, 0], pad_maps[:, :, :, WP - 1]):
            zeros = [s.dve(lambda e, i, edge=edge: e.memset(edge, 0.0), after=zeros)]
        s.dve(lambda e, i: e.memset(v_ext[:, :, :, HD:HD + 1], 1.0), after=read)
        for w in range(WIDES):
            s.keep(f"wide{w} free", *read)
        for q in range(4):
            s.keep(f"U{q} free", *read)
        fixed_wide.clear()
        s.keep("y free", *zeros, *flat([s.last("layer 1")]))
        next(bns[0], None)
        for _ in cv1_steps(s.kept["gn1 parts"] + s.last("bn cv1 0")):
            pass
        for t in bns[1:]:
            next(t, None)
        s.dve(lambda e, i: e.tensor_scalar(qkv_unit[:, :, 0:4], qkv_unit[:, :, 0:4], 1.0 / WEIGHT_TOP, None, ALU.mult), after=[w_done])
        s.dve(lambda e, i: e.tensor_scalar(qkv_unit[:, :, 4:6], qkv_unit[:, :, 4:6],
                                           ACTIVATION_SCALE / (WS * V_SHIFT), None, ALU.mult), after=[w_done])
        k2z = s.pool(lambda e, i: e.memset(k2_stack[:, :, :], 0.0), after=read)
        s.pool(lambda e, i: e.memset(q2_stack[:, :, :], 0.0), after=[Done(s.sem("vector"), s.sem("vector").n)])
        for h in range(HEADS):
            row = HD if h % 2 == 0 else 0
            s.act(lambda e, i, h=h, row=row: e.activation(k2_stack[row:row + 1, h, :], k2_stack[row:row + 1, h, :], ACT.Copy,
                                                          scale=0.0, bias=SHIFT_UNIT), after=[k2z])
        setup = s

        s = Section(nc, ctx, "batch", loop=True)
        s.held = Sem(ctx.enter_context(nc.semaphore("held")))
        loaded = load_x(s, lambda i: bass.ds((i + 1) % B, 1))

        def first_norm_ahead():
            ready = gn1_stats(s, loaded)
            yield
            for _ in group_norm_stats(s, 0, "gn1", ready):
                yield
            factors = Done(s.sem("vector"), s.sem("vector").n)
            yield
            parts = []
            for t in range(CT):
                parts.append(normalise(s, 0, t, xn[:, t, :], xn_parts[:, t], [], factors, in_place=True))
                s.keep("gn1 factors used", parts[-1])
                s.keep("gn1 parts", *parts)
                yield

        norm_ahead = first_norm_ahead()
        NORM_PARTS = {(1, 0, 0): 2, (1, 1, 1): 0}
        conv_banks = {}

        def conv_part(b, m, n, bank, rows, after, start=False, stop=False):
            mms = []
            for k in range(HT):
                for dy in rows:
                    for dx in range(3):
                        mms += three(lambda j: w_c3[:, j, k, 3 * dy + dx, m * P:(m + 1) * P],
                                     lambda j: pad_view(b * HT + k, j, n * ROWS + dy, dx, ROWS))
            return unit_part(bank, mms, after, start, stop)

        def conv_begin(b, m, n):
            conv_banks[m, n] = unit_bank()
            conv_part(b, m, n, conv_banks[m, n], [0, 1], [s.last("w_c3")] + [s.last(f"y{HT + b * HT + k}{q}") for k in range(HT) for q in range(n + 1)],
                      start=True)

        def bottleneck(b):
            y0 = HT + b * HT
            if not conv_banks:
                conv_begin(b, 0, 0)
                conv_begin(b, 1, 0)
            z_ready = {}
            for n in range(2):
                for m in range(HT):
                    if n == 1:
                        conv_begin(b, m, n)
                    bank = conv_banks.pop((m, n))
                    mm = conv_part(b, m, n, bank, [2], [s.last(f"y{y0 + k}1") for k in range(HT)], stop=True)
                    u, ready, slot = silu(bank, mm, "m1", b * HT + m)
                    z_ready[m, n] = split_to(u, ready, z[:, m, 0, HH[n]], z[:, m, 1, HH[n]], slot, after=[s.last("z free")])
                    for _ in range(NORM_PARTS.get((b, n, m), 1)):
                        next(norm_ahead, None)
            s.keep("w_c3", s.dma("c3", lambda e, i: e.dma_start(w_c3[:, :, :, :, :].rearrange("p a b c d -> p (a b c d)"),
                                                                w_c3_dram[(b + 1) % NB]), after=[mm]))

            q_ready = {(h, n): [] for h in range(HEADS) for n in range(2)}
            k_ready = {(h, n): [] for h in range(HEADS) for n in range(2)}
            v_ready = []
            z_all = {n: [z_ready[m, n] for m in range(HT)] for n in range(2)}

            def project(kind, pair, n):
                m = 2 * kind + pair
                mms = []
                for k in range(HT):
                    mms += three(lambda j: w_qkv[:, b, j, k, m * P:(m + 1) * P], lambda j: z[:, k, j, HH[n]])
                if kind == 1:
                    mms.append((w_r[:, b, pair, :], pick[:, HH[n]]))
                bank, mm = unit_group(mms, z_all[n])
                slot = next_wide()
                f = wide[:, slot, 0:HALF]
                both = wide[:, slot, HALF:HW].bitcast(F16)
                hi16, lo16 = both[:, 0:HALF], both[:, HALF:HW]
                full = s.act(lambda e, i: e.activation(f, ps_u[:, bank, :], ACT.Identity, scale=qkv_unit[:, b, m:m + 1]),
                             after=[mm, s.last(f"wide{slot} free")])
                s.keep(f"U{bank} free", full)
                hi = s.act(lambda e, i: e.activation(hi16, f, ACT.Copy), after=[full])
                lo = s.pool(lambda e, i: e.tensor_tensor(lo16, f, hi16, ALU.subtract), after=[hi])
                cols, done = HH[n], []

                def copy(dst, src, ready, on_act=False):
                    if on_act:
                        c = s.act(lambda e, i: e.activation(dst, src, ACT.Copy), after=[ready, s.last("qk free")])
                    else:
                        c = s.dve(lambda e, i: e.tensor_copy(dst, src), after=[ready, s.last("qk free")])
                    done.append(c)
                    return c
                for h, nat, oth in ((2 * pair, slice(0, HD), slice(HD, P)), (2 * pair + 1, slice(HD, P), slice(0, HD))):
                    if kind == 0:
                        q_ready[h, n] += [copy(q_stack[nat, h, cols], hi16[nat], hi, on_act=h % 2 == 0),
                                          copy(q2_stack[nat, h, cols], hi16[nat], hi)]
                    else:
                        k_ready[h, n] += [copy(k_stack[nat, h, cols], hi16[nat], hi),
                                          copy(k_stack[oth, h, cols], hi16[nat], hi, on_act=True)]

                def lows():
                    for h, nat, oth in ((2 * pair, slice(0, HD), slice(HD, P)), (2 * pair + 1, slice(HD, P), slice(0, HD))):
                        if kind == 0:
                            q_ready[h, n].append(copy(q_stack[oth, h, cols], lo16[nat], lo))
                        else:
                            k_ready[h, n].append(copy(k2_stack[nat, h, cols], lo16[nat], lo))
                    s.keep(f"wide{slot} free", *done)
                while lows_later:
                    lows_later.pop()()
                lows_later.append(lows)

            lows_later = []

            def project_v(jj):
                bank = turn[0] % 4
                turn[0] += 1

                def fn(e, i):
                    for q in range(2):
                        px = ps_u[:, bank, q * CH:(q + 1) * CH]
                        j = slice((2 * jj + q) * P, (2 * jj + q + 1) * P)
                        mms = []
                        for k in range(HT):
                            mms += [(z[:, k, a, j], w_qkv[:, b, c, k, 2 * CH:3 * CH]) for a, c in ((0, 0), (0, 1), (1, 0))]
                        for t, (lhsT, rhs) in enumerate(mms):
                            ins = e.matmul(px, lhsT, rhs, start=(t == 0), stop=(t == len(mms) - 1))
                    return ins
                mm = s.pe(fn, after=[z_all[jj // 2], s.last(f"U{bank} free")])
                px = ps_u[:, bank, :].rearrange("p (a d) -> p a d", d=HD)
                ve = v_ext[:, 2 * jj:2 * jj + 2, :, :].rearrange("p j h d -> p (j h) d")
                hi = s.act(lambda e, i: e.activation(ve[:, :, 0:HD], px, ACT.Copy, scale=V_SHIFT), after=[mm, s.last("v free")])
                lo = s.dve(lambda e, i: e.scalar_tensor_tensor(ve[:, :, HD + 1:2 * HD + 1], px, V_SHIFT, ve[:, :, 0:HD], ALU.mult, ALU.subtract), after=[hi])
                s.keep(f"U{bank} free", lo)
                v_ready.append(lo)

            a_turn = [0]

            def max_tile(h, it, n):
                bank = a_turn[0] % 2
                a_turn[0] += 1
                mm = s.pe(lambda e, i: e.matmul(ps_a[:, bank, :], q_stack[:, h, it * P:(it + 1) * P], k_stack[:, h, HH[n]], start=True, stop=True),
                          after=[q_ready[h, it // 4], k_ready[h, n], s.last(f"A{bank} free")])
                d = s.dve(lambda e, i: e.reduce_max(row_max[:, h % 2, it, n:n + 1], ps_a[:, bank, :], axis=AX.X),
                          after=[mm, s.last(f"row_max{h % 2}{it // 4} free")])
                s.keep(f"A{bank} free", d)
                return d

            def shifts(h, half, maxima):
                its = slice(4 * half, 4 * half + 4)
                a = s.dve(lambda e, i: e.tensor_reduce(shift[:, h % 2, 0, its], row_max[:, h % 2, its, :], AX.X, ALU.max), after=[maxima])
                s.keep(f"row_max{h % 2}{half} free", a)
                return s.dve(lambda e, i: e.tensor_scalar(shift16[:, h % 2, its], shift[:, h % 2, 0, its], -1.0 / SHIFT_UNIT, None, ALU.mult),
                             after=[a, s.last(f"shift{h % 2}{half} free")])

            def shift_row(h, half, ready):
                bank = a_turn[0] % 2
                a_turn[0] += 1

                def fn(e, i):
                    for q in range(4):
                        ins = e.matmul(ps_a[:, bank, q * P:(q + 1) * P],
                                       shift16[:, h % 2, 4 * half + q:4 * half + q + 1].to_broadcast([P, P]), ident16[:, :], start=True, stop=True)
                    return ins
                mm = s.pe(fn, after=[ready, s.last(f"A{bank} free")])
                s.keep(f"shift{h % 2}{half} free", mm)
                row = slice(HD, HD + 1) if h % 2 == 0 else slice(0, 1)
                c = s.act(lambda e, i: e.activation(q2_stack[row, h, HH[half]], ps_a[row, bank, :], ACT.Copy), after=[mm, s.last("qk free")])
                s.keep(f"A{bank} free", c)
                shift_ready[h, half] = c

            shift_ready = {}

            def maxima_ahead():
                waiting, made = [], {}
                order = [(0, 0, 0), (1, 0, 0), (0, 0, 1), (1, 0, 1)]
                order += [(h, half, n) for h, half in ((2, 0), (3, 0), (0, 1), (1, 1), (2, 1), (3, 1)) for n in range(2)]
                for h, half, n in order:
                    tiles = made.setdefault((h, half), [])
                    for it in range(4 * half, 4 * half + 4):
                        tiles.append(max_tile(h, it, n))
                        if waiting and it % 4 == 1:
                            yield
                            shift_row(*waiting.pop())
                        yield
                    if len(tiles) == 8:
                        waiting.append((h, half, shifts(h, half, tiles)))
                yield
                shift_row(*waiting.pop())

            ahead = maxima_ahead()

            def take(count=1):
                for _ in range(count):
                    next(ahead, None)

            for piece, tiles in ((lambda: project(0, 0, 0), 0), (lambda: project(1, 0, 0), 0), (lambda: project(0, 1, 0), 0),
                                 (lambda: project(1, 1, 0), 1), (lambda: project_v(0), 2), (lambda: project_v(1), 2),
                                 (lambda: project(1, 0, 1), 1), (lambda: project(0, 0, 1), 2), (lambda: project(0, 1, 1), 1),
                                 (lambda: project(1, 1, 1), 2), (lambda: project_v(2), 2), (lambda: project_v(3), 1)):
                piece()
                take(tiles)
            while lows_later:
                lows_later.pop()()

            STEPS = HEADS * 8
            exp_done, lo_done = {}, {}

            def logits_step(st_):
                (h, c), g = CHUNKS[st_ // 2], st_ % 2
                q0 = c * QC
                pair_bank = turn[0] // 2 % 2
                turn[0] += 2

                def fn(e, i):
                    for jt in range(4):
                        j = slice((4 * g + jt) * P, (4 * g + jt + 1) * P)
                        o = ps_u[:, 2 * pair_bank + jt // 2, (jt % 2) * QC:(jt % 2 + 1) * QC]
                        e.matmul(o, k_stack[:, h, j], q_stack[:, h, q0:q0 + QC], start=True, stop=False)
                        ins = e.matmul(o, k2_stack[:, h, j], q2_stack[:, h, q0:q0 + QC], start=False, stop=True)
                    return ins
                mm = s.pe(fn, after=[q_ready[h, c // 2], k_ready[h, g], shift_ready[h, c // 2], s.last(f"U{2 * pair_bank} free"), s.last(f"U{2 * pair_bank + 1} free")])
                slot = (st_ // 2) % PROBS
                w = next_wide()
                ex = s.act(lambda e, i: e.activation(wide[:, w, :], ps_u[:, 2 * pair_bank:2 * pair_bank + 2, :].rearrange("p a b -> p (a b)"),
                                                     ACT.Exp, scale=1.0 / (ACTIVATION_SCALE ** 2 * HD ** 0.5), bias=exp_top[:, 0:1]),
                           after=[mm, s.last(f"wide{w} free")])
                s.keep(f"U{2 * pair_bank} free", ex)
                s.keep(f"U{2 * pair_bank + 1} free", ex)
                free = s.last(f"probs{slot} free")
                dst = [probs[:, slot, part, 4 * g:4 * g + 4, :].rearrange("p j q -> p (j q)") for part in range(2)]
                border = 416 if st_ < MAXIMA_STEPS else 640
                A, B_ = slice(0, border), slice(border, HW)
                hi_a = s.act(lambda e, i: e.activation(dst[0][:, A], wide[:, w, A], ACT.Copy), after=[ex, free])
                hi_b = s.pool(lambda e, i: e.tensor_scalar(dst[0][:, B_], wide[:, w, B_], 1.0, 0.0, ALU.mult, ALU.add), after=[ex, free])
                lo_b = s.pool(lambda e, i: e.tensor_tensor(dst[1][:, B_], wide[:, w, B_], dst[0][:, B_], ALU.subtract), after=[hi_b])
                exp_done[st_] = (w, dst, hi_a, lo_b, A)

            def low_step(st_):
                w, dst, hi_a, lo_b, A = exp_done[st_]
                lo = s.dve(lambda e, i: e.tensor_tensor(dst[1][:, A], wide[:, w, A], dst[0][:, A], ALU.subtract), after=[hi_a])
                s.keep(f"wide{w} free", lo, lo_b)
                lo_done[st_] = [lo, lo_b]

            o_turn = [0]
            av_bank = {}

            def av_half(chunk, half):
                (h, c), slot = CHUNKS[chunk], chunk % PROBS
                if half == 0:
                    av_bank[chunk] = o_turn[0] % 2
                    o_turn[0] += 1
                bank = av_bank[chunk]

                def fn(e, i):
                    for jt in range(JT):
                        cols = slice(half * P, (half + 1) * P)
                        o = ps_o[:, bank, half * (HD + 1):(half + 1) * (HD + 1)]
                        e.matmul(o, probs[:, slot, 0, jt, cols], v_ext[:, jt, h, 0:HD + 1], start=(jt == 0), stop=False)
                        e.matmul(o[:, 0:HD], probs[:, slot, 0, jt, cols], v_ext[:, jt, h, HD + 1:2 * HD + 1], start=False, stop=False)
                        ins = e.matmul(o, probs[:, slot, 1, jt, cols], v_ext[:, jt, h, 0:HD + 1], start=False,
                                       stop=(jt == JT - 1))
                    return ins
                mm = s.pe(fn, after=[lo_done[2 * chunk], lo_done[2 * chunk + 1], v_ready, s.last(f"O{bank} free")])
                if half == 0:
                    return
                s.keep(f"probs{slot} free", mm)
                normalise_later.append((h, c, bank, mm))

            def normalise_chunk(h, c, bank, mm):
                r = c % 2
                src = ps_o[:, bank, 0:2 * (HD + 1)].rearrange("p (a q) -> p a q", a=2)
                rc = s.dve(lambda e, i: e.reciprocal(recip[:, r, :], src[:, :, HD]), after=[mm, s.last(f"recip{r} free")])
                nr = s.dve(lambda e, i: e.tensor_tensor(o_nat[:, h // 2, 2 * c:2 * c + 2, h % 2 * HD:h % 2 * HD + HD], src[:, :, 0:HD],
                                                        recip[:, r, :].unsqueeze(2).to_broadcast([P, 2, HD]), ALU.mult),
                           after=[rc, s.last(f"o_nat{h // 2} free")])
                s.keep(f"recip{r} free", nr)
                s.keep(f"O{bank} free", nr)
                norm_done[h, c] = nr

            normalise_later = []
            norm_done = {}

            def transpose_half(pair, n):
                bank = a_turn[0] % 2
                a_turn[0] += 1

                def fn(e, i):
                    for q in range(4):
                        ins = e.transpose(ps_a[:, bank, q * P:(q + 1) * P], o_nat[:, pair, 4 * n + q, :], ident[:, :])
                    return ins
                need = [norm_done[2 * pair + hh, 2 * n + cc] for hh in range(2) for cc in range(2)]
                mm = s.pe(fn, after=[need, s.last(f"A{bank} free")])
                if n == 1:
                    s.keep(f"o_nat{pair} free", mm)
                slot = next_wide()
                f = wide[:, slot, 0:HALF]
                full = s.act(lambda e, i: e.activation(f, ps_a[:, bank, :], ACT.Copy, scale=qkv_unit[:, b, 4 + pair:5 + pair]),
                             after=[mm, s.last(f"wide{slot} free")])
                s.keep(f"A{bank} free", full)
                hi = s.act(lambda e, i: e.activation(z[:, pair, 0, HH[n]], f, ACT.Copy), after=[full, z_read])
                yield
                lo = s.dve(lambda e, i: e.tensor_tensor(z[:, pair, 1, HH[n]], f, z[:, pair, 0, HH[n]], ALU.subtract), after=[hi])
                s.keep(f"wide{slot} free", lo)
                o_ready[pair, n] = lo

            o_ready = {}
            z_read = Done(s.sem("tensor"), s.sem("tensor").n)
            turn[0] += turn[0] % 2

            def second_conv(m, n):
                mms = []
                for k in range(HT):
                    mms += three(lambda j: w_m2[:, b, j, k, m * P:(m + 1) * P], lambda j: z[:, k, j, HH[n]])
                bank, mm = unit_group(mms, [o_ready[0, n], o_ready[1, n]])
                s.keep("z free", mm)
                th, yh, halves, slot = silu_halves(bank, mm, "m2", b * HT + m)
                yield
                ready = silu_product(th, yh, halves)
                a = add_to(yh, y_half(y0 + m, 0, n), ready)
                yield
                a = add_to(yh, y_half(y0 + m, 1, n), a)
                t = y0 + HT + m
                hi = split_hi(img(yh), a, y_half(t, 0, n), after=[s.last("y free")])
                yield
                s.keep(f"y{t}{n}", split_lo(img(yh), hi, y_half(t, 0, n), y_half(t, 1, n), slot))

            begin_after = {2 * 3 + LAG + 3: transpose_half(0, 0), 2 * 7 + LAG + 3: transpose_half(1, 0),
                           2 * 7 + LAG + 7: second_conv(0, 0), 2 * 7 + LAG + 10: second_conv(1, 0),
                           2 * 11 + LAG + 4: transpose_half(0, 1)}
            background = []

            def advance():
                for thread in list(background):
                    if next(thread, thread) is thread:
                        background.remove(thread)

            def drain(*threads):
                for thread in threads:
                    for _ in thread:
                        pass

            due = 0.0
            for st_ in range(STEPS + LAG):
                due += MAXIMA_PER_STEP
                if LAG <= st_ < STEPS + LAG:
                    av_half((st_ - LAG) // 2, st_ % 2)
                if due >= 1:
                    take()
                    due -= 1
                if st_ < STEPS:
                    logits_step(st_)
                while normalise_later:
                    normalise_chunk(*normalise_later.pop())
                advance()
                if 1 <= st_ <= STEPS:
                    low_step(st_ - 1)
                while due >= 1:
                    take()
                    due -= 1
                advance()
                if st_ in begin_after:
                    background.append(begin_after[st_])
                    next(background[-1])
                    turn[0] += turn[0] % 2
            s.keep("qk free", Done(s.sem("tensor"), s.sem("tensor").n))
            s.keep("v free", Done(s.sem("tensor"), s.sem("tensor").n))
            cover = [lambda m=m: conv_begin(b + 1, m, 0) if b + 1 < NB else cv2_unit(m, 0) for m in range(HT)]
            drain(*background)
            while normalise_later:
                normalise_chunk(*normalise_later.pop())
            drain(transpose_half(1, 1))
            cover[0]()
            drain(second_conv(0, 1), second_conv(1, 1))
            cover[1]()

        LAG = 4
        MAXIMA_PER_STEP = 2.2
        MAXIMA_STEPS = 28
        CHUNKS = [(h, c) for n in range(2) for h in range(HEADS) for c in (2 * n, 2 * n + 1)]
        cv2_last = []

        def cv2_unit(m, n):
            mms = []
            for k in range(YT):
                mms += three(lambda j: w_cv2[:, j, k, m * P:(m + 1) * P], lambda j: y_half(k, j, n))
            bank, mm = unit_group(mms, [s.last(f"y{k}{n}") for k in range(YT)])
            cv2_last[:] = [mm]
            u, ready, slot = silu(bank, mm, "cv2", m)
            xa = x_turn[0] % 2
            x_turn[0] += 1

            def fn(e, i):
                src = x[bass.ds(i, 1), m * P:(m + 1) * P, n * ROWS:(n + 1) * ROWS, :].rearrange("b p h w -> p (b h w)")
                return e.dma_start(x_again[:, xa, :], src)
            got = s.dma(f"again{xa}", fn, after=[s.last(f"x_again{xa} free"), s.last("o_nat0 free")])
            a = s.dve(lambda e, i: e.tensor_tensor(x1[:, m, HH[n]], u, x_again[:, xa, :], ALU.add),
                      after=[ready, got, s.last("qk free"), s.last("x1 stored")])
            s.keep(f"wide{slot} free", a)
            s.keep(f"x_again{xa} free", a)
            x_again_read.append(a)
            ready2[m].append(s.dve(lambda e, i: e.bn_stats(stats[:, 1, m, n, :], x1[:, m, HH[n]]), after=[a]))

        x_turn, x_again_read, ready2 = [0], [], [[] for _ in range(CT)]
        for b in range(NB):
            bottleneck(b)
        for m, n in [(m, 0) for m in range(HT, CT)] + [(m, 1) for m in range(CT)]:
            cv2_unit(m, n)
        s.keep("y free", *cv2_last)
        s.keep("o_nat0 free", *x_again_read)
        gn2 = group_norm_stats(s, 1, "gn2", ready2)
        next(gn2)
        ahead_cv1 = cv1_steps(s.kept["gn1 parts"])
        next(ahead_cv1)
        next(gn2)
        next(ahead_cv1)
        next(ahead_cv1)
        next(gn2, None)
        factors = Done(s.sem("vector"), s.sem("vector").n)
        parts = []
        for t in range(CT):
            parts.append(normalise(s, 1, t, x1[:, t, :], x1_parts[:, t], [], [factors, [s.last(f"probs{q} free") for q in range(PROBS)]]))
            if t % 2:
                next(ahead_cv1)
        for _ in ahead_cv1:
            pass
        s.keep("gn2 factors used", parts[-1])

        def l1_unit_group(m, n):
            mms = []
            for k in range(CT):
                mms += three(lambda j: w_l1[:, j, k, m * P:(m + 1) * P], lambda j: x1_parts[:, k, j, HH[n]])
            bank, mm = unit_group(mms, [parts])
            a = s.dve(lambda e, i: e.scalar_tensor_tensor(x1[:, m, HH[n]], ps_u[:, bank, :], l1_unit[:, m:m + 1], x1[:, m, HH[n]],
                                                          ALU.mult, ALU.add), after=[mm, parts])
            s.keep(f"U{bank} free", a)
            return mm, a

        stored = []
        for m in range(CT):
            for n in range(2):
                mm, a = l1_unit_group(m, n)

            def fn(e, i, m=m):
                return e.dma_start(out[bass.ds(i, 1), m * P:(m + 1) * P, :, :].rearrange("b p h w -> p (b h w)"), x1[:, m, :])
            stored.append(s.dma(f"out{m}", fn, after=[a]))
        s.keep("qk free", *stored)
        s.keep("x1 stored", *stored)
        for q in range(PROBS):
            s.keep(f"probs{q} free", mm)
        body = s

        block = ctx.enter_context(nc.Block())

        def program(name):
            def run(e):
                setup.emit(name, e, None)
                setup.finals(e)
                for sname, sm_ in body.sems.items():
                    if sname == name or (name == "sync" and sname not in Section.ENGINES):
                        e.sem_inc(sm_.handle, sm_.n)
                with e.Fori(0, B) as i:
                    body.emit(name, e, i)
                if name == "sync":
                    for m in range(CT):
                        e.wait_ge(body.sems[f"out{m}"].handle, (B + 1) * 16)
            return run
        block.sync(program("sync"))
        block.tensor(program("tensor"))
        block.vector(program("vector"))
        block.scalar(program("scalar"))
        block.gpsimd(program("gpsimd"))


_INS = ["x", "L0_conv_cv1_w", "L0_conv_cv1_bn", "L0_conv_cv2_w", "L0_conv_cv2_bn", "L0_conv_m_cv1_w", "L0_conv_m_cv1_bn",
        "L0_conv_m_qkv_w", "L0_conv_m_rw", "L0_conv_m_rh", "L0_conv_m_cv2_w", "L0_conv_m_cv2_bn", "L1_conv_conv",
        "L1_conv_S", "L1_conv_T"]


def kernel(**inputs):
    import numpy as _np
    import concourse.bacc as _bacc
    from concourse import mybir as _mybir
    from concourse.bass_utils import run_bass_kernel_spmd as _run

    nc = _bacc.Bacc("TRN2", target_bir_lowering=False, num_devices=1, dynamic_dma_scratch_size=DMA_SCRATCH)
    arrays, args = {}, []
    for name in _INS:
        a = _np.ascontiguousarray(inputs[name])
        arrays[f"in_{name}_dram"] = a
        args.append(nc.dram_tensor(f"in_{name}_dram", a.shape, _mybir.dt.from_np(a.dtype), kind="ExternalInput").ap())
    shape = inputs["x"].shape
    args.append(nc.dram_tensor("out_0_dram", shape, _mybir.dt.float32, kind="ExternalOutput").ap())
    build(nc, *args)
    r = _run(nc, [arrays], core_ids=[0])
    return r.results[0]["out_0_dram"]
```
